# Optimizing a Trainium2 kernel written in Bass

```python
import numpy as np
import jax
import jax.numpy as jnp

def _softmax(x, axis=-1):
    return jax.nn.softmax(x, axis=axis)

def _gelu(x):
    return jax.nn.gelu(x, approximate=True)

def _silu(x):
    return jax.nn.silu(x)

def _sigmoid(x):
    return jax.nn.sigmoid(x)

def _layernorm(x, axis=-1, eps=1e-05):
    m = jnp.mean(x, axis=axis, keepdims=True)
    v = jnp.var(x, axis=axis, keepdims=True)
    return (x - m) / jnp.sqrt(v + eps)

def _scatter_add(tgt, idx, src, axis=0):
    return tgt.at[idx].add(src)

def _segment_sum(src, seg, n):
    return jax.ops.segment_sum(src, seg, n)
kernel_name = 'mk_adaln_d2_jaxref_r8_933ce2'

def setup_inputs(seed: int=0):
    np.random.seed(seed)
    _w = jnp.asarray

    def _L0_attn_setup():
        import jax, jax.numpy as jnp
        import numpy as np
        HID = 256
        H = 16
        D_NOPE = 128
        D_ROPE = 64
        D_Q = D_NOPE + D_ROPE
        D_V = 128
        QR = 192
        KVR = 64
        PH = 16
        PD = HID // PH
        THETA = 10000.0
        EPS = 1e-06

        def rmsnorm(x, w):
            var = jnp.mean(jnp.square(x), axis=-1, keepdims=True)
            return x * jax.lax.rsqrt(var + EPS) * w

        def rope_cos_sin(seq_len):
            inv_freq = 1.0 / THETA ** (jnp.arange(0, D_ROPE, 2, dtype=jnp.float32) / D_ROPE)
            t = jnp.arange(seq_len, dtype=jnp.float32)
            freqs = jnp.outer(t, inv_freq)
            emb = jnp.concatenate([freqs, freqs], -1)
            return (jnp.cos(emb), jnp.sin(emb))

        def rotate_half(x):
            x1, x2 = jnp.split(x, 2, axis=-1)
            return jnp.concatenate([-x2, x1], axis=-1)

        def apply_rope(x, cos, sin):
            return x * cos[None, None] + rotate_half(x) * sin[None, None]
        key = jax.random.key(seed)
        ks = jax.random.split(key, 12)

        def w(k, shape):
            return (jax.random.normal(k, shape, jnp.float32) / np.sqrt(shape[-1])).astype(jnp.float32)
        B, S = (2, 128)
        return {'hidden_states': jax.random.normal(ks[0], (B, S, HID), jnp.float32), 'q_a_w': w(ks[1], (QR, HID)), 'q_a_ln_w': jnp.ones((QR,), jnp.float32), 'q_b_w': w(ks[2], (H * D_Q, QR)), 'kv_a_w': w(ks[3], (KVR + H * D_ROPE, HID)), 'kv_a_ln_w': jnp.ones((KVR,), jnp.float32), 'kv_b_w': w(ks[4], (H * (D_NOPE + D_V), KVR)), 'o_w': w(ks[5], (HID, H * D_V)), 'sp_q_w': w(ks[6], (HID, HID)), 'sp_k_w': w(ks[7], (HID, HID)), 'sp_v_w': w(ks[8], (HID, HID)), 'sp_o_w': w(ks[9], (HID, HID)), 'gate_w': w(ks[10], (2, HID)), 'gate_b': jnp.zeros((2,), jnp.float32)}
    _L0_attn_in = _L0_attn_setup()

    def _L0_ffn_setup():
        import jax, jax.numpy as jnp
        import numpy as np
        GOLDEN_CENTER = 1.0 / np.e
        GOLDEN_LOWER = 0.5 - np.log(4.0 / 3.0)
        GOLDEN_UPPER = 0.5

        def _golden_weights(x, Wr, temperature):
            inh = jax.nn.sigmoid(x @ Wr / temperature)
            in_zone = (inh >= GOLDEN_LOWER) & (inh <= GOLDEN_UPPER)
            distance = jnp.abs(inh - GOLDEN_CENTER)
            weights = jnp.exp(-distance / 0.1) * in_zone.astype(x.dtype)
            wsum = jnp.sum(weights, axis=-1, keepdims=True)
            no_expert = wsum < 1e-08
            fb = jnp.exp(-distance / 0.3)
            _, top2 = jax.lax.top_k(fb, 2)
            fb_mask = jnp.sum(jax.nn.one_hot(top2, weights.shape[-1], dtype=x.dtype), axis=-2)
            fb_w = fb * fb_mask
            fb_w = fb_w / jnp.maximum(jnp.sum(fb_w, axis=-1, keepdims=True), 1e-08)
            weights = jnp.where(no_expert, fb_w, weights)
            weights = weights / jnp.maximum(jnp.sum(weights, axis=-1, keepdims=True), 1e-08)
            return weights
        key = jax.random.key(seed)
        ks = jax.random.split(key, 5)
        B, T, D, E, F = (2, 256, 256, 8, 256)
        s_in = 1.0 / np.sqrt(D)
        s_f = 1.0 / np.sqrt(F)
        return {'x': jax.random.normal(ks[0], (B, T, D), dtype=jnp.float32), 'Wg': jax.random.normal(ks[1], (E, D, F), dtype=jnp.float32) * s_in, 'Wu': jax.random.normal(ks[2], (E, D, F), dtype=jnp.float32) * s_in, 'Wd': jax.random.normal(ks[3], (E, F, D), dtype=jnp.float32) * s_f, 'Wr': jax.random.normal(ks[4], (D, E), dtype=jnp.float32) * s_in, 'temperature': jnp.ones((1,), dtype=jnp.float32)}
    _L0_ffn_in = _L0_ffn_setup()
    _L0_c = _w((lambda *s: np.random.randn(*s).astype(np.float32) * 0.05)(1, 256))
    _L0_wmod = _w((lambda *s: np.random.randn(*s).astype(np.float32) * 0.05)(256, 6 * 256) * 256 ** (-0.5))

    def _L1_attn_setup():
        import math
        import jax, jax.numpy as jnp
        import numpy as np
        NUM_HEAD = 16

        def get_slopes(n):

            def pow2(n):
                start = 2 ** (-2 ** (-(math.log2(n) - 3)))
                return [start * start ** i for i in range(n)]
            if math.log2(n).is_integer():
                return pow2(n)
            c = 2 ** math.floor(math.log2(n))
            return pow2(c) + get_slopes(2 * c)[0::2][:n - c]
        key = jax.random.key(seed)
        ks = jax.random.split(key, 9)
        B, T, C = (2, 256, 256)
        x = jax.random.normal(ks[0], (B, T, C), dtype=jnp.float32)
        std = 0.02
        Wq = std * jax.random.normal(ks[1], (C, C), dtype=jnp.float32)
        Wk = std * jax.random.normal(ks[2], (C, C), dtype=jnp.float32)
        Wv = std * jax.random.normal(ks[3], (C, C), dtype=jnp.float32)
        Wo = 0.02 / np.sqrt(2 * 24) * jax.random.normal(ks[4], (C, C), dtype=jnp.float32)
        bq = jnp.zeros((C,), jnp.float32)
        bk = jnp.zeros((C,), jnp.float32)
        bv = jnp.zeros((C,), jnp.float32)
        bo = jnp.zeros((C,), jnp.float32)
        return {'x': x, 'Wq': Wq, 'bq': bq, 'Wk': Wk, 'bk': bk, 'Wv': Wv, 'bv': bv, 'Wo': Wo, 'bo': bo}
    _L1_attn_in = _L1_attn_setup()

    def _L1_ffn_setup():
        import jax, jax.numpy as jnp
        import numpy as np
        D_MODEL, D_FF, NS, NR, KR = (256, 176, 2, 16, 4)
        B, S = (4, 256)

        def _moe_forward(u, shared_w1, shared_b1, shared_w2, shared_b2, routed_w1, routed_b1, routed_w2, routed_b2, centroids, bias):
            b, s, d = u.shape
            flat = u.reshape(-1, d)
            T = flat.shape[0]
            h = jax.nn.relu(jnp.einsum('td,ndf->ntf', flat, shared_w1) + shared_b1[:, None, :])
            shared_out = jnp.einsum('ntf,nfd->td', h, shared_w2) + shared_b2.sum(0)
            out = flat + shared_out
            scores = jax.nn.sigmoid(flat @ centroids.T) + bias
            vals, idx = jax.lax.top_k(scores, KR)
            gating = jnp.zeros_like(scores).at[jnp.arange(T)[:, None], idx].set(vals)
            gating = gating / jnp.clip(gating.sum(-1, keepdims=True), 1e-08)

            def step(acc, ew):
                w1, b1, w2, b2, g = ew
                hj = jax.nn.relu(flat @ w1 + b1)
                yj = hj @ w2 + b2
                return (acc + yj * g[:, None], None)
            rout0 = jnp.zeros_like(flat)
            rout, _ = jax.lax.scan(step, rout0, (routed_w1, routed_b1, routed_w2, routed_b2, gating.T))
            return (out + rout).reshape(b, s, d)
        key = jax.random.key(seed)
        ks = jax.random.split(key, 10)
        s1 = 1.0 / np.sqrt(D_MODEL)
        s2 = 1.0 / np.sqrt(D_FF)
        return {'u': jax.random.normal(ks[0], (B, S, D_MODEL), dtype=jnp.float32), 'shared_w1': jax.random.normal(ks[1], (NS, D_MODEL, D_FF), dtype=jnp.float32) * s1, 'shared_b1': jnp.zeros((NS, D_FF), dtype=jnp.float32), 'shared_w2': jax.random.normal(ks[2], (NS, D_FF, D_MODEL), dtype=jnp.float32) * s2, 'shared_b2': jnp.zeros((NS, D_MODEL), dtype=jnp.float32), 'routed_w1': jax.random.normal(ks[3], (NR, D_MODEL, D_FF), dtype=jnp.float32) * s1, 'routed_b1': jnp.zeros((NR, D_FF), dtype=jnp.float32), 'routed_w2': jax.random.normal(ks[4], (NR, D_FF, D_MODEL), dtype=jnp.float32) * s2, 'routed_b2': jnp.zeros((NR, D_MODEL), dtype=jnp.float32), 'centroids': jax.random.normal(ks[5], (NR, D_MODEL), dtype=jnp.float32) * s1, 'bias': jnp.zeros((NR,), dtype=jnp.float32)}
    _L1_ffn_in = _L1_ffn_setup()
    _L1_c = _w((lambda *s: np.random.randn(*s).astype(np.float32) * 0.05)(1, 256))
    _L1_wmod = _w((lambda *s: np.random.randn(*s).astype(np.float32) * 0.05)(256, 6 * 256) * 256 ** (-0.5))
    _d = {'L0_attn_hidden_states': _L0_attn_in['hidden_states'], 'L0_attn_q_a_w': _L0_attn_in['q_a_w'], 'L0_attn_q_a_ln_w': _L0_attn_in['q_a_ln_w'], 'L0_attn_q_b_w': _L0_attn_in['q_b_w'], 'L0_attn_kv_a_w': _L0_attn_in['kv_a_w'], 'L0_attn_kv_a_ln_w': _L0_attn_in['kv_a_ln_w'], 'L0_attn_kv_b_w': _L0_attn_in['kv_b_w'], 'L0_attn_o_w': _L0_attn_in['o_w'], 'L0_attn_sp_q_w': _L0_attn_in['sp_q_w'], 'L0_attn_sp_k_w': _L0_attn_in['sp_k_w'], 'L0_attn_sp_v_w': _L0_attn_in['sp_v_w'], 'L0_attn_sp_o_w': _L0_attn_in['sp_o_w'], 'L0_attn_gate_w': _L0_attn_in['gate_w'], 'L0_attn_gate_b': _L0_attn_in['gate_b'], 'L0_ffn_Wg': _L0_ffn_in['Wg'], 'L0_ffn_Wu': _L0_ffn_in['Wu'], 'L0_ffn_Wd': _L0_ffn_in['Wd'], 'L0_ffn_Wr': _L0_ffn_in['Wr'], 'L0_ffn_temperature': _L0_ffn_in['temperature'], 'L0_c': _L0_c, 'L0_wmod': _L0_wmod, 'L1_attn_Wq': _L1_attn_in['Wq'], 'L1_attn_bq': _L1_attn_in['bq'], 'L1_attn_Wk': _L1_attn_in['Wk'], 'L1_attn_bk': _L1_attn_in['bk'], 'L1_attn_Wv': _L1_attn_in['Wv'], 'L1_attn_bv': _L1_attn_in['bv'], 'L1_attn_Wo': _L1_attn_in['Wo'], 'L1_attn_bo': _L1_attn_in['bo'], 'L1_ffn_shared_w1': _L1_ffn_in['shared_w1'], 'L1_ffn_shared_b1': _L1_ffn_in['shared_b1'], 'L1_ffn_shared_w2': _L1_ffn_in['shared_w2'], 'L1_ffn_shared_b2': _L1_ffn_in['shared_b2'], 'L1_ffn_routed_w1': _L1_ffn_in['routed_w1'], 'L1_ffn_routed_b1': _L1_ffn_in['routed_b1'], 'L1_ffn_routed_w2': _L1_ffn_in['routed_w2'], 'L1_ffn_routed_b2': _L1_ffn_in['routed_b2'], 'L1_ffn_centroids': _L1_ffn_in['centroids'], 'L1_ffn_bias': _L1_ffn_in['bias'], 'L1_c': _L1_c, 'L1_wmod': _L1_wmod}
    _x0 = _d['L0_attn_hidden_states']
    _d['L0_attn_hidden_states'] = jax.random.normal(jax.random.fold_in(jax.random.key(seed), 1), (1, 1024, 256), dtype=_x0.dtype)
    del _x0
    return _d

def reference(L0_attn_hidden_states, L0_attn_q_a_w, L0_attn_q_a_ln_w, L0_attn_q_b_w, L0_attn_kv_a_w, L0_attn_kv_a_ln_w, L0_attn_kv_b_w, L0_attn_o_w, L0_attn_sp_q_w, L0_attn_sp_k_w, L0_attn_sp_v_w, L0_attn_sp_o_w, L0_attn_gate_w, L0_attn_gate_b, L0_ffn_Wg, L0_ffn_Wu, L0_ffn_Wd, L0_ffn_Wr, L0_ffn_temperature, L0_c, L0_wmod, L1_attn_Wq, L1_attn_bq, L1_attn_Wk, L1_attn_bk, L1_attn_Wv, L1_attn_bv, L1_attn_Wo, L1_attn_bo, L1_ffn_shared_w1, L1_ffn_shared_b1, L1_ffn_shared_w2, L1_ffn_shared_b2, L1_ffn_routed_w1, L1_ffn_routed_b1, L1_ffn_routed_w2, L1_ffn_routed_b2, L1_ffn_centroids, L1_ffn_bias, L1_c, L1_wmod):

    def _L0_attn_ref(hidden_states, q_a_w, q_a_ln_w, q_b_w, kv_a_w, kv_a_ln_w, kv_b_w, o_w, sp_q_w, sp_k_w, sp_v_w, sp_o_w, gate_w, gate_b):
        import jax, jax.numpy as jnp
        import numpy as np
        HID = 256
        H = 16
        D_NOPE = 128
        D_ROPE = 64
        D_Q = D_NOPE + D_ROPE
        D_V = 128
        QR = 192
        KVR = 64
        PH = 16
        PD = HID // PH
        THETA = 10000.0
        EPS = 1e-06

        def rmsnorm(x, w):
            var = jnp.mean(jnp.square(x), axis=-1, keepdims=True)
            return x * jax.lax.rsqrt(var + EPS) * w

        def rope_cos_sin(seq_len):
            inv_freq = 1.0 / THETA ** (jnp.arange(0, D_ROPE, 2, dtype=jnp.float32) / D_ROPE)
            t = jnp.arange(seq_len, dtype=jnp.float32)
            freqs = jnp.outer(t, inv_freq)
            emb = jnp.concatenate([freqs, freqs], -1)
            return (jnp.cos(emb), jnp.sin(emb))

        def rotate_half(x):
            x1, x2 = jnp.split(x, 2, axis=-1)
            return jnp.concatenate([-x2, x1], axis=-1)

        def apply_rope(x, cos, sin):
            return x * cos[None, None] + rotate_half(x) * sin[None, None]
        b, s, _ = hidden_states.shape
        dt = hidden_states.dtype
        q_mid = rmsnorm(hidden_states @ q_a_w.T, q_a_ln_w)
        q = (q_mid @ q_b_w.T).reshape(b, s, H, D_Q).transpose(0, 2, 1, 3)
        q_nope, q_pe = (q[..., :D_NOPE], q[..., D_NOPE:])
        kv_a = hidden_states @ kv_a_w.T
        kv_lora, k_pe_flat = (kv_a[..., :KVR], kv_a[..., KVR:])
        k_pe = k_pe_flat.reshape(b, s, H, D_ROPE).transpose(0, 2, 1, 3)
        kv = rmsnorm(kv_lora, kv_a_ln_w) @ kv_b_w.T
        kv = kv.reshape(b, s, H, D_NOPE + D_V).transpose(0, 2, 1, 3)
        k_nope, v = (kv[..., :D_NOPE], kv[..., D_NOPE:])
        cos, sin = rope_cos_sin(s)
        q_pe = apply_rope(q_pe, cos, sin)
        k_pe = apply_rope(k_pe, cos, sin)
        qf = jnp.concatenate([q_nope, q_pe], -1)
        kf = jnp.concatenate([k_nope, k_pe], -1)
        scale = D_Q ** (-0.5)
        scores = jnp.einsum('bhqd,bhkd->bhqk', qf, kf) * scale
        probs = jax.nn.softmax(scores.astype(jnp.float32), axis=-1).astype(dt)
        ctx = jnp.einsum('bhqk,bhkd->bhqd', probs, v)
        main_out = ctx.transpose(0, 2, 1, 3).reshape(b, s, H * D_V) @ o_w.T

        def split_heads(x):
            return x.reshape(b, s, PH, PD).transpose(0, 2, 1, 3)
        pq = split_heads(hidden_states @ sp_q_w.T)
        pk = split_heads(hidden_states @ sp_k_w.T)
        pv = split_heads(hidden_states @ sp_v_w.T)
        p_scores = jnp.einsum('bhqd,bhkd->bhqk', pq, pk) * PD ** (-0.5)
        p_probs = jax.nn.softmax(p_scores.astype(jnp.float32), axis=-1).astype(dt)
        p_ctx = jnp.einsum('bhqk,bhkd->bhqd', p_probs, pv)
        pattern_out = p_ctx.transpose(0, 2, 1, 3).reshape(b, s, HID) @ sp_o_w.T
        gates = jax.nn.softmax(hidden_states @ gate_w.T + gate_b, axis=-1)
        return gates[..., 0:1] * main_out + gates[..., 1:2] * pattern_out

    def _L0_ffn_ref(x, Wg, Wu, Wd, Wr, temperature):
        import jax, jax.numpy as jnp
        import numpy as np
        GOLDEN_CENTER = 1.0 / np.e
        GOLDEN_LOWER = 0.5 - np.log(4.0 / 3.0)
        GOLDEN_UPPER = 0.5

        def _golden_weights(x, Wr, temperature):
            inh = jax.nn.sigmoid(x @ Wr / temperature)
            in_zone = (inh >= GOLDEN_LOWER) & (inh <= GOLDEN_UPPER)
            distance = jnp.abs(inh - GOLDEN_CENTER)
            weights = jnp.exp(-distance / 0.1) * in_zone.astype(x.dtype)
            wsum = jnp.sum(weights, axis=-1, keepdims=True)
            no_expert = wsum < 1e-08
            fb = jnp.exp(-distance / 0.3)
            _, top2 = jax.lax.top_k(fb, 2)
            fb_mask = jnp.sum(jax.nn.one_hot(top2, weights.shape[-1], dtype=x.dtype), axis=-2)
            fb_w = fb * fb_mask
            fb_w = fb_w / jnp.maximum(jnp.sum(fb_w, axis=-1, keepdims=True), 1e-08)
            weights = jnp.where(no_expert, fb_w, weights)
            weights = weights / jnp.maximum(jnp.sum(weights, axis=-1, keepdims=True), 1e-08)
            return weights
        weights = _golden_weights(x, Wr, temperature)
        gate = jnp.einsum('btd,edf->betf', x, Wg)
        up = jnp.einsum('btd,edf->betf', x, Wu)
        h = jax.nn.silu(gate) * up
        e_out = jnp.einsum('betf,efd->betd', h, Wd)
        out = jnp.einsum('bte,betd->btd', weights, e_out)
        return out

    def _L1_attn_ref(x, Wq, bq, Wk, bk, Wv, bv, Wo, bo):
        import math
        import jax, jax.numpy as jnp
        import numpy as np
        NUM_HEAD = 16

        def get_slopes(n):

            def pow2(n):
                start = 2 ** (-2 ** (-(math.log2(n) - 3)))
                return [start * start ** i for i in range(n)]
            if math.log2(n).is_integer():
                return pow2(n)
            c = 2 ** math.floor(math.log2(n))
            return pow2(c) + get_slopes(2 * c)[0::2][:n - c]
        B, T, C = x.shape
        H = NUM_HEAD
        D = C // H
        slopes = jnp.asarray(get_slopes(H), dtype=jnp.float32)

        def split_heads(y):
            return y.reshape(B, T, H, D).transpose(0, 2, 1, 3)
        q = split_heads(x @ Wq + bq)
        k = split_heads(x @ Wk + bk)
        v = split_heads(x @ Wv + bv)
        attn = jnp.einsum('bhqd,bhkd->bhqk', q, k) / jnp.sqrt(jnp.float32(D))
        alibi = slopes[:, None, None] * (jnp.arange(T, dtype=jnp.float32) - (T - 1))[None, None, :]
        attn = attn + alibi
        causal = jnp.tril(jnp.ones((T, T), dtype=bool))[None, None]
        attn = jnp.where(causal, attn, jnp.finfo(jnp.float32).min)
        p = jax.nn.softmax(attn, axis=-1)
        o = jnp.einsum('bhqk,bhkd->bhqd', p, v).transpose(0, 2, 1, 3).reshape(B, T, C)
        return o @ Wo + bo

    def _L1_ffn_ref(u, shared_w1, shared_b1, shared_w2, shared_b2, routed_w1, routed_b1, routed_w2, routed_b2, centroids, bias):
        import jax, jax.numpy as jnp
        import numpy as np
        D_MODEL, D_FF, NS, NR, KR = (256, 176, 2, 16, 4)
        B, S = (4, 256)

        def _moe_forward(u, shared_w1, shared_b1, shared_w2, shared_b2, routed_w1, routed_b1, routed_w2, routed_b2, centroids, bias):
            b, s, d = u.shape
            flat = u.reshape(-1, d)
            T = flat.shape[0]
            h = jax.nn.relu(jnp.einsum('td,ndf->ntf', flat, shared_w1) + shared_b1[:, None, :])
            shared_out = jnp.einsum('ntf,nfd->td', h, shared_w2) + shared_b2.sum(0)
            out = flat + shared_out
            scores = jax.nn.sigmoid(flat @ centroids.T) + bias
            vals, idx = jax.lax.top_k(scores, KR)
            gating = jnp.zeros_like(scores).at[jnp.arange(T)[:, None], idx].set(vals)
            gating = gating / jnp.clip(gating.sum(-1, keepdims=True), 1e-08)

            def step(acc, ew):
                w1, b1, w2, b2, g = ew
                hj = jax.nn.relu(flat @ w1 + b1)
                yj = hj @ w2 + b2
                return (acc + yj * g[:, None], None)
            rout0 = jnp.zeros_like(flat)
            rout, _ = jax.lax.scan(step, rout0, (routed_w1, routed_b1, routed_w2, routed_b2, gating.T))
            return (out + rout).reshape(b, s, d)
        return _moe_forward(u, shared_w1, shared_b1, shared_w2, shared_b2, routed_w1, routed_b1, routed_w2, routed_b2, centroids, bias)
    x = L0_attn_hidden_states
    mod = (_silu(L0_c) @ L0_wmod).reshape(L0_c.shape[0], 6, 1, -1)
    sa, ca, ga, sb, cb, gb = (mod[:, 0], mod[:, 1], mod[:, 2], mod[:, 3], mod[:, 4], mod[:, 5])
    ga = (2 * (ga >= 0) - 1) * jnp.maximum(jnp.abs(ga), 0.25)
    gb = (2 * (gb >= 0) - 1) * jnp.maximum(jnp.abs(gb), 0.25)
    h = _layernorm(x, axis=-1) * (1 + ca) + sa
    x = x + ga * _L0_attn_ref(h, L0_attn_q_a_w, L0_attn_q_a_ln_w, L0_attn_q_b_w, L0_attn_kv_a_w, L0_attn_kv_a_ln_w, L0_attn_kv_b_w, L0_attn_o_w, L0_attn_sp_q_w, L0_attn_sp_k_w, L0_attn_sp_v_w, L0_attn_sp_o_w, L0_attn_gate_w, L0_attn_gate_b)
    h = _layernorm(x, axis=-1) * (1 + cb) + sb
    x = x + gb * _L0_ffn_ref(h, L0_ffn_Wg, L0_ffn_Wu, L0_ffn_Wd, L0_ffn_Wr, L0_ffn_temperature)
    mod = (_silu(L1_c) @ L1_wmod).reshape(L1_c.shape[0], 6, 1, -1)
    sa, ca, ga, sb, cb, gb = (mod[:, 0], mod[:, 1], mod[:, 2], mod[:, 3], mod[:, 4], mod[:, 5])
    ga = (2 * (ga >= 0) - 1) * jnp.maximum(jnp.abs(ga), 0.25)
    gb = (2 * (gb >= 0) - 1) * jnp.maximum(jnp.abs(gb), 0.25)
    h = _layernorm(x, axis=-1) * (1 + ca) + sa
    x = x + ga * _L1_attn_ref(h, L1_attn_Wq, L1_attn_bq, L1_attn_Wk, L1_attn_bk, L1_attn_Wv, L1_attn_bv, L1_attn_Wo, L1_attn_bo)
    h = _layernorm(x, axis=-1) * (1 + cb) + sb
    x = x + gb * _L1_ffn_ref(h, L1_ffn_shared_w1, L1_ffn_shared_b1, L1_ffn_shared_w2, L1_ffn_shared_b2, L1_ffn_routed_w1, L1_ffn_routed_b1, L1_ffn_routed_w2, L1_ffn_routed_b2, L1_ffn_centroids, L1_ffn_bias)
    return x

_drawn_inputs = setup_inputs


def setup_inputs(seed=0):
    import zlib

    import numpy as np

    out = dict(_drawn_inputs(seed))
    spreads = {'L0_attn_q_a_ln_w': (1.0, 0.6),
     'L0_attn_kv_a_ln_w': (1.0, 0.6),
     'L0_attn_gate_b': (0.0, 0.8),
     'L1_attn_bq': (0.0, 0.8),
     'L1_attn_bk': (0.0, 2.0),
     'L1_attn_bv': (0.0, 0.8),
     'L1_attn_bo': (0.0, 0.288),
     'L1_ffn_shared_b1': (0.0, 0.342),
     'L1_ffn_shared_b2': (0.0, 0.581),
     'L1_ffn_routed_b1': (0.0, 2.0),
     'L1_ffn_routed_b2': (0.0, 0.66),
     'L1_ffn_bias': (0.0, 0.1)}
    factors = {'L0_attn_kv_a_w': 3.677,
     'L0_attn_sp_q_w': 4.136,
     'L0_attn_sp_k_w': 4.013,
     'L0_attn_sp_v_w': 3.709,
     'L0_attn_sp_o_w': 3.82,
     'L0_attn_gate_w': 3.746,
     'L1_attn_Wq': 8.0,
     'L1_attn_Wk': 8.0,
     'L1_attn_Wv': 8.0,
     'L1_attn_Wo': 8.0}
    for name, (base, spread) in spreads.items():
        noise = np.random.default_rng([zlib.crc32(name.encode()), seed]).standard_normal(out[name].shape)
        drawn = base * np.exp(spread * noise) if base else spread * noise
        out[name] = jnp.asarray(drawn.astype(out[name].dtype))
    for name, factor in factors.items():
        out[name] = (out[name] * factor).astype(out[name].dtype)
    return out
```

```python
import math

import numpy as np

import concourse.bass as bass
from concourse import mybir

F32 = mybir.dt.float32
F32R = mybir.dt.float32r
BF16 = mybir.dt.bfloat16
ALU = mybir.AluOpType
ACT = mybir.ActivationFunctionType
AX = mybir.AxisListType.X

T, D, NT = 1024, 256, 8
H = 16
NE0, NE1, NS1, FF1 = 8, 16, 2, 176
NF = 25
NEG = -1e30
SC0 = 192.0 ** -0.5
G_LO = float(np.float32(0.5 - np.log(4.0 / 3.0)))
G_C = float(np.float32(1.0 / np.e))


class Queue:

    def __init__(self, sem):
        self.sem, self.n, self.ops = sem, 0, []

    def do(self, fn, *waits):
        self.n += 1
        self.ops.append((fn, waits, True))
        return (self.sem, self.n)

    def issue(self, fn, *waits):
        self.ops.append((fn, waits, False))

    def replay(self, eng):
        seen = {}

        def wait(w):
            if w is None:
                return
            if isinstance(w, list):
                for x in w:
                    wait(x)
                return
            sem, value = w
            if seen.get(id(sem), 0) < value:
                seen[id(sem)] = value
                eng.wait_ge(sem, value)

        for fn, waits, signals in self.ops:
            wait(list(waits))
            last = fn(eng)
            if signals:
                last.then_inc(self.sem, 1)


class Loads:

    def __init__(self, sem, queue):
        self.sem, self.q, self.n = sem, queue, 0

    def dma(self, dst, src, *waits):
        self.n += 16
        self.q.issue(lambda e: e.dma_start(dst, src).then_inc(self.sem, 16), *waits)
        return (self.sem, self.n)


def program(nc, a, out):
    def sem(name):
        return nc.alloc_semaphore(name)

    pe, dve, act, pool = (Queue(sem(f"q_{n}")) for n in ("pe", "dve", "act", "pool"))
    sp = Queue(sem("q_sp"))

    base = [16512]

    def sb(name, shape, dt, at=None):
        size = int(np.prod(shape[1:])) * (2 if dt == BF16 else 4)
        size = (size + 31) // 32 * 32
        if at is None:
            at = base[0]
            base[0] += size
        return nc.alloc_sbuf_tensor_at(name, list(shape), dt, offset=at)

    class Region:

        def __init__(self, at):
            self.at = at

        def sb(self, name, shape, dt):
            size = int(np.prod(shape[1:])) * (2 if dt == BF16 else 4)
            size = (size + 31) // 32 * 32
            t = nc.alloc_sbuf_tensor_at(name, list(shape), dt, offset=self.at)
            self.at += size
            assert self.at <= 229344, (name, self.at)
            return t

    bank = [nc.alloc_psum_tensor(f"bank{i}", [128, 512], F32) for i in range(8)]
    free = [None] * 8

    x = sb("x", [128, NT, D], F32)
    hT = sb("hT", [128, 2, T], F32)
    HTP = base[0]
    hTh = sb("hTh", [128, 2, T], F32R)
    hTl = sb("hTl", [128, 2, T], F32R)
    idf = sb("idf", [128, 128], F32)
    idr = sb("idr", [128, 128], F32R)
    ones1 = sb("ones1", [128, 1], F32)
    idb = sb("idb", [128, 128], BF16)
    maskq = sb("maskq", [128, 128], BF16)
    maskk = sb("maskk", [128, 128], BF16)
    dmask = sb("dmask", [11, 4, 128], F32)
    esum = sb("esum", [128, 17], F32)
    ones3 = sb("ones3", [128, 128], F32)
    tri = sb("tri", [128, 16, 16], F32)
    modc = sb("modc", [128, 2, 12], F32)
    gab = sb("gab", [128, 4, D], F32)
    hn = sb("hn", [128, 2, D], F32)
    st6 = sb("st6", [128, NT, 6], F32)
    mv = sb("mv", [128, NT, 2], F32)
    sd = sb("sd", [128, NT], F32)
    rs = sb("rs", [128, NT], F32)
    mp = sb("mp", [128, 3, 4, 2], F32)
    mcat = sb("mcat", [128, 2, 11], F32)
    mbf = sb("mbf", [128, 4], BF16)
    rcp = sb("rcp", [128, 2, 4], F32)
    PHASE = base[0]

    loads = {}

    def group(name):
        loads[name] = Loads(sem(f"d_{name}"), sp)
        return loads[name]

    l_x, l_c, l_mod = group("x"), group("c"), group("mod")
    A = Region(PHASE)
    cosT = A.sb("cosT", [128, T], F32)
    sinT = A.sb("sinT", [128, T], F32)
    W0A = A.at
    w0a = A.sb("w0a", [128, 2, 258], F32)
    WSP = A.at
    wsp = A.sb("wsp", [128, 4, 2, 256], F32)
    wkpe = A.sb("wkpe", [128, 2, 8, 128], F32)
    wqpa = A.sb("wqpa", [128, 8, 128], F32)
    wqpb = A.sb("wqpb", [64, 8, 128], F32)
    waba = A.sb("waba", [128, 16, 64], F32)
    wabb = A.sb("wabb", [64, 16, 64], F32)
    mo = A.sb("mo", [128, 16, 256], F32)
    lnw = A.sb("lnw", [128, 256], F32)
    qmTa = A.sb("qmTa", [128, T], F32)
    qmTb = A.sb("qmTb", [64, T], F32)
    kvT = A.sb("kvT", [128, T], F32)
    kvx = A.sb("kvx", [128, NT, 64], F32)
    gat = A.sb("gat", [128, NT, 2], F32)
    gsb = A.sb("gsb", [128, 2], F32)
    pctx = sb("pctx", [128, NT, D], F32, at=HTP)
    acc = sb("acc", [128, NT, D], F32, at=HTP + 4 * NT * D)
    S0 = A.at
    PB = Region(S0 + 64 * 1024)
    Pb = [PB.sb(f"Pb{i}", [128, 512], F32) for i in range(9)]
    PBE = PB.at
    vx = PB.sb("vx", [128, NT, 16 * 17], F32)
    S = Region(S0)
    qst = S.sb("qst", [107, 16, T], BF16)
    kst = S.sb("kst", [107, 16, T], BF16)
    PJ = Region(S0 + 64 * 1024)
    q32 = PJ.sb("q32", [128, T], F32)
    qr = PJ.sb("qr", [128, T], F32)
    stg = PJ.sb("stg", [128, 3, T], BF16)

    C = Region(S0)
    qbn = C.sb("qbn", [128, 16, 192], F32)
    kvbk = C.sb("kvbk", [128, 16, 64], F32)
    kvbv = C.sb("kvbv", [128, 16, 64], F32)
    owT = C.sb("owT", [128, 16, 256], F32)
    wm = C.sb("wm", [128, 2, 1536], F32)
    cc = C.sb("cc", [128, 2, 2], F32)
    sc_ = C.sb("sc_", [128, 2, 2], F32)
    scb = C.sb("scb", [128, 2, 2, 128], F32)

    for i in range(2):
        l_x.dma(x[:, 4 * i:4 * i + 4, :], a["x"].rearrange("a (i p) d -> p (a i) d", p=128)[:, 4 * i:4 * i + 4, :])
    l_c.dma(idf[:], a["idf"])
    l_c.dma(cc[:], a["cc"])
    l_c.dma(idb[:], a["idb"])
    l_c.dma(maskq[:], a["maskq"])
    l_c.dma(maskk[:], a["maskk"])
    l_c.dma(dmask[:], a["dmask"])
    l_c.dma(tri[:], a["tri"])
    l_c.dma(esum[:], a["esum"])
    l_c.dma(ones3[:], a["ones3"])
    t_c = (l_c.sem, l_c.n)
    t_x = (l_x.sem, l_x.n)
    t_wm = l_mod.dma(wm[:], a["wmod0"])
    l_w = group("w")
    l_w.dma(wsp[:], a["wsp0"])
    t_wsp = (l_w.sem, l_w.n)
    l_w2 = group("w2")
    l_w2.dma(w0a[:], a["w0a"])
    l_w2.dma(lnw[:, 0:192], a["q_ln"].partition_broadcast(128))
    l_w2.dma(lnw[:, 192:256], a["kv_ln"].partition_broadcast(128))
    l_w2.dma(gsb[:], a["gate_b"].partition_broadcast(128))
    t_w2 = (l_w2.sem, l_w2.n)
    l_w3 = group("w3")
    l_w3.dma(qbn[:], a["qbn"])
    l_w3.dma(kvbk[:], a["kvbk"])
    l_w3.dma(kvbv[:], a["kvbv"])
    l_w3.dma(owT[:], a["owT"])
    t_w3 = (l_w3.sem, l_w3.n)
    l_w4 = group("w4")
    for d, s in ((wkpe, "wkpe"), (wqpa, "wqpa"), (wqpb, "wqpb"), (cosT, "cosT"), (sinT, "sinT")):
        l_w4.dma(d[:], a[s])
    t_w4 = (l_w4.sem, l_w4.n)

    t_idr = act.do(lambda e: e.activation(idr[:], idf[:], ACT.Copy), t_c)

    def modulation(layer, t_w):
        c, s = cc[:, layer, :], sc_[:, layer, :]
        t = act.do(lambda e: e.activation(s, c, ACT.Silu), t_c)

        def spread(e):
            for k in range(2):
                last = e.tensor_scalar(scb[:, layer, k, :], idf[:], 0.0, sc_[:, layer, k:k + 1], ALU.mult, ALU.add)
            return last
        t = dve.do(spread, t)

        def cols(e):
            for j in range(12):
                for k in range(2):
                    last = e.matmul(bank[0][:, j:j + 1], wm[:, k, j * 128:(j + 1) * 128], scb[:, layer, k, 0:1],
                                    start=(k == 0), stop=(k == 1))
            return last

        def rows(e):
            for g in range(2):
                for k in range(2):
                    lo = 512 + 768 * g
                    last = e.matmul(bank[1 + g][:, 0:256], scb[:, layer, k, :], wm[:, k, lo:lo + 256],
                                    start=(k == 0), stop=(k == 1))
            return last
        tc = pe.do(cols, t, t_w, free[0])
        tr = pe.do(rows, free[1], free[2])
        t = dve.do(lambda e: e.tensor_copy(modc[:, layer, :], bank[0][:, 0:12]), tc)
        free[0] = t

        def plus1(e):
            e.tensor_scalar(modc[:, layer, 2:4], modc[:, layer, 2:4], 1.0, None, ALU.add)
            return e.tensor_scalar(modc[:, layer, 8:10], modc[:, layer, 8:10], 1.0, None, ALU.add)
        t_cols = dve.do(plus1, t)
        for g in range(2):
            b, o = bank[1 + g][:, 0:256], gab[:, 2 * layer + g, :]
            tmp = hn[:, g, :]
            ta = dve.do(lambda e, b=b, tmp=tmp: e.tensor_scalar(tmp, b, -1.0, 0.25, ALU.mult, ALU.max), tr)
            ta = dve.do(lambda e, b=b, tmp=tmp: e.scalar_tensor_tensor(out=tmp, in0=b, scalar=1.0, in1=tmp,
                                                                      op0=ALU.mult, op1=ALU.max), ta)
            tb = dve.do(lambda e, b=b, o=o: e.tensor_scalar(o, b, 0.0, 2.0, ALU.is_ge, ALU.mult), tr)
            free[1 + g] = tb
            t_g = dve.do(lambda e, o=o, tmp=tmp: e.scalar_tensor_tensor(out=o, in0=o, scalar=-1.0, in1=tmp,
                                                                       op0=ALU.add, op1=ALU.mult), ta, tb)
        return t_cols, t_g, tr

    t_mod0, t_g0, t_pe = modulation(0, t_wm)
    t_wm1 = l_mod.dma(wm[:], a["wmod1"], t_pe)
    t_mod1, t_g1, _ = modulation(1, t_wm1)

    def norm(layer, second, t_in, parts, waits=()):
        s0, c0 = (6, 8) if second else (0, 2)
        ts = []
        for i in range(NT):
            ts.append(dve.do(lambda e, i=i: e.bn_stats(st6[:, i, :], x[:, i, :]), t_in[i]))
        for i in range(NT):
            t = dve.do(lambda e, i=i: e.bn_aggr(mv[:, i, :], st6[:, i, :]), ts[i])
        t = dve.do(lambda e: e.tensor_scalar(sd[:], mv[:, :, 1], 1e-5, None, ALU.add), t)
        t = act.do(lambda e: e.activation(sd[:], sd[:], ACT.Sqrt), t)
        t_rs = dve.do(lambda e: e.reciprocal(rs[:], sd[:]), t)
        t_h, t_p = [], []
        t_tr = [None] * NT
        for half in range(2):
            b0, b1 = 2 * half, 2 * half + 1
            for j in range(4):
                i = 4 * half + j
                t_n = dve.do(lambda e, i=i: e.tensor_scalar(hn[:, i % 2, :], x[:, i, :], mv[:, i, 0:1], rs[:, i:i + 1],
                                                            ALU.subtract, ALU.mult), t_rs, t_tr[i - 2] if i > 1 else None)

                def tr(e, i=i, j=j, b0=b0, b1=b1):
                    e.transpose(bank[b0][:, j * 128:(j + 1) * 128], hn[:, i % 2, 0:128], idf[:])
                    return e.transpose(bank[b1][:, j * 128:(j + 1) * 128], hn[:, i % 2, 128:256], idf[:])
                t_tr[i] = pe.do(tr, t_n, t_c, free[b0], free[b1])
            tt = []
            for k in range(2):
                cs = slice(half * 512, half * 512 + 512)
                te = dve.do(lambda e, k=k, cs=cs, b=b0 + k: e.tensor_scalar(
                    hT[:, k, cs], bank[b][:], modc[:, layer, c0 + k:c0 + k + 1], modc[:, layer, s0 + k:s0 + k + 1],
                    ALU.mult, ALU.add), t_tr[4 * half + 3], t_mod1 if layer else t_mod0, *waits)
                free[b0 + k] = te
                tt.append(te)
                if parts:
                    th = act.do(lambda e, k=k, cs=cs: e.activation(hTh[:, k, cs], hT[:, k, cs], ACT.Copy), te, *waits)
                    tl = dve.do(lambda e, k=k, cs=cs: e.tensor_tensor(
                        hTl[:, k, cs], hT[:, k, cs], hTh[:, k, cs].bitcast(F32), ALU.subtract), th)
                    t_p += [th, tl]
            t_h.append(tt)
        return t_h, t_p

    t_h, _ = norm(0, False, [t_x] * NT, False)
    t_hall = [t_h[0], t_h[1]]

    def project16(layer, w, t_w, t_stack_free, t_pj_free, bq=None, bk=None, bvb=None, scratch=None):
        g_out, g_in = group(f"so{layer}"), group(f"si{layer}")
        t_stg = None
        t_last = None
        t_w32 = None
        for n, (wi, bias) in enumerate(((0, bq), (1, bk))):
            for m in range(2):
                for half in range(2):
                    b = half + 4
                    cs = slice(half * 512, half * 512 + 512)

                    def mm(e, wi=wi, m=m, cs=cs, b=b):
                        for k in range(2):
                            last = e.matmul(bank[b][:], w[:, wi, k, m * 128:(m + 1) * 128], hT[:, k, cs],
                                            start=(k == 0), stop=(k == 1))
                        return last
                    t = pe.do(mm, t_w, t_h_cur[half], free[b])
                    if bias is None:
                        t = act.do(lambda e, cs=cs, b=b: e.activation(q32[:, cs], bank[b][:], ACT.Copy), t, t_pj_free,
                                   t_last)
                    else:
                        t = act.do(lambda e, cs=cs, b=b, bias=bias, m=m: e.activation(
                            q32[:, cs], bank[b][:], ACT.Identity, bias=bias[:, m:m + 1]), t, t_pj_free, t_last)
                    free[b] = t
                t1 = act.do(lambda e: e.activation(stg[:, 0, :], q32[:], ACT.Copy), t, t_stg)
                t2 = dve.do(lambda e: e.tensor_tensor(qr[:], q32[:], stg[:, 0, :], ALU.subtract), t1)
                t_last = t2
                t3 = act.do(lambda e: e.activation(stg[:, 1, :], qr[:], ACT.Copy), t2)
                t4 = dve.do(lambda e: e.tensor_tensor(stg[:, 2, :], qr[:], stg[:, 1, :], ALU.subtract), t3)
                row = (n * 2 + m) * 128
                t_stg = g_out.dma(scratch[row:row + 128, :, :], stg[:], t4)
        t_v = []
        tm = pool.do(lambda e: e.memset(vx[:].rearrange("p i (h c) -> p (i h) c", c=17)[:, :, 16:17], 1.0), t_pj_free)
        for i in range(NT):
            b = 6 + i % 2

            def mm(e, i=i, b=b):
                for k in range(2):
                    last = e.matmul(bank[b][:, 0:256], hT[:, k, i * 128:(i + 1) * 128], w[:, 2, k, :],
                                    start=(k == 0), stop=(k == 1))
                return last
            t = pe.do(mm, t_w, t_h_cur[i // 4], free[b])
            dst = vx[:, i, :].rearrange("p (h c) -> p h c", c=17)[:, :, 0:16]
            src = bank[b][:, 0:256].rearrange("p (h c) -> p h c", c=16)
            if bvb is None:
                t = act.do(lambda e, dst=dst, src=src: e.activation(dst, src, ACT.Copy), t, t_pj_free)
            else:
                t = dve.do(lambda e, dst=dst, src=src: e.tensor_tensor(
                    dst, src, bvb[:].rearrange("p (h c) -> p h c", c=16), ALU.add), t, t_pj_free)
            free[b] = t
            t_v.append(t)
        t_v.append(tm)
        QP, KP = (0, 0, 1, 0, 2, 1), (0, 1, 0, 2, 0, 1)
        for n, (st, parts) in enumerate(((qst, QP), (kst, KP))):
            for s, part in enumerate(parts):
                src = scratch[n * 256:(n + 1) * 256, part, :].rearrange("(h d) t -> d h t", d=16)
                g_in.dma(st[16 * s:16 * s + 16, :, :], src, t_stg, t_stack_free)
            g_in.dma(st[96:107, :, :], a["qrow" if n == 0 else f"krow{layer}"], t_stack_free)
        return (g_in.sem, g_in.n), t_v, (g_in.sem, g_in.n)

    def attention(units, causal, score, row, value, evac, stbanks, extra, scale, G, t_p0, OT, npb, summed=None,
                  mxbanks=(0, 1)):
        n = len(units)
        t_mp, t_tr, t_row = {}, {}, {}
        t_neg = {}
        t_sfree = [t_p0 if summed is None else [t_p0, None]] * len(Pb)
        scount = [0]
        mcount = [0]

        def max_steps(u):
            h, half = units[u]
            steps = []
            for j in range(4):
                qi = 4 * half + j
                for kh in range(2):
                    keys = (qi + 1) * 128 if causal else T
                    c = min(512, keys - 512 * kh)
                    if c > 0:
                        steps.append((j, qi, kh, c))
            return steps

        def do_max(u, step):
            j, qi, kh, c = step
            h, half = units[u]
            b = mxbanks[mcount[0] % len(mxbanks)]
            mcount[0] += 1
            diag = causal and (qi // 4) == kh

            def mm(e):
                last = score(e, "max", h, qi, kh, c, bank[b][:, 0:c])
                if diag:
                    last = e.matmul(bank[b][:, c - 128:c], idb[:], maskq[:], start=False, stop=True,
                                    skip_group_check=True)
                return last
            t = pe.do(mm, free[b], extra(u, "max"))
            t = dve.do(lambda e: e.tensor_reduce(mp[:, u % 3, j, kh:kh + 1], bank[b][:, 0:c], AX, ALU.max), t)
            free[b] = t
            t_mp[u] = t

        def do_neg(u):
            h, half = units[u]
            two = not (causal and half == 0)
            dst = mcat[:, u % 2, 3:7]
            if two:
                t = dve.do(lambda e: e.tensor_reduce(dst, mp[:, u % 3, :, :], AX, ALU.max, negate=True),
                           t_mp[u], t_tr.get(u - 2))
            else:
                t = dve.do(lambda e: e.tensor_scalar(dst, mp[:, u % 3, :, 0], -1.0, None, ALU.mult),
                           t_mp[u], t_tr.get(u - 2))
            t = dve.do(lambda e: e.tensor_copy(mbf[:], dst), t)
            t = dve.do(lambda e: e.tensor_tensor(mcat[:, u % 2, 7:11], dst, mbf[:], ALU.subtract), t)
            t_neg[u] = t

        def do_tr(u):
            t_tr[u] = pe.do(lambda e: e.transpose(bank[6][0:11, 0:128], mcat[:, u % 2, :], idf[:]),
                            t_neg[u], free[6], t_c)

        def do_row(u):
            h, half = units[u]
            o = (qst[96:107, h, half * 512:half * 512 + 512] if row is None else row[u % 2][0:11, :])
            t = dve.do(lambda e: e.tensor_tensor(
                o.rearrange("p (j c) -> p j c", j=4), bank[6][0:11, 0:128].unsqueeze(1).to_broadcast([11, 4, 128]),
                dmask[:], ALU.mult), t_tr[u], t_stdone.get(u - 2))
            free[6] = t
            t_row[u] = t

        t_stdone = {}
        t_exp = {}

        def do_st(u, kt):
            h, half = units[u]
            q0 = max(128 * kt, 512 * half) if causal else 512 * half
            c = 512 * (half + 1) - q0
            b = stbanks[scount[0] % len(stbanks)]
            p = scount[0] % npb
            scount[0] += 1
            diag = causal and kt >= 4 * half

            def mm(e):
                last = score(e, "st", h, kt, q0, c, bank[b][:, 0:c], u)
                if diag:
                    last = e.matmul(bank[b][:, 0:128], idb[:], maskk[:], start=False, stop=True,
                                    skip_group_check=True)
                return last
            t = pe.do(mm, free[b], t_row[u])
            t_stdone[u] = t
            te = act.do(lambda e: e.activation(Pb[p][:, 0:c], bank[b][:, 0:c], ACT.Exp, scale=scale), t, t_sfree[p])
            free[b] = te
            t_exp[u, kt] = (te, p, q0)
            if summed is not None:
                t_sfree[p] = [None, summed(u, kt, Pb[p], te)]
                if kt == 1:
                    p0 = t_exp[u, 0][1]
                    t_sfree[p0] = [t_sfree[p0][0], t_sfree[p][1]]

        def do_pv(u, kts):
            h, half = units[u]
            b = 4 + half
            nk = 4 * half + 4 if causal else NT
            w = 128 // G

            def mm(e):
                for kt in kts:
                    _, p, q0 = t_exp[u, kt]
                    v = value(h, kt)
                    g = w * (kt % G)
                    last = e.matmul(bank[b][g:g + v.shape[1], q0 - 512 * half:512], v, Pb[p][:, 0:512 * (half + 1) - q0],
                                    start=(kt < G), stop=(kt + G >= nk), skip_group_check=True)
                return last
            t = pe.do(mm, [t_exp[u, kt][0] for kt in kts], free[b] if kts[0] == 0 else None, extra(u, "pv"))
            for kt in kts:
                p = t_exp[u, kt][1]
                t_sfree[p] = [t, t_sfree[p][1]] if summed is not None else t
            if kts[-1] == nk - 1:
                to = act.do(lambda e: e.activation(OT[half][:], bank[b][:], ACT.Copy), t, t_ot[half])
                free[b] = to
                later(3, lambda: evac(u, h, half, to, t_ot, later))

        due = []

        def later(n, f):
            due.append((scount[0] + n, f))

        t_ot = [t_p0, t_p0]

        def run_due():
            for d in [d for d in due if d[0] <= scount[0]]:
                due.remove(d)
                d[1]()

        for s in max_steps(0):
            do_max(0, s)
        do_neg(0)
        do_tr(0)
        do_row(0)
        if n > 1:
            for s in max_steps(1):
                do_max(1, s)
        for u in range(n):
            h, half = units[u]
            nk = 4 * half + 4 if causal else NT
            steps = max_steps(u + 2) if u + 2 < n else []
            total, given = len(steps), 0
            extra(u, "begin")
            if u + 1 < n:
                do_neg(u + 1)
            for k in range(nk):
                do_st(u, k)
                if k == 1 and u + 1 < n:
                    do_tr(u + 1)
                    do_row(u + 1)
                while given * nk < total * (k + 1):
                    do_max(u + 2, steps[given])
                    given += 1
                extra(u, ("step", k))
                if k % G == G - 1:
                    due.append((scount[0] + 2, lambda u=u, ks=list(range(k - G + 1, k + 1)): do_pv(u, ks)))
                run_due()
        while due:
            scount[0] += 1
            run_due()

    t_h_cur = t_h

    def fold(e):
        for h in range(H):
            b = 4 + h // 8
            e.matmul(bank[b][:, (h % 8) * 64:(h % 8) * 64 + 64], qbn[:, h, 0:128], kvbk[:, h, :], start=True, stop=True)
        for h in range(H):
            b = 6 + h // 8
            last = e.matmul(bank[b][0:64, (h % 8) * 64:(h % 8) * 64 + 64], qbn[:, h, 128:192], kvbk[:, h, :],
                            start=True, stop=True)
        return last
    t = pe.do(fold, t_w3, free[4], free[5], free[6], free[7])

    def put(e):
        for b in range(2):
            last = e.tensor_copy(waba[:, 8 * b:8 * b + 8, :].rearrange("p h c -> p (h c)"), bank[4 + b][:])
        for b in range(2):
            last = e.tensor_copy(wabb[:, 8 * b:8 * b + 8, :].rearrange("p h c -> p (h c)"), bank[6 + b][0:64, :])
        return last
    t_wab = dve.do(put, t)
    free[4] = free[5] = free[6] = free[7] = t_wab
    for p2 in range(8):
        b = 4 + p2 % 4

        def foldv(e, p2=p2, b=b):
            for q in range(2):
                for s in range(2):
                    h = 2 * p2 + q
                    last = e.matmul(bank[b][64 * s:64 * s + 64, 256 * q:256 * q + 256], kvbv[:, h, :], owT[:, h, :],
                                    start=True, stop=True)
            return last
        t_fold = pe.do(foldv, free[b])
        t_mo = act.do(lambda e, p2=p2, b=b: e.activation(
            mo[:, 2 * p2:2 * p2 + 2, :].rearrange("p a c -> p (a c)"), bank[b][:], ACT.Copy), t_fold)
        free[b] = t_mo

    scratch = nc.dram_tensor("scratch", (512, 3, T), BF16, kind="Internal").ap()
    scratch1 = nc.dram_tensor("scratch1", (512, 3, T), BF16, kind="Internal").ap()
    t_modpe = (pe.sem, pe.n)
    t_stacks, t_v, _ = project16(0, wsp, t_wsp, [t_fold, t_modpe, t_wab, t_g1], None, scratch=scratch)

    sq = PJ.sb("sq", [128, 192], F32)
    ss = PJ.sb("ss", [128, NT, 2], F32)
    rr = PJ.sb("rr", [128, NT, 2], F32)
    rq = PJ.sb("rq", [128, NT, 2], F32)
    gw_ = PJ.sb("gw_", [128, NT, 2], F32)
    gm_ = PJ.sb("gm_", [128, NT], F32)
    qkv = PJ.sb("qkv", [128, 2, 256 + 64], F32)
    assert PJ.at <= PBE
    raw = sb("raw", [128, NT, 256], F32, at=HTP + 4 * NT * D)
    t_pj0 = [(act.sem, act.n), (dve.sem, dve.n)]
    t3 = None
    for i in range(NT):
        b = i % 4

        def mm(e, i=i, b=b):
            for k in range(2):
                last = e.matmul(bank[b][:, 0:258], hT[:, k, i * 128:(i + 1) * 128], w0a[:, k, :],
                                start=(k == 0), stop=(k == 1))
            return last
        t = pe.do(mm, t_w2, t_h[i // 4], free[b])
        t = act.do(lambda e, i=i, b=b: e.activation(raw[:, i, :], bank[b][:, 0:256], ACT.Copy), t)
        t_gw = act.do(lambda e, i=i, b=b: e.activation(gw_[:, i, :], bank[b][:, 256:258], ACT.Copy))
        free[b] = t_gw
        t2 = dve.do(lambda e, i=i: e.tensor_tensor_reduce(sq[:], raw[:, i, 0:192], raw[:, i, 0:192], 1.0 / 192, 0.0,
                                                          ALU.mult, ALU.add, ss[:, i, 0:1]), t, t3)
        t3 = dve.do(lambda e, i=i: e.tensor_tensor_reduce(sq[:, 0:64], raw[:, i, 192:256], raw[:, i, 192:256],
                                                          1.0 / 64, 0.0, ALU.mult, ALU.add, ss[:, i, 1:2]), t2)
    t = dve.do(lambda e: e.tensor_scalar(rr[:], ss[:], 1e-6, None, ALU.add), t2, t3)
    t = act.do(lambda e: e.activation(rr[:], rr[:], ACT.Sqrt), t)
    t_rq = dve.do(lambda e: e.reciprocal(rq[:], rr[:]), t)
    t = dve.do(lambda e: e.tensor_tensor(gw_[:], gw_[:], gsb[:].unsqueeze(1).to_broadcast([128, NT, 2]), ALU.add),
               t_gw)
    t = dve.do(lambda e: e.tensor_reduce(gm_[:], gw_[:], AX, ALU.max), t)
    t = dve.do(lambda e: e.tensor_tensor(gw_[:], gw_[:], gm_[:].unsqueeze(2).to_broadcast([128, NT, 2]),
                                         ALU.subtract), t)
    t = act.do(lambda e: e.activation(gw_[:], gw_[:], ACT.Exp), t)
    t = dve.do(lambda e: e.tensor_reduce(gm_[:], gw_[:], AX, ALU.add), t)
    t = dve.do(lambda e: e.reciprocal(gm_[:], gm_[:]), t)
    t_gat = dve.do(lambda e: e.tensor_tensor(gat[:], gw_[:], gm_[:].unsqueeze(2).to_broadcast([128, NT, 2]),
                                             ALU.mult), t)
    t_ones = pool.do(lambda e: e.memset(ones1[:], 1.0))
    t_qt = [None] * NT
    for half in range(2):
        b0, b1, b2 = 0, 1, 2
        for j in range(4):
            i = 4 * half + j
            z = i % 2

            def sc(e, i=i, z=z):
                e.scalar_tensor_tensor(out=qkv[:, z, 0:192], in0=raw[:, i, 0:192], scalar=rq[:, i, 0:1],
                                       in1=lnw[:, 0:192], op0=ALU.mult, op1=ALU.mult)
                return e.scalar_tensor_tensor(out=qkv[:, z, 192:256], in0=raw[:, i, 192:256], scalar=rq[:, i, 1:2],
                                              in1=lnw[:, 192:256], op0=ALU.mult, op1=ALU.mult)
            t = dve.do(sc, t_rq, t_w2, t_qt[i - 2] if i > 1 else None)
            t = dve.do(lambda e, z=z: e.tensor_copy(qkv[:, z, 256:320], qkv[:, z, 192:256]), t)
            t_kvx = dve.do(lambda e, i=i, z=z: e.tensor_copy(kvx[:, i, 0:64], qkv[:, z, 192:256]), t)

            def tr(e, j=j, z=z):
                js = slice(j * 128, (j + 1) * 128)
                e.transpose(bank[b0][:, js], qkv[:, z, 0:128], idf[:])
                e.transpose(bank[b1][0:64, js], qkv[:, z, 128:192], idf[:])
                return e.transpose(bank[b2][:, js], qkv[:, z, 192:320], idf[:])
            t_qt[i] = pe.do(tr, t_kvx, t, free[b0], free[b1], free[b2])
        cs = slice(half * 512, half * 512 + 512)
        free[b0] = act.do(lambda e, cs=cs: e.activation(qmTa[:, cs], bank[b0][:], ACT.Copy), t_qt[4 * half + 3])
        free[b1] = act.do(lambda e, cs=cs: e.activation(qmTb[:, cs], bank[b1][0:64, :], ACT.Copy), t_qt[4 * half + 3])
        free[b2] = act.do(lambda e, cs=cs: e.activation(kvT[:, cs], bank[b2][:], ACT.Copy), t_qt[4 * half + 3])
    t_lat = [(act.sem, act.n), t_kvx, t_ones]

    t_mc = pool.do(lambda e: e.memset(mcat[:], 1.0))
    units = [(h, half) for h in range(H) for half in range(2)]

    def score16(e, kind, h, i, j, c, o, u=None):
        if kind == "max":
            return e.matmul(o, qst[0:99, h, i * 128:(i + 1) * 128], kst[0:99, h, j * 512:j * 512 + c],
                            start=True, stop=True)
        return e.matmul(o, kst[0:107, h, i * 128:(i + 1) * 128], qst[0:107, h, j:j + c], start=True, stop=True)

    def value16(h, kt):
        return vx[:, kt, h * 17:h * 17 + 17]

    t_rc = {}

    def evac16(gated, dst, causal, OT):
        def f(u, h, half, to, t_ot, later):
            def mm(e):
                for j in range(4):
                    rows = 32 * (j + 1) if causal and half == 0 else 128
                    last = e.matmul(bank[6][:, 128 + 17 * j:145 + 17 * j], OT[half][0:rows, 128 * j:128 * j + 128],
                                    esum[0:rows, :], start=True, stop=True)
                return last
            t = pe.do(mm, to, free[6])
            t_ot[half] = t
            r = rcp[:, u % 2, :]
            v = bank[6][:, 128:196].rearrange("p (j c) -> p j c", c=17)
            tr = dve.do(lambda e: e.reciprocal(r, v[:, :, 16]), t)
            if gated:
                tr = dve.do(lambda e: e.tensor_tensor(r, r, gat[:, 4 * half:4 * half + 4, 1], ALU.mult), tr, t_gat)
            free[6] = dve.do(lambda e: e.tensor_tensor(dst[:, 4 * half:4 * half + 4, h * 16:h * 16 + 16],
                                                       v[:, :, 0:16], r.unsqueeze(2).to_broadcast([128, 4, 16]),
                                                       ALU.mult), tr)
        return f

    def clear(t):
        for b in (4, 5):
            free[b] = dve.do(lambda e, b=b: e.memset(bank[b][:], 0.0), free[b], t)

    t_pj1 = [(act.sem, act.n), (dve.sem, dve.n), (pe.sem, pe.n)]

    def extra16(t_stack, tv):
        def f(u, what):
            if what == "max":
                return [t_stack, t_mc]
            if what == "pv":
                return tv
            return None
        return f

    OTa = [sb(f"OTa{i}", [128, 512], F32, at=HTP + 4 * NT * D + 2048 * i) for i in range(2)]
    clear(t_lat)
    attention(units, False, score16, None, value16, evac16(True, pctx, False, OTa), (2, 3),
              extra16(t_stacks, t_v), 0.25, 4, t_pj1, OTa, 9, mxbanks=(0, 1, 7))

    S2 = Region(S0)
    QKh = [[S2.sb(f"qk{n}h{i}", [128, T], F32R) for i in range(4)] for n in "qk"]
    QKl = [[S2.sb(f"qk{n}l{i}", [128, T], F32R) for i in range(4)] for n in "qk"]
    M0 = Region(WSP)
    t12 = M0.sb("t12", [128, 2, 512], F32)
    Rt = M0.sb("Rt", [128, 512], F32)
    M2 = Region(PBE - 2048)
    mrow = [M2.sb(f"mrow{i}", [128, 512], F32R) for i in range(2)]
    onesr = M2.sb("onesr", [128, 128], F32R)
    OTm = [M2.sb(f"OTm{i}", [128, 512], F32) for i in range(2)]
    Ps = [M2.sb("Ps0", [128, 512], F32), sb("Ps1", [128, 512], F32, at=W0A)]
    t_old = [(pe.sem, pe.n), (dve.sem, dve.n), (act.sem, act.n)]

    def zero(e):
        for i in range(2):
            e.tensor_scalar(mrow[i][:], idf[:, 0:1].to_broadcast([128, 512]), 0.0, None, ALU.mult)
        return e.tensor_copy(onesr[:], ones3[:])
    t_zero = dve.do(zero, t_old, t_c)

    def kvh(e):
        for i in range(4):
            r = slice(0, 64) if i % 2 == 0 else slice(64, 128)
            last = e.activation(QKh[1][i][r, :], kvT[r, :], ACT.Copy)
        return last

    def kvl(e):
        for i in range(4):
            r = slice(0, 64) if i % 2 == 0 else slice(64, 128)
            last = e.tensor_tensor(QKl[1][i][r, :], kvT[r, :], QKh[1][i][r, :].bitcast(F32), ALU.subtract)
        return last
    t_kvh = act.do(kvh, t_old, t_lat)
    t_kvl = dve.do(kvl, t_kvh)

    t_qk = {}
    t_t12, t_R = [None], [None]

    def prep_steps(p, waits):
        z = 2 * (p % 2)
        done = t_qk.setdefault(p, [])

        def rope(n, half):
            cs = slice(half * 512, half * 512 + 512)
            t = {}

            def product():
                def mm(e):
                    if n == 1:
                        for k in range(2):
                            last = e.matmul(bank[7][:], wkpe[:, k, p, :], hT[:, k, cs], start=(k == 0), stop=(k == 1))
                        return last
                    e.matmul(bank[7][:], wqpa[:, p, :], qmTa[:, cs], start=True, stop=False)
                    return e.matmul(bank[7][:], wqpb[:, p, :], qmTb[:, cs], start=False, stop=True)
                t[0] = pe.do(mm, free[7], t_lat, t_w4)

            def swap():
                def f(e):
                    for q in range(4):
                        last = e.activation(t12[32 * (q ^ 1):32 * (q ^ 1) + 32, 1, :], bank[7][32 * q:32 * q + 32, :],
                                            ACT.Copy)
                    return last
                t[1] = act.do(f, t[0], t_t12[0], *waits)

            def turn():
                ts = pool.do(lambda e: e.tensor_tensor(t12[:, 1, :], t12[:, 1, :], sinT[:, cs], ALU.mult), t[1])
                tc = dve.do(lambda e: e.tensor_tensor(t12[:, 0, :], bank[7][:], cosT[:, cs], ALU.mult), t[1],
                            t_t12[0], *waits)
                free[7] = tc
                t[2] = pool.do(lambda e: e.tensor_tensor(Rt[:], t12[:, 0, :], t12[:, 1, :], ALU.add), tc, ts, t_R[0])
                t_t12[0] = t[2]

            def high():
                def hi(e):
                    e.activation(QKh[n][z][64:128, cs], Rt[64:128, :], ACT.Copy)
                    return e.activation(QKh[n][z + 1][0:64, cs], Rt[0:64, :], ACT.Copy)
                t[3] = act.do(hi, t[2], *waits)

            def low():
                def lo(e):
                    e.tensor_tensor(QKl[n][z][64:128, cs], Rt[64:128, :], QKh[n][z][64:128, cs].bitcast(F32),
                                    ALU.subtract)
                    return e.tensor_tensor(QKl[n][z + 1][0:64, cs], Rt[0:64, :], QKh[n][z + 1][0:64, cs].bitcast(F32),
                                           ALU.subtract)
                tl = dve.do(lo, t[3], *waits)
                t_R[0] = tl
                done.extend([t[3], tl])
            return [product, swap, turn, high, low]

        def lat(half):
            cs = slice(half * 512, half * 512 + 512)
            t = {}

            def product():
                def mm(e):
                    wa = waba[:, 2 * p:2 * p + 2, :].rearrange("p h c -> p (h c)")
                    wb = wabb[:, 2 * p:2 * p + 2, :].rearrange("p h c -> p (h c)")
                    e.matmul(bank[7][:], wa, qmTa[:, cs], start=True, stop=False)
                    return e.matmul(bank[7][:], wb, qmTb[:, cs], start=False, stop=True)
                t[0] = pe.do(mm, free[7], t_lat, t_wab)

            def high():
                def hi(e):
                    e.activation(QKh[0][z][0:64, cs], bank[7][0:64, :], ACT.Copy)
                    return e.activation(QKh[0][z + 1][64:128, cs], bank[7][64:128, :], ACT.Copy)
                t[1] = act.do(hi, t[0], *waits)

            def low():
                def lo(e):
                    e.tensor_tensor(QKl[0][z][0:64, cs], bank[7][0:64, :], QKh[0][z][0:64, cs].bitcast(F32),
                                    ALU.subtract)
                    return e.tensor_tensor(QKl[0][z + 1][64:128, cs], bank[7][64:128, :],
                                           QKh[0][z + 1][64:128, cs].bitcast(F32), ALU.subtract)
                tl = dve.do(lo, t[1])
                free[7] = tl
                done.extend([t[1], tl])
            return [product, high, low]
        r = [rope(1, 0), rope(1, 1), rope(0, 0), rope(0, 1)]
        q = [lat(0), lat(1)]
        steps = [(r[0][0],), (r[0][1],), (r[0][2],),
                 (r[1][0],), (r[1][1], r[0][3]), (r[0][4], r[1][2]),
                 (q[0][0],), (q[0][1], r[1][3]), (q[0][2], r[1][4]),
                 (r[2][0],), (r[2][1],), (r[2][2],),
                 (r[3][0],), (r[3][1], r[2][3]), (r[2][4], r[3][2]),
                 (q[1][0],), (q[1][1], r[3][3]), (q[1][2], r[3][4])]
        return steps

    def bufs(h):
        i = 2 * ((h // 2) % 2) + h % 2
        return QKh[0][i], QKl[0][i], QKh[1][i], QKl[1][i]

    def score_main(e, kind, h, i, j, c, o, u=None):
        qh, ql, kh, kl = bufs(h)
        if kind == "max":
            return e.matmul(o, qh[:, i * 128:(i + 1) * 128], kh[:, j * 512:j * 512 + c], start=True, stop=True)
        ks, qs = slice(i * 128, (i + 1) * 128), slice(j, j + c)
        e.matmul(o, kh[:, ks], qh[:, qs], start=True, stop=False)
        e.matmul(o, kh[:, ks], ql[:, qs], start=False, stop=False)
        e.matmul(o, kl[:, ks], qh[:, qs], start=False, stop=False)
        return e.matmul(o, onesr[:], mrow[u % 2][:], start=False, stop=True)

    t_acc = [None] * NT
    t_ps = [t_old, t_old]

    def summed(u, kt, P, te):
        o = Ps[u % 2][:]
        if kt == 0:
            held[u] = P
            return None
        if kt == 1:
            t = pool.do(lambda e: e.tensor_tensor(o, held[u][:], P[:], ALU.add), te, t_ps[u % 2])
        else:
            t = pool.do(lambda e: e.tensor_tensor(o, o, P[:], ALU.add), te, t_ps[u % 2])
        t_ps[u % 2] = t
        return t

    held = {}

    def evac_main(u, h, half, to, t_ot, later):
        def den(e):
            for j in range(4):
                last = e.matmul(bank[4 + half][:, j:j + 1], Ps[u % 2][:, 128 * j:128 * j + 128], ones1[:],
                                start=True, stop=True)
            return last
        t = pe.do(den, t_ps[u % 2], free[4 + half])
        t_ps[u % 2] = t
        r = rcp[:, u % 2, :]
        tr = dve.do(lambda e: e.reciprocal(r, bank[4 + half][:, 0:4]), t)
        free[4 + half] = tr
        tr = dve.do(lambda e: e.tensor_tensor(r, r, gat[:, 4 * half:4 * half + 4, 0], ALU.mult), tr)

        def project(q):
            def mm(e):
                for s in range(2):
                    j = 2 * q + s
                    last = e.matmul(bank[6][:, 256 * s:256 * s + 256], OTm[half][:, 128 * j:128 * j + 128],
                                    mo[:, h, :], start=True, stop=True)
                return last
            t2 = pe.do(mm, to, free[6], t_mo)
            t_ot[half] = t2
            for s in range(2):
                i = 4 * half + 2 * q + s
                src, w = bank[6][:, 256 * s:256 * s + 256], r[:, 2 * q + s:2 * q + s + 1]
                if h == 0:
                    t2 = dve.do(lambda e, i=i, src=src, w=w: e.tensor_scalar(acc[:, i, :], src, w, None, ALU.mult), t2,
                                tr)
                else:
                    t2 = dve.do(lambda e, i=i, src=src, w=w: e.scalar_tensor_tensor(
                        out=acc[:, i, :], in0=src, scalar=w, in1=acc[:, i, :], op0=ALU.mult, op1=ALU.add), t2, tr,
                        t_acc[i])
                t_acc[i] = t2
            free[6] = t2
        later(1, lambda: project(0))
        later(3, lambda: project(1))

    chunks = []

    def extra_main(u, what):
        p = u // 4
        if what == "max":
            return [t_qk[p], t_kvh, t_kvl, t_zero]
        if what == "pv":
            return t_lat
        if what == "begin":
            if u % 4 == 0 and p + 1 < 8:
                chunks.extend(prep_steps(p + 1, [(pe.sem, pe.n)]))
            return None
        if isinstance(what, tuple):
            k = what[1]
            left = 8 * (2 - u % 4) - k
            for _ in range(-(-len(chunks) // left) if left > 0 else len(chunks)):
                for f in chunks.pop(0):
                    f()
        return None

    for step in prep_steps(0, [t_old]):
        for f in step:
            f()
    attention(units, False, score_main, mrow, lambda h, kt: kvx[:, kt, :], evac_main, (2, 3), extra_main,
              SC0, 2, t_old, OTm, 8, summed)

    def out_projection(src, w, t_src, add, t_w, region, name):
        cT = region.sb(name, [128, 2, 2, 128], F32)
        t_x_new, t_c0 = [], [None, None]
        tmp = region.sb(name + "t", [128, 2, D], F32)
        for i in range(NT):
            z = i % 2

            def tr(e, i=i, z=z):
                for k in range(2):
                    last = e.transpose(bank[z][:, k * 128:(k + 1) * 128], src[:, i, k * 128:(k + 1) * 128], idf[:])
                return last
            t = pe.do(tr, t_src, free[z])
            t = act.do(lambda e, z=z: e.activation(cT[:, z, :, :].rearrange("p k c -> p (k c)"), bank[z][:, 0:256],
                                                   ACT.Copy), t, t_c0[z])
            free[z] = t

            def mm(e, z=z):
                for k in range(2):
                    last = e.matmul(bank[2 + z][:, 0:256], cT[:, z, k, :], w[:, 3, k, :], start=(k == 0),
                                    stop=(k == 1))
                return last
            t = pe.do(mm, t, free[2 + z], t_w)
            t_c0[z] = t
            t = dve.do(lambda e, i=i, z=z: e.tensor_tensor(tmp[:, z, :], bank[2 + z][:, 0:256], add(i), ALU.add), t,
                       t_src)
            free[2 + z] = t
            layer = 0 if name == "cT0" else 1
            t = dve.do(lambda e, z=z, layer=layer: e.tensor_tensor(tmp[:, z, :], tmp[:, z, :], gab[:, 2 * layer, :],
                                                                   ALU.mult), t, t_g0, t_g1)
            t = dve.do(lambda e, i=i, z=z: e.tensor_tensor(x[:, i, :], x[:, i, :], tmp[:, z, :], ALU.add), t)
            t_x_new.append(t)
        return t_x_new

    t_x1 = out_projection(pctx, wsp, [(dve.sem, dve.n)], lambda i: acc[:, i, :], t_wsp, Region(S0), "cT0")

    F = Region(PHASE)
    t_phase = [(pe.sem, pe.n), (dve.sem, dve.n), (act.sem, act.n), (pool.sem, pool.n)]
    acc0 = F.sb("acc0", [128, NT, D], F32)
    wr = F.sb("wr", [128, 2, 8], F32)
    tmpr = F.sb("tmpr", [128, 2], F32)
    wraw = F.sb("wraw", [128, 2, 6 * 256], F32)
    wh = [F.sb(f"wh{i}", [128, 6 * 256], F32R) for i in range(2)]
    wl = [F.sb(f"wl{i}", [128, 6 * 256], F32R) for i in range(2)]
    sg = F.sb("sg", [128, 2, 512], F32)
    hf = F.sb("hf", [128, 2, 512], F32)
    hh = [F.sb(f"hh{i}", [128, 2, T], F32R) for i in range(2)]
    hl = [F.sb(f"hl{i}", [128, 2, T], F32R) for i in range(2)]
    gz = F.sb("gz", [128, 8, 64], F32)
    g64 = F.sb("g64", [128, 3, NT * 64], F32)
    l_f = group("f0")
    l_f.dma(wr[:], a["wr"], t_phase)
    l_f.dma(tmpr[:, 0:1], a["temp"].partition_broadcast(128), t_phase)
    t_fr = (l_f.sem, l_f.n)
    l_fw = [group("fw0"), group("fw1")]
    t_wraw = [None] * 8
    for i in range(2):
        t_wraw[i] = l_fw[i].dma(wraw[:, i, :], a["wf0"][i], t_phase)

    t_h, t_p = norm(0, True, t_x1, True)
    t_h_cur = t_h

    def logits(e):
        for i in range(NT):
            for k in range(2):
                last = e.matmul(bank[4][:, i * 8:i * 8 + 8], hT[:, k, i * 128:(i + 1) * 128], wr[:, k, :],
                                start=(k == 0), stop=(k == 1))
        return last
    t_lg = pe.do(logits, t_h[0], t_h[1], t_fr, free[4])
    t = dve.do(lambda e: e.reciprocal(tmpr[:, 1:2], tmpr[:, 0:1]), t_fr)
    Z = [gz[:, i, :] for i in range(8)]
    V = [gz[:, i, :].rearrange("p (i e) -> p i e", e=8) for i in range(8)]

    def chain(steps, t):
        for q, f in steps:
            t = q.do(f, t)
        return t

    def bc(v):
        return v.unsqueeze(2).to_broadcast([128, NT, 8])
    s1 = [g64[:, 0, i * 8:i * 8 + 8] for i in range(4)]
    big = g64[:, 1, :].rearrange("p (i j k) -> p i j k", j=8, k=8)
    big2 = g64[:, 2, :].rearrange("p (i j k) -> p i j k", j=8, k=8)
    small = [gz[:, 7, i * 8:i * 8 + 8] for i in range(4)]

    def rank_steps(f, ne, o, bigs, tri_):
        b1, b2 = bigs

        def pairs(e, op, dst, i):
            v = f[:, i, :]
            return e.tensor_tensor(dst[:, i, :, :], v.unsqueeze(1).to_broadcast([128, ne, ne]),
                                   v.unsqueeze(2).to_broadcast([128, ne, ne]), op)

        def gt(e):
            for i in range(NT):
                last = pairs(e, ALU.is_gt, b1, i)
            return last

        def eq(e):
            for i in range(NT):
                last = pairs(e, ALU.is_equal, b2, i)
            return last

        def low(e):
            for i in range(NT):
                last = e.tensor_tensor(b2[:, i, :, :], b2[:, i, :, :], tri_, ALU.mult)
            return last
        return [(dve, gt), (dve, eq), (dve, low),
                (dve, lambda e: e.tensor_tensor(b1.rearrange("p i j k -> p (i j k)"),
                                                b1.rearrange("p i j k -> p (i j k)"),
                                                b2.rearrange("p i j k -> p (i j k)"), ALU.add)),
                (dve, lambda e: e.tensor_reduce(o, b1.rearrange("p i j k -> p (i j) k"), AX, ALU.add))]

    t = chain([
        (dve, lambda e: e.tensor_scalar(Z[0], bank[4][:, 0:64], tmpr[:, 1:2], -1.0, ALU.mult, ALU.mult)),
        (act, lambda e: e.activation(Z[0], Z[0], ACT.Exp)),
        (dve, lambda e: e.tensor_scalar(Z[0], Z[0], 1.0, None, ALU.add)),
        (dve, lambda e: e.reciprocal(Z[0], Z[0])),
    ], [t, t_lg])
    free[4] = t
    t = chain([
        (dve, lambda e: e.tensor_scalar(Z[1], Z[0], G_C, None, ALU.subtract)),
        (dve, lambda e: e.scalar_tensor_tensor(out=Z[1], in0=Z[1], scalar=-1.0, in1=Z[1], op0=ALU.mult, op1=ALU.max)),
        (dve, lambda e: e.tensor_scalar(Z[2], Z[0], G_LO, None, ALU.is_ge)),
        (dve, lambda e: e.tensor_scalar(Z[3], Z[0], 0.5, None, ALU.is_le)),
        (dve, lambda e: e.tensor_tensor(Z[2], Z[2], Z[3], ALU.mult)),
        (act, lambda e: e.activation(Z[3], Z[1], ACT.Exp, scale=-1.0 / 0.1)),
        (act, lambda e: e.activation(Z[4], Z[1], ACT.Exp, scale=-1.0 / 0.3)),
        (dve, lambda e: e.tensor_tensor(Z[2], Z[2], Z[3], ALU.mult)),
        (dve, lambda e: e.tensor_reduce(small[0], V[2], AX, ALU.add)),
        (dve, lambda e: e.tensor_scalar(small[0], small[0], 1e-8, None, ALU.is_lt)),
    ] + rank_steps(V[4], 8, Z[5], (big, big2), tri[:, 0:8, 0:8]) + [
        (dve, lambda e: e.scalar_tensor_tensor(out=Z[4], in0=Z[5], scalar=2.0, in1=Z[4], op0=ALU.is_lt, op1=ALU.mult)),
        (dve, lambda e: e.tensor_reduce(small[1], V[4], AX, ALU.add)),
        (dve, lambda e: e.tensor_scalar(small[1], small[1], 1e-8, None, ALU.max)),
        (dve, lambda e: e.reciprocal(small[1], small[1])),
        (dve, lambda e: e.tensor_tensor(small[1], small[1], small[0], ALU.mult)),
        (dve, lambda e: e.tensor_tensor(V[4], V[4], bc(small[1]), ALU.mult)),
        (dve, lambda e: e.tensor_scalar(small[0], small[0], -1.0, 1.0, ALU.mult, ALU.add)),
        (dve, lambda e: e.tensor_tensor(V[2], V[2], bc(small[0]), ALU.mult)),
        (dve, lambda e: e.tensor_tensor(Z[2], Z[2], Z[4], ALU.add)),
        (dve, lambda e: e.tensor_reduce(small[2], V[2], AX, ALU.add)),
        (dve, lambda e: e.tensor_scalar(small[2], small[2], 1e-8, None, ALU.max)),
        (dve, lambda e: e.reciprocal(small[2], small[2])),
        (dve, lambda e: e.tensor_tensor(V[6], V[2], bc(small[2]), ALU.mult)),
    ], t)
    t_gw = t

    def three(e, o, lh, ll, rh, rl, start, stop, **k):
        e.matmul(o, lh, rh, start=start, stop=False, **k)
        e.matmul(o, lh, rl, start=False, stop=False, **k)
        return e.matmul(o, ll, rh, start=False, stop=stop, **k)

    t_down = {}
    t_hf = [None, None]
    t_sg = [None, None]
    t_a0 = [None] * NT
    down_q = []
    nf = [0]

    def split_w(e_):
        z = e_ % 2
        th = act.do(lambda e: e.activation(wh[z][:], wraw[:, z, :], ACT.Copy), t_wraw[e_], t_down.get(e_ - 2))
        tl = dve.do(lambda e: e.tensor_tensor(wl[z][:], wraw[:, z, :], wh[z][:].bitcast(F32), ALU.subtract), th)
        if e_ + 2 < 8:
            t_wraw[e_ + 2] = l_fw[z].dma(wraw[:, z, :], a["wf0"][e_ + 2], th, tl)
        return [th, tl]

    def up0(e_, m, half, tw):
        z = e_ % 2
        cs = slice(half * 512, half * 512 + 512)
        n = nf[0] % 2
        nf[0] += 1
        bg, bu = 2 * n, 2 * n + 1

        def mm(e):
            for g, b in ((0, bg), (1, bu)):
                for k in range(2):
                    ws = slice((2 * g + k) * 256 + m * 128, (2 * g + k) * 256 + m * 128 + 128)
                    last = three(e, bank[b][:], wh[z][:, ws], wl[z][:, ws], hTh[:, k, cs], hTl[:, k, cs], k == 0, k == 1)
            return last
        t = pe.do(mm, tw, t_p, free[bg], free[bu])
        t1 = act.do(lambda e: e.activation(sg[:, n, :], bank[bg][:], ACT.Silu), t, t_sg[n])
        free[bg] = t1
        t2 = dve.do(lambda e: e.tensor_tensor(hf[:, n, :], sg[:, n, :], bank[bu][:], ALU.mult), t1, t_hf[n])
        free[bu] = t_sg[n] = t2
        th = act.do(lambda e: e.activation(hh[z][:, m, cs], hf[:, n, :], ACT.Copy), t2, t_down.get(e_ - 2))
        tl = pool.do(lambda e: e.tensor_tensor(hl[z][:, m, cs], hf[:, n, :], hh[z][:, m, cs].bitcast(F32),
                                               ALU.subtract), th)
        t_hf[n] = tl
        return [th, tl]

    def down0(e_, i, th):
        z = e_ % 2
        b = 4 + i % 4
        ts = slice(i * 128, (i + 1) * 128)

        def mm(e):
            for k in range(2):
                ws = slice((4 + k) * 256, (5 + k) * 256)
                last = three(e, bank[b][:, 0:256], hh[z][:, k, ts], hl[z][:, k, ts], wh[z][:, ws], wl[z][:, ws],
                             k == 0, k == 1)
            return last
        t = pe.do(mm, th, free[b])
        t_down[e_] = t
        w = gz[:, 6, i * 8 + e_:i * 8 + e_ + 1]
        if e_ == 0:
            t = dve.do(lambda e: e.tensor_scalar(acc0[:, i, :], bank[b][:, 0:256], w, None, ALU.mult), t, t_gw)
        else:
            t = dve.do(lambda e: e.scalar_tensor_tensor(out=acc0[:, i, :], in0=bank[b][:, 0:256], scalar=w,
                                                        in1=acc0[:, i, :], op0=ALU.mult, op1=ALU.add), t, t_a0[i])
        free[b] = t_a0[i] = t

    tw = split_w(0)
    for e_ in range(8):
        ths = [[], []]
        for half in range(2):
            for m in range(2):
                ths[half] += up0(e_, m, half, tw)
                for _ in range(2):
                    if down_q:
                        down0(*down_q.pop(0))
        if e_ + 1 < 8:
            tw = split_w(e_ + 1)
        down_q = [(e_, i, ths[i // 4]) for i in range(NT)]
    for d in down_q:
        down0(*d)
    t_x2 = []
    for i in range(NT):
        t = dve.do(lambda e, i=i: e.tensor_tensor(acc0[:, i, :], acc0[:, i, :], gab[:, 1, :], ALU.mult), t_a0[i], t_g0)
        t_x2.append(dve.do(lambda e, i=i: e.tensor_tensor(x[:, i, :], x[:, i, :], acc0[:, i, :], ALU.add), t))

    t_phase = [(pe.sem, pe.n), (dve.sem, dve.n), (act.sem, act.n), (pool.sem, pool.n)]
    bcol = F_at = Region(PHASE + 8 * 1024)
    w1a = F_at.sb("w1a", [128, 4, 2, 256], F32)
    bcol = F_at.sb("bcol", [128, 4], F32)
    bvb = F_at.sb("bvb", [128, 256], F32)
    bob = F_at.sb("bob", [128, 256], F32)
    octx = F_at.sb("octx", [128, NT, D], F32)
    assert F_at.at <= S0
    l_a1 = group("a1")
    l_a1.dma(w1a[:], a["w1a"], t_phase)
    l_a1.dma(bcol[:], a["bqk"], t_phase)
    l_a1.dma(bvb[:], a["bv"].partition_broadcast(128), t_phase)
    l_a1.dma(bob[:], a["bo"].partition_broadcast(128), t_phase)
    t_w1a = (l_a1.sem, l_a1.n)
    t_h, _ = norm(1, False, t_x2, False)
    t_h_cur = t_h
    t_stacks, t_v, _ = project16(1, w1a, t_w1a, t_phase, t_phase, bq=bcol[:, 0:2], bk=bcol[:, 2:4], bvb=bvb,
                                 scratch=scratch1)
    t_pj = [(act.sem, act.n), (dve.sem, dve.n), (pe.sem, pe.n)]
    t_mc = dve.do(lambda e: e.memset(mcat[:], 1.0), t_pj)
    clear(t_pj)
    attention(units, True, score16, None, value16, evac16(False, octx, True, OTa), (2, 3),
              extra16(t_stacks, t_v), 0.25, 4, t_pj, OTa, 9, mxbanks=(0, 1, 7))
    t_x3 = out_projection(octx, w1a, [(dve.sem, dve.n)], lambda i: bob[:], t_w1a, Region(S0), "cT1")

    t_phase = [(pe.sem, pe.n), (dve.sem, dve.n), (act.sem, act.n), (pool.sem, pool.n)]
    E = Region(PHASE)
    cen = E.sb("cen", [128, 2, 16], F32)
    bib = E.sb("bib", [128, 16], F32)
    b1c = E.sb("b1c", [128, NF], F32)
    b2r = E.sb("b2r", [18, 256], F32)
    selt = E.sb("selt", [113, NF * 128], BF16)
    wr1 = E.sb("wr1", [128, 4, 512], F32)
    v1h = [E.sb(f"v1h{i}", [128, 512], F32R) for i in range(4)]
    v1l = [E.sb(f"v1l{i}", [128, 512], F32R) for i in range(4)]
    gc = E.sb("gc", [128, NT, 113], F32)
    g3 = E.sb("g3", [113, T], BF16)
    gT = E.sb("gT", [18, T], F32)
    sgm = E.sb("sgm", [128, 3, 128], F32)
    gb3 = E.sb("gb3", [128, NT, 16], BF16)
    pr1 = E.sb("pr1", [128, NT * 256], F32)
    pr2 = E.sb("pr2", [128, NT * 256], F32)
    rl = E.sb("rl", [128, 2, 512], F32)
    hg = E.sb("hg", [128, 2, 512], F32)
    h1h = [E.sb(f"h1h{i}", [128, T], F32R) for i in range(2)]
    h1l = [E.sb(f"h1l{i}", [128, T], F32R) for i in range(2)]
    fin = E.sb("fin", [128, 2, 512], F32)
    l_e = group("e")
    l_e.dma(cen[:], a["cen"], t_phase)
    l_e.dma(bib[:], a["ebias"].partition_broadcast(128), t_phase)
    l_e.dma(b1c[:], a["b1c"], t_phase)
    l_e.dma(b2r[:], a["b2r"], t_phase)
    l_e.dma(selt[64:113, :], a["sel"], t_phase)
    t_e = (l_e.sem, l_e.n)
    l_ew = [group(f"ew{i}") for i in range(4)]
    t_ew = [None] * NF
    for i in range(4):
        t_ew[i] = l_ew[i].dma(wr1[:, i, :], a["wf1"][i], t_phase)
    t_gc0 = dve.do(lambda e: e.memset(gc[:], 1.0), t_phase)

    t_h, t_p = norm(1, True, t_x3, True)

    def logits1(e):
        for i in range(NT):
            for k in range(2):
                last = e.matmul(bank[6][:, i * 16:i * 16 + 16], hT[:, k, i * 128:(i + 1) * 128], cen[:, k, :],
                                start=(k == 0), stop=(k == 1))
        return last
    t = pe.do(logits1, t_h[0], t_h[1], t_e, free[6])
    sgf = [sgm[:, i, :] for i in range(3)]
    sgv = [sgm[:, i, :].rearrange("p (i e) -> p i e", e=16) for i in range(3)]
    sm = sd
    t = chain([
        (act, lambda e: e.activation(sgf[0], bank[6][:, 0:128], ACT.Exp, scale=-1.0)),
        (dve, lambda e: e.tensor_scalar(sgf[0], sgf[0], 1.0, None, ALU.add)),
        (dve, lambda e: e.reciprocal(sgf[0], sgf[0])),
        (dve, lambda e: e.tensor_tensor(sgv[0], sgv[0], bib[:].unsqueeze(1).to_broadcast([128, NT, 16]), ALU.add)),
    ] + rank_steps(sgv[0], 16, sgf[1], (pr1[:].rearrange("p (i j k) -> p i j k", j=16, k=16),
                                        pr2[:].rearrange("p (i j k) -> p i j k", j=16, k=16)), tri[:]) + [
        (dve, lambda e: e.scalar_tensor_tensor(out=sgf[0], in0=sgf[1], scalar=4.0, in1=sgf[0], op0=ALU.is_lt,
                                               op1=ALU.mult)),
        (dve, lambda e: e.tensor_reduce(sm[:], sgv[0], AX, ALU.add)),
        (dve, lambda e: e.tensor_scalar(sm[:], sm[:], 1e-8, None, ALU.max)),
        (dve, lambda e: e.reciprocal(sm[:], sm[:])),
        (dve, lambda e: e.tensor_tensor(gc[:, :, 0:16], sgv[0], sm[:].unsqueeze(2).to_broadcast([128, NT, 16]),
                                        ALU.mult)),
        (dve, lambda e: e.tensor_copy(gb3[:], gc[:, :, 0:16])),
        (dve, lambda e: e.tensor_copy(gc[:, :, 64:80], gb3[:])),
        (dve, lambda e: e.tensor_tensor(sgv[1], gc[:, :, 0:16], gc[:, :, 64:80], ALU.subtract)),
        (dve, lambda e: e.tensor_copy(gb3[:], sgv[1])),
        (dve, lambda e: e.tensor_copy(gc[:, :, 80:96], gb3[:])),
        (dve, lambda e: e.tensor_tensor(gc[:, :, 96:112], sgv[1], gc[:, :, 80:96], ALU.subtract)),
    ], [t, t_gc0])
    free[6] = t
    t_gt = []
    for half in range(2):
        b = 6 + half

        def tr(e, half=half, b=b):
            for j in range(4):
                last = e.transpose(bank[b][0:113, j * 128:(j + 1) * 128], gc[:, 4 * half + j, :], idf[:])
            return last
        tt = pe.do(tr, t, free[b])
        cs = slice(half * 512, half * 512 + 512)
        t1 = act.do(lambda e, b=b, cs=cs: e.activation(g3[64:113, cs], bank[b][64:113, :], ACT.Copy), tt)
        t2 = act.do(lambda e, b=b, cs=cs: e.activation(gT[:, cs], bank[b][0:18, :], ACT.Copy), tt)
        free[b] = t2
        t_gt += [t1, t2]

    def begin_sums(e):
        for i in range(NT):
            o = bank[i // 2][:, 256 * (i % 2):256 * (i % 2) + 256]
            ts = slice(i * 128, (i + 1) * 128)
            e.matmul(o, gT[:, ts], b2r[:], start=(i % 2 == 0), stop=False, skip_group_check=True)
            for k in range(2):
                for part in (hTh, hTl):
                    last = e.matmul(o[:, k * 128:(k + 1) * 128], part[:, k, ts], idr[:], start=False, stop=False,
                                    skip_group_check=True)
        return last
    pe.do(begin_sums, t_gt, t_p, t_e, t_idr, free[0], free[1], free[2], free[3])

    t_w1 = [None] * NF
    t_dn = [None] * NF
    t_rl, t_hg = [None, None], [None, None]

    def split1(f):
        z = f % 4
        th = act.do(lambda e: e.activation(v1h[z][:], wr1[:, z, :], ACT.Copy), t_ew[f], t_dn[f - 4] if f > 3 else None)
        tl = pool.do(lambda e: e.tensor_tensor(v1l[z][:], wr1[:, z, :], v1h[z][:].bitcast(F32), ALU.subtract), th)
        if f + 4 < NF:
            t_ew[f + 4] = l_ew[z].dma(wr1[:, z, :], a["wf1"][f + 4], th, tl)
        t_w1[f] = [th, tl]

    def up1(f, half):
        z, y = f % 4, f % 2
        cs = slice(half * 512, half * 512 + 512)
        bu, bg = 4 + half, 6 + half

        def mm(e):
            e.matmul(bank[bg][:], selt[64:113, f * 128:(f + 1) * 128], g3[64:113, cs], start=True, stop=True)
            for k in range(2):
                ws = slice(k * 128, (k + 1) * 128)
                last = three(e, bank[bu][:], v1h[z][:, ws], v1l[z][:, ws], hTh[:, k, cs], hTl[:, k, cs], k == 0, k == 1)
            return last
        t = pe.do(mm, t_w1[f], t_gt, free[bu], free[bg])
        t1 = act.do(lambda e: e.activation(rl[:, half, :], bank[bu][:], ACT.Relu, bias=b1c[:, f:f + 1]), t, t_rl[half])
        free[bu] = t1
        t2 = dve.do(lambda e: e.tensor_tensor(hg[:, half, :], rl[:, half, :], bank[bg][:], ALU.mult), t1, t_hg[half])
        free[bg] = t_rl[half] = t2
        th = act.do(lambda e: e.activation(h1h[y][:, cs], hg[:, half, :], ACT.Copy), t2, t_dn[f - 2] if f > 1 else None)
        tl = dve.do(lambda e: e.tensor_tensor(h1l[y][:, cs], hg[:, half, :], h1h[y][:, cs].bitcast(F32), ALU.subtract),
                    th)
        t_hg[half] = tl
        return [th, tl]

    def down1(f, half, th):
        z, y = f % 4, f % 2

        def mm(e):
            for i in range(4 * half, 4 * half + 4):
                o = bank[i // 2][:, 256 * (i % 2):256 * (i % 2) + 256]
                ts = slice(i * 128, (i + 1) * 128)
                last = three(e, o, h1h[y][:, ts], h1l[y][:, ts], v1h[z][:, 256:512], v1l[z][:, 256:512], False,
                             f == NF - 1, skip_group_check=True)
            return last
        t_dn[f] = pe.do(mm, th)
        return t_dn[f]

    split1(0)
    split1(1)
    ready_h = []
    t_out = {}
    for f in range(NF):
        if f + 2 < NF:
            split1(f + 2)
        for half in range(2):
            th = up1(f, half)
            ready_h.append((f, half, th))
            if len(ready_h) > 2:
                down1(*ready_h.pop(0))
    for r in ready_h:
        t_out[r[1]] = down1(*r)
    l_o = group("out")
    out_v = out.rearrange("a (i p) d -> p (a i) d", p=128)
    t_st = [None, None]
    for j in range(4):
        g = gab[:, 3, :].unsqueeze(1).to_broadcast([128, 2, 256])
        o = fin[:, j % 2, :].rearrange("p (a c) -> p a c", a=2)
        src = bank[j][:].rearrange("p (a c) -> p a c", a=2)
        t = dve.do(lambda e, o=o, src=src, g=g: e.tensor_tensor(o, src, g, ALU.mult), t_out[j // 2], t_st[j % 2], t_g1)
        xs = x[:, 2 * j:2 * j + 2, :]
        t = dve.do(lambda e, o=o, xs=xs: e.tensor_tensor(xs, xs, o, ALU.add), t)
        t_st[j % 2] = t
        l_o.dma(out_v[:, 2 * j:2 * j + 2, :], xs, t)
    sp.ops.append((lambda e: e.wait_ge(l_o.sem, l_o.n), (), False))

    with nc.Block() as block:
        block.sync(sp.replay)
        block.gpsimd(pool.replay)
        block.scalar(act.replay)
        block.vector(dve.replay)
        block.tensor(pe.replay)


def bits(x):
    u = np.ascontiguousarray(x, np.float32).view(np.uint32)
    return ((u + 0x7FFF + ((u >> 16) & 1)) >> 16).astype(np.uint16)


def value_of(b):
    return (b.astype(np.uint32) << 16).view(np.float32)


def constants():
    c = {}
    eye = np.eye(128, dtype=np.float32)
    c["idf"] = eye
    c["idb"] = bits(eye)
    q, k = np.arange(128)[:, None], np.arange(128)[None, :]
    c["maskq"] = bits(np.where(k > q, NEG, 0.0))
    c["maskk"] = np.ascontiguousarray(c["maskq"].T)
    dm = np.zeros((11, 4, 128), np.float32)
    dm[0:3] = 1.0
    for j in range(4):
        dm[3 + j, j] = 1.0
        dm[7 + j, j] = 1.0
    c["dmask"] = dm
    es = np.zeros((128, 17), np.float32)
    for g in range(4):
        es[32 * g:32 * g + 17] = np.eye(17)
    c["esum"] = es
    c["ones3"] = np.ones((128, 128), np.float32)
    c["ones3"][0:3] = 0.0
    j = np.arange(16)
    c["tri"] = np.broadcast_to((j[None, :] < j[:, None]).astype(np.float32), (128, 16, 16)).copy()
    inv = (np.float32(1.0) / np.power(np.float32(10000.0), np.arange(0, 64, 2, dtype=np.float32) / np.float32(64)))
    fr = np.outer(np.arange(T, dtype=np.float32), inv.astype(np.float32)).astype(np.float32)
    cos, sin = np.cos(fr).T.astype(np.float32), np.sin(fr).T.astype(np.float32)
    c["cosT"] = np.concatenate([cos] * 4, 0)
    c["sinT"] = np.concatenate([-sin, sin] * 2, 0)
    start = 2 ** (-2 ** (-(math.log2(H) - 3)))
    slopes = np.array([start * start ** i for i in range(H)], np.float32)
    al = (slopes[:, None] * (np.arange(T, dtype=np.float32) - np.float32(T - 1))[None, :]) * np.float32(4)
    rows = np.ones((11, H, T), np.float32)
    c["qrow"] = bits(rows)
    k0 = rows.copy()
    k0[0:3] = 0.0
    c["krow0"] = bits(k0)
    r = al.astype(np.float32)
    k1 = bits(rows)
    for i in range(3):
        k1[i] = bits(r)
        r = r - value_of(k1[i])
    c["krow1"] = k1
    sel = np.zeros((49, NF * 128), np.float32)
    ex = np.arange(NF * 128) // FF1
    for f in range((NS1 + NE1) * FF1):
        if ex[f] < NS1:
            sel[48, f] = 1.0
        else:
            for p in range(3):
                sel[16 * p + ex[f] - NS1, f] = 1.0
    c["sel"] = bits(sel)
    return c


def layout(i):
    def rows2(w):
        return np.ascontiguousarray(w.reshape(2, 128, -1).transpose(1, 0, 2))

    def cat(*w):
        return np.concatenate(w, 0)
    d = {"x": i["L0_attn_hidden_states"]}
    d["cc"] = np.ascontiguousarray(np.stack([i["L0_c"][0], i["L1_c"][0]], 0).reshape(2, 2, 128).transpose(2, 0, 1))
    d["wmod0"], d["wmod1"] = rows2(i["L0_wmod"]), rows2(i["L1_wmod"])
    kva = i["L0_attn_kv_a_w"]
    d["w0a"] = rows2(cat(i["L0_attn_q_a_w"], kva[:64], i["L0_attn_gate_w"]).T)
    d["q_ln"], d["kv_ln"], d["gate_b"] = i["L0_attn_q_a_ln_w"], i["L0_attn_kv_a_ln_w"], i["L0_attn_gate_b"]
    kpe = kva[64:].reshape(8, 2, 64, 256)[:, ::-1].reshape(1024, 256).T
    d["wkpe"] = np.ascontiguousarray(kpe.reshape(2, 128, 8, 128).transpose(1, 0, 2, 3))
    qb = i["L0_attn_q_b_w"].reshape(16, 192, 192)
    qpe = qb[:, 128:, :].reshape(8, 2, 64, 192)[:, ::-1].reshape(8, 128, 192).transpose(2, 0, 1)
    d["wqpa"], d["wqpb"] = np.ascontiguousarray(qpe[:128]), np.ascontiguousarray(qpe[128:])
    d["qbn"] = np.ascontiguousarray(qb[:, :128, :].transpose(1, 0, 2))
    kvb = i["L0_attn_kv_b_w"].reshape(16, 256, 64)
    d["kvbk"] = np.ascontiguousarray(kvb[:, :128].transpose(1, 0, 2))
    d["kvbv"] = np.ascontiguousarray(kvb[:, 128:].transpose(1, 0, 2))
    d["owT"] = np.ascontiguousarray(i["L0_attn_o_w"].reshape(256, 16, 128).transpose(2, 1, 0))
    d["wsp0"] = np.ascontiguousarray(np.stack(
        [rows2(i[f"L0_attn_sp_{n}_w"].T) for n in "qkvo"], 1))
    d["wr"], d["temp"] = rows2(i["L0_ffn_Wr"]), i["L0_ffn_temperature"]

    def tiles(w):
        return w.reshape(8, 2, 128, 256).transpose(0, 2, 1, 3).reshape(8, 128, 512)
    d["wf0"] = np.ascontiguousarray(np.concatenate(
        [tiles(i["L0_ffn_Wg"]), tiles(i["L0_ffn_Wu"]), tiles(i["L0_ffn_Wd"])], 2))
    d["w1a"] = np.ascontiguousarray(np.stack([rows2(i[f"L1_attn_W{n}"]) for n in "qkvo"], 1))
    d["bqk"] = np.ascontiguousarray(np.concatenate(
        [i["L1_attn_bq"].reshape(2, 128).T, i["L1_attn_bk"].reshape(2, 128).T], 1))
    d["bv"], d["bo"] = i["L1_attn_bv"], i["L1_attn_bo"]
    d["cen"] = rows2(i["L1_ffn_centroids"].T)
    d["ebias"] = i["L1_ffn_bias"]
    pad = NF * 128 - 18 * FF1
    w1 = cat(i["L1_ffn_shared_w1"], i["L1_ffn_routed_w1"]).transpose(1, 0, 2).reshape(256, 18 * FF1)
    w1 = np.concatenate([w1, np.zeros((256, pad), w1.dtype)], 1).reshape(2, 128, NF, 128).transpose(2, 1, 0, 3)
    w2 = cat(i["L1_ffn_shared_w2"], i["L1_ffn_routed_w2"]).reshape(18 * FF1, 256)
    w2 = cat(w2, np.zeros((pad, 256), w2.dtype)).reshape(NF, 128, 256)
    d["wf1"] = np.ascontiguousarray(np.concatenate([w1.reshape(NF, 128, 256), w2], 2))
    b1 = cat(i["L1_ffn_shared_b1"], i["L1_ffn_routed_b1"]).reshape(-1)
    d["b1c"] = np.ascontiguousarray(cat(b1, np.zeros(pad, b1.dtype)).reshape(NF, 128).T)
    d["b2r"] = np.ascontiguousarray(cat(i["L1_ffn_routed_b2"], i["L1_ffn_shared_b2"]))
    return d


def kernel(**inputs):
    import concourse.bacc as _bacc
    from concourse.bass_utils import run_bass_kernel_spmd as _run

    arrays = {k: np.ascontiguousarray(v) for k, v in layout({k: np.asarray(v) for k, v in inputs.items()}).items()}
    arrays.update(constants())
    nc = _bacc.Bacc("TRN2", target_bir_lowering=False, num_devices=1)
    aps = {n: nc.dram_tensor(n, v.shape, mybir.dt.from_np(v.dtype), kind="ExternalInput").ap()
           for n, v in arrays.items()}
    aps = {n: ap.bitcast(BF16) if arrays[n].dtype == np.uint16 else ap for n, ap in aps.items()}
    o = nc.dram_tensor("out_x", (1, T, D), F32, kind="ExternalOutput").ap()
    program(nc, aps, o)
    r = _run(nc, [arrays], core_ids=[0])
    return r.results[0]["out_x"]
```

```python
import math

import numpy as np

import concourse.bass as bass
from concourse import mybir

F32 = mybir.dt.float32
F32R = mybir.dt.float32r
BF16 = mybir.dt.bfloat16
ALU = mybir.AluOpType
ACT = mybir.ActivationFunctionType
AX = mybir.AxisListType.X

T, D, NT = 1024, 256, 8
H = 16
NE0, NE1, NS1, FF1 = 8, 16, 2, 176
NF = 25
NEG = -1e30
SC0 = 192.0 ** -0.5
G_LO = float(np.float32(0.5 - np.log(4.0 / 3.0)))
G_C = float(np.float32(1.0 / np.e))


class Queue:

    def __init__(self, sem):
        self.sem, self.n, self.ops = sem, 0, []

    def do(self, fn, *waits):
        self.n += 1
        self.ops.append((fn, waits, True))
        return (self.sem, self.n)

    def issue(self, fn, *waits):
        self.ops.append((fn, waits, False))

    def replay(self, eng):
        seen = {}

        def wait(w):
            if w is None:
                return
            if isinstance(w, list):
                for x in w:
                    wait(x)
                return
            sem, value = w
            if seen.get(id(sem), 0) < value:
                seen[id(sem)] = value
                eng.wait_ge(sem, value)

        for fn, waits, signals in self.ops:
            wait(list(waits))
            last = fn(eng)
            if signals:
                last.then_inc(self.sem, 1)


class Loads:

    def __init__(self, sem, queue):
        self.sem, self.q, self.n = sem, queue, 0

    def dma(self, dst, src, *waits):
        self.n += 16
        self.q.issue(lambda e: e.dma_start(dst, src).then_inc(self.sem, 16), *waits)
        return (self.sem, self.n)


def program(nc, a, out):
    def sem(name):
        return nc.alloc_semaphore(name)

    pe, dve, act, pool = (Queue(sem(f"q_{n}")) for n in ("pe", "dve", "act", "pool"))
    sp = Queue(sem("q_sp"))

    base = [16512]

    def sb(name, shape, dt, at=None):
        size = int(np.prod(shape[1:])) * (2 if dt == BF16 else 4)
        size = (size + 31) // 32 * 32
        if at is None:
            at = base[0]
            base[0] += size
        return nc.alloc_sbuf_tensor_at(name, list(shape), dt, offset=at)

    class Region:

        def __init__(self, at):
            self.at = at

        def sb(self, name, shape, dt):
            size = int(np.prod(shape[1:])) * (2 if dt == BF16 else 4)
            size = (size + 31) // 32 * 32
            t = nc.alloc_sbuf_tensor_at(name, list(shape), dt, offset=self.at)
            self.at += size
            assert self.at <= 229344, (name, self.at)
            return t

    bank = [nc.alloc_psum_tensor(f"bank{i}", [128, 512], F32) for i in range(8)]
    free = [None] * 8

    x = sb("x", [128, NT, D], F32)
    hT = sb("hT", [128, 2, T], F32)
    HTP = base[0]
    hTh = sb("hTh", [128, 2, T], F32R)
    hTl = sb("hTl", [128, 2, T], F32R)
    idf = sb("idf", [128, 128], F32)
    idr = sb("idr", [128, 128], F32R)
    ones1 = sb("ones1", [128, 64], F32)
    idb = sb("idb", [128, 128], BF16)
    maskq = sb("maskq", [128, 128], BF16)
    maskk = sb("maskk", [128, 128], BF16)
    dmask = sb("dmask", [11, 4, 128], F32)
    esum = sb("esum", [128, 17], F32)
    ones3 = sb("ones3", [128, 128], F32)
    tri = sb("tri", [128, 16, 16], F32)
    modc = sb("modc", [128, 2, 12], F32)
    gab = sb("gab", [128, 4, D], F32)
    HN = base[0]
    hn = sb("hn", [128, 2, D], F32)
    st6 = sb("st6", [128, NT, 6], F32)
    mv = sb("mv", [128, NT, 2], F32)
    sd = sb("sd", [128, NT], F32)
    rs = sb("rs", [128, NT], F32)
    mp = sb("mp", [128, 3, 2, 4, 2], F32)
    mcat = sb("mcat", [128, 2, 2, 11], F32)
    mbf = sb("mbf", [128, 2, 4], BF16)
    cc = sb("cc", [128, 2, 2], F32)
    sc_ = sb("sc_", [128, 2, 2], F32)
    rcp = sb("rcp", [128, 2, 4], F32)
    PHASE = base[0]

    loads = {}

    def group(name):
        loads[name] = Loads(sem(f"d_{name}"), sp)
        return loads[name]

    l_x, l_c, l_mod = [group("x0"), group("x1")], group("c"), group("mod")
    A = Region(PHASE)
    KV = A.at
    cosT = A.sb("cosT", [128, T], F32)
    sinT = A.sb("sinT", [128, T], F32)
    W0A = A.at
    w0a = A.sb("w0a", [128, 2, 258], F32)
    WSP = A.at
    wsp = A.sb("wsp", [128, 4, 2, 256], F32)
    wkpe = A.sb("wkpe", [128, 2, 8, 128], F32)
    wqpa = A.sb("wqpa", [128, 8, 128], F32)
    wqpb = A.sb("wqpb", [64, 8, 128], F32)
    waba = A.sb("waba", [128, 16, 64], F32)
    wabb = A.sb("wabb", [64, 16, 64], F32)
    mo = A.sb("mo", [128, 8, 256], F32)
    MP = Region(A.at)
    A.at += 6144
    lnw = A.sb("lnw", [128, 256], F32)
    qmTa = A.sb("qmTa", [128, T], F32)
    qmTb = A.sb("qmTb", [64, T], F32)
    kvT = A.sb("kvT", [128, T], F32)
    kvx = A.sb("kvx", [128, NT, 64], F32)
    gat = A.sb("gat", [128, NT, 2], F32)
    gsb = A.sb("gsb", [128, 2], F32)
    pctx = sb("pctx", [128, NT, D], F32, at=HTP)
    acc = sb("acc", [128, NT, D], F32, at=HTP + 4 * NT * D)
    S0 = A.at
    PB = Region(S0 + 64 * 1024)
    Pb = [PB.sb(f"Pb{i}", [128, 512], F32) for i in range(9)]
    PBE = PB.at
    vx = PB.sb("vx", [128, NT, 16 * 17], F32)
    S = Region(S0)
    qst = S.sb("qst", [107, 16, T], BF16)
    kst = S.sb("kst", [107, 16, T], BF16)
    PJ = Region(S0 + 64 * 1024)
    res = PJ.sb("res", [128, 2, 512], F32)
    stg = [PJ.sb(f"stg{i}", [128, 3, T], BF16) for i in range(2)]

    qbn = sb("qbn", [128, 16, 192], F32, at=S0 + 48 * 1024)
    kvbk = sb("kvbk", [128, 16, 64], F32, at=S0 + 60 * 1024)
    owT = sb("owT", [128, 16, 256], F32, at=S0 + 16 * 1024)
    kvbv = sb("kvbv", [128, 16, 64], F32, at=KV)
    C = Region(S0 + 32 * 1024)
    wm0 = C.sb("wm0", [128, 2, 1536], F32)
    scb0 = C.sb("scb0", [128, 2, 128], F32)
    gt0 = C.sb("gt0", [128, 2, 256], F32)

    l_c.dma(idf[:], a["idf"])
    l_c.dma(cc[:], a["cc"])
    t_c = (l_c.sem, l_c.n)
    t_x = []
    for i in range(2):
        t_x += [(l_x[i].dma(x[:, 4 * i:4 * i + 4, :],
                            a["x"].rearrange("a (i p) d -> p (a i) d", p=128)[:, 4 * i:4 * i + 4, :]))] * 4
    t_wm = l_mod.dma(wm0[:], a["wmod0"])
    l_w, l_wv = group("w"), group("wv")
    t_wqk = l_w.dma(wsp[:, 0:2, :, :], a["wsp0"][:, 0:2, :, :])
    t_wsp = l_wv.dma(wsp[:, 2:4, :, :], a["wsp0"][:, 2:4, :, :])
    l_w2 = group("w2")
    l_w2.dma(w0a[:], a["w0a"])
    l_w2.dma(lnw[:, 0:192], a["q_ln"].partition_broadcast(128))
    l_w2.dma(lnw[:, 192:256], a["kv_ln"].partition_broadcast(128))
    l_w2.dma(gsb[:], a["gate_b"].partition_broadcast(128))
    t_w2 = (l_w2.sem, l_w2.n)
    l_k, l_w3, l_w4, l_cs = group("k"), group("w3"), group("w4"), group("cs")

    def later_loads():
        for d, n in ((idb, "idb"), (maskq, "maskq"), (maskk, "maskk"), (dmask, "dmask"), (tri, "tri"), (esum, "esum"),
                     (ones3, "ones3")):
            l_k.dma(d[:], a[n])
        for d, n in ((qbn, "qbn"), (kvbk, "kvbk"), (owT, "owT"), (kvbv, "kvbv")):
            l_w3.dma(d[:], a[n])
        for d, n in ((wkpe, "wkpe"), (wqpa, "wqpa"), (wqpb, "wqpb")):
            l_w4.dma(d[:], a[n])
        return (l_k.sem, l_k.n), (l_w3.sem, l_w3.n), (l_w4.sem, l_w4.n)

    t_idr = act.do(lambda e: e.activation(idr[:], idf[:], ACT.Copy), t_c)

    t_mod, t_g = {}, {}

    def modulation(layer, wm, scb, tmp, t_w, banks, waits=None):
        c, s = cc[:, layer, :], sc_[:, layer, :]
        t = act.do(lambda e: e.activation(s, c, ACT.Silu), t_c)

        def spread(e):
            for k in range(2):
                last = e.tensor_scalar(scb[:, k, :], idf[:], 0.0, sc_[:, layer, k:k + 1], ALU.mult, ALU.add)
            return last
        t_s = dve.do(spread, t, waits)
        b0, b1, b2 = banks

        def columns():
            def mm(e):
                for j in (0, 1, 2, 3, 6, 7, 8, 9):
                    for k in range(2):
                        last = e.matmul(bank[b0][:, j:j + 1], wm[:, k, j * 128:(j + 1) * 128], scb[:, k, 0:1],
                                        start=(k == 0), stop=(k == 1))
                return last
            tc = pe.do(mm, t_s, t_w, free[b0])

            def put(e):
                e.tensor_copy(modc[:, layer, 0:2], bank[b0][:, 0:2])
                e.tensor_copy(modc[:, layer, 6:8], bank[b0][:, 6:8])
                e.tensor_scalar(modc[:, layer, 2:4], bank[b0][:, 2:4], 1.0, None, ALU.add)
                return e.tensor_scalar(modc[:, layer, 8:10], bank[b0][:, 8:10], 1.0, None, ALU.add)
            free[b0] = t_mod[layer] = dve.do(put, tc)

        def gates():
            def rows(e):
                for g, b in ((0, b1), (1, b2)):
                    for k in range(2):
                        lo = 512 + 768 * g
                        last = e.matmul(bank[b][:, 0:256], scb[:, k, :], wm[:, k, lo:lo + 256],
                                        start=(k == 0), stop=(k == 1))
                return last
            tr = pe.do(rows, t_s, t_w, free[b1], free[b2])
            for g, bn in ((0, b1), (1, b2)):
                b, o, m = bank[bn][:, 0:256], gab[:, 2 * layer + g, :], tmp[:, g, :]
                ta = dve.do(lambda e, b=b, m=m: e.tensor_scalar(m, b, -1.0, 0.25, ALU.mult, ALU.max), tr)
                ta = dve.do(lambda e, b=b, m=m: e.scalar_tensor_tensor(out=m, in0=b, scalar=1.0, in1=m,
                                                                      op0=ALU.mult, op1=ALU.max), ta)
                tb = dve.do(lambda e, b=b, o=o: e.tensor_scalar(o, b, 0.0, 2.0, ALU.is_ge, ALU.mult), tr)
                free[bn] = tb
                t_g[layer] = dve.do(lambda e, o=o, m=m: e.scalar_tensor_tensor(out=o, in0=o, scalar=-1.0, in1=m,
                                                                              op0=ALU.add, op1=ALU.mult), ta, tb)
            return tr
        return columns, gates

    def norm(layer, second, t_in, parts, hook=None):
        s0, c0 = (6, 8) if second else (0, 2)
        t_h, t_p, t_rs = [], [], {}
        t_tr = [None] * NT

        def stats(half):
            ts = []
            hs = slice(4 * half, 4 * half + 4)
            for i in range(4 * half, 4 * half + 4):
                ts.append(dve.do(lambda e, i=i: e.bn_stats(st6[:, i, :], x[:, i, :]), t_in[i]))
            for j in range(4):
                t = dve.do(lambda e, i=4 * half + j: e.bn_aggr(mv[:, i, :], st6[:, i, :]), ts[j])
            t = dve.do(lambda e: e.tensor_scalar(sd[:, hs], mv[:, hs, 1], 1e-5, None, ALU.add), t)
            t = act.do(lambda e: e.activation(sd[:, hs], sd[:, hs], ACT.Sqrt), t)
            t_rs[half] = dve.do(lambda e: e.reciprocal(rs[:, hs], sd[:, hs]), t)

        def turn(half):
            b0, b1 = 2 * half, 2 * half + 1
            for j in range(4):
                i = 4 * half + j
                t_n = dve.do(lambda e, i=i: e.tensor_scalar(hn[:, i % 2, :], x[:, i, :], mv[:, i, 0:1], rs[:, i:i + 1],
                                                            ALU.subtract, ALU.mult), t_rs[half],
                             t_tr[i - 2] if i > 1 else None)

                def tr(e, i=i, j=j):
                    e.transpose(bank[b0][:, j * 128:(j + 1) * 128], hn[:, i % 2, 0:128], idf[:])
                    return e.transpose(bank[b1][:, j * 128:(j + 1) * 128], hn[:, i % 2, 128:256], idf[:])
                t_tr[i] = pe.do(tr, t_n, t_c, free[b0], free[b1])

        def put(half):
            b0 = 2 * half
            tt = []
            cs = slice(half * 512, half * 512 + 512)
            for k in range(2):
                te = act.do(lambda e, k=k, b=b0 + k: e.activation(
                    hT[:, k, cs], bank[b][:], ACT.Identity, bias=modc[:, layer, s0 + k:s0 + k + 1],
                    scale=modc[:, layer, c0 + k:c0 + k + 1]), t_tr[4 * half + 3], t_mod[layer])
                free[b0 + k] = te
                tt.append(te)
                if parts:
                    th = act.do(lambda e, k=k: e.activation(hTh[:, k, cs], hT[:, k, cs], ACT.Copy), te)
                    tl = dve.do(lambda e, k=k: e.tensor_tensor(
                        hTl[:, k, cs], hT[:, k, cs], hTh[:, k, cs].bitcast(F32), ALU.subtract), th)
                    t_p.extend([th, tl])
            t_h.append(tt)
        stats(0)
        if hook:
            stats(1)
        turn(0)
        if not hook:
            stats(1)
            put(0)
        turn(1)
        if hook:
            hook()
            put(0)
        put(1)
        return t_h, t_p

    columns, gates = modulation(0, wm0, scb0, gt0, t_wm, (4, 5, 6))
    t_h, _ = norm(0, False, t_x, False, columns)

    BLK = (0, 2, 1, 3)
    GROUPS = ((0, 4), (4, 8), (8, 16))

    def project16(layer, w, t_wqk, t_wv, t_stack_free, t_pj_free, bq=None, bk=None, bvb=None, scratch=None,
                  between=None):
        g_out = [group(f"so{layer}{i}") for i in range(2)]
        g_in = [group(f"si{layer}{i}") for i in range(3)]
        t_stack, t_out = {}, {}
        t_res = [None, None]
        QP, KP = (0, 0, 1, 0, 2, 1), (0, 1, 0, 2, 0, 1)

        def load_heads(g, waits):
            h0, h1 = GROUPS[g]
            hs = slice(h0, h1)
            m = [t_out[h0 // 8], t_out[2 + h0 // 8]]
            for n, (st, parts) in enumerate(((qst, QP), (kst, KP))):
                for s, part in enumerate(parts):
                    src = scratch[n * 256 + 16 * h0:n * 256 + 16 * h1, part, :].rearrange("(h d) t -> d h t", d=16)
                    g_in[g].dma(st[16 * s:16 * s + 16, hs, :], src, m, waits)
                g_in[g].dma(st[96:107, hs, :], a["qrow" if n == 0 else f"krow{layer}"][:, hs, :], waits)
            t_stack[g] = (g_in[g].sem, g_in[g].n)

        for blk, (n, m) in enumerate(((0, 0), (1, 0), (0, 1), (1, 1))):
            bias = (bq, bk)[n]
            z = blk % 2
            for half in range(2):
                b = 4 + (2 * blk + half) % 4
                cs = slice(half * 512, half * 512 + 512)

                def mm(e, n=n, m=m, b=b, cs=cs):
                    for k in range(2):
                        last = e.matmul(bank[b][:], w[:, n, k, m * 128:(m + 1) * 128], hT[:, k, cs],
                                        start=(k == 0), stop=(k == 1))
                    return last
                bc_ = 0.0 if bias is None else bias[:, m:m + 1]
                t_o = t_out.get(BLK[blk - 2]) if blk > 1 else None

                def run(mm=mm, bc_=bc_, b=b, cs=cs, half=half, z=z, t_o=t_o, bias=bias):
                    t = pe.do(mm, t_wqk, t_h_cur[half], free[b])
                    t1 = act.do(lambda e: e.activation(stg[z][:, 0, cs], bank[b][:],
                                                       ACT.Copy if bias is None else ACT.Identity, bias=bc_), t, t_o,
                                t_pj_free)
                    t2 = dve.do(lambda e: e.scalar_tensor_tensor(out=res[:, half, :], in0=bank[b][:], scalar=bc_,
                                                                 in1=stg[z][:, 0, cs], op0=ALU.add, op1=ALU.subtract),
                                t1, t_res[half], t_pj_free)
                    free[b] = t2
                    t3 = act.do(lambda e: e.activation(stg[z][:, 1, cs], res[:, half, :], ACT.Copy), t2)
                    t_res[half] = dve.do(lambda e: e.tensor_tensor(stg[z][:, 2, cs], res[:, half, :],
                                                                   stg[z][:, 1, cs], ALU.subtract), t3)
                    return t_res[half]
                t4 = run()
            row = (n * 2 + m) * 128
            t_out[n * 2 + m] = g_out[z].dma(scratch[row:row + 128, :, :], stg[z][:], t4)
            if blk == 1:
                load_heads(0, t_stack_free)
                load_heads(1, t_stack_free)
                if between:
                    between()
        t_v = []
        tm = pool.do(lambda e: e.memset(vx[:].rearrange("p i (h c) -> p (i h) c", c=17)[:, :, 16:17], 1.0), t_pj_free)
        for i in range(NT):
            b = 6 + i % 2

            def mm(e, i=i, b=b):
                for k in range(2):
                    last = e.matmul(bank[b][:, 0:256], hT[:, k, i * 128:(i + 1) * 128], w[:, 2, k, :],
                                    start=(k == 0), stop=(k == 1))
                return last
            t = pe.do(mm, t_wv, t_h_cur[i // 4], free[b])
            dst = vx[:, i, :].rearrange("p (h c) -> p h c", c=17)[:, :, 0:16]
            src = bank[b][:, 0:256].rearrange("p (h c) -> p h c", c=16)
            if bvb is None:
                t = act.do(lambda e, dst=dst, src=src: e.activation(dst, src, ACT.Copy), t, t_pj_free)
            else:
                t = dve.do(lambda e, dst=dst, src=src: e.tensor_tensor(
                    dst, src, bvb[:].rearrange("p (h c) -> p h c", c=16), ALU.add), t, t_pj_free)
            free[b] = t
            t_v.append(t)
        t_v.append(tm)
        return t_stack, t_v, list(t_out.values()), load_heads

    def attention(units, causal, score, row, value, evac, stbanks, extra, scale, G, t_p0, OT, npb, summed=None,
                  mxbanks=(0, 1), ahead=2):
        n = len(units)
        nh = len(units[0][0])
        w = 128 // (G * nh)
        t_mp, t_tr, t_row = {}, {}, {}
        t_neg = {}
        t_sfree = [t_p0 if summed is None else [t_p0, None]] * len(Pb)
        scount = [0]
        mcount = [0]

        def max_steps(u):
            hs, half = units[u]
            steps = []
            for a in range(nh):
                for j in range(4):
                    qi = 4 * half + j
                    for kh in range(2):
                        keys = (qi + 1) * 128 if causal else T
                        c = min(512, keys - 512 * kh)
                        if c > 0:
                            steps.append((a, j, qi, kh, c))
            return steps

        def do_max(u, step):
            a, j, qi, kh, c = step
            hs, half = units[u]
            mb = mxbanks(u) if callable(mxbanks) else mxbanks
            b = mb[mcount[0] % len(mb)]
            mcount[0] += 1
            diag = causal and (qi // 4) == kh

            def mm(e):
                last = score(e, "max", hs[a], qi, kh, c, bank[b][:, 0:c])
                if diag:
                    last = e.matmul(bank[b][:, c - 128:c], idb[:], maskq[:], start=False, stop=True,
                                    skip_group_check=True)
                return last
            t = pe.do(mm, free[b], extra(u, "max"))
            t = dve.do(lambda e: e.tensor_reduce(mp[:, u % 3, a, j, kh:kh + 1], bank[b][:, 0:c], AX, ALU.max), t)
            free[b] = t
            t_mp[u] = t

        def do_neg(u):
            hs, half = units[u]
            two = not (causal and half == 0)
            dst, low = mcat[:, u % 2, 0:nh, 3:7], mcat[:, u % 2, 0:nh, 7:11]
            if two:
                t = dve.do(lambda e: e.tensor_reduce(dst, mp[:, u % 3, 0:nh, :, :], AX, ALU.max, negate=True),
                           t_mp[u], t_tr.get(u - 2, t_p0))
            else:
                t = dve.do(lambda e: e.tensor_scalar(dst, mp[:, u % 3, 0:nh, :, 0], -1.0, None, ALU.mult),
                           t_mp[u], t_tr.get(u - 2, t_p0))
            t = dve.do(lambda e: e.tensor_copy(mbf[:, 0:nh, :], dst), t)
            t = dve.do(lambda e: e.tensor_tensor(low, dst, mbf[:, 0:nh, :], ALU.subtract), t)
            t_neg[u] = t

        def do_tr(u):
            def tr(e):
                for a in range(nh):
                    last = e.transpose(bank[6][0:11, 128 * a:128 * a + 128], mcat[:, u % 2, a, :], idf[:])
                return last
            t_tr[u] = pe.do(tr, t_neg[u], free[6], t_k)

        def do_row(u):
            hs, half = units[u]
            for a in range(nh):
                o = (qst[96:107, hs[a], half * 512:half * 512 + 512] if row is None else row[u % 2 * 2 + a][0:11, :])
                t = dve.do(lambda e, a=a, o=o: e.tensor_tensor(
                    o.rearrange("p (j c) -> p j c", j=4),
                    bank[6][0:11, 128 * a:128 * a + 128].unsqueeze(1).to_broadcast([11, 4, 128]),
                    dmask[:], ALU.mult), t_tr[u], t_stdone.get(u - 2, t_p0))
            free[6] = t
            t_row[u] = t

        t_stdone = {}
        t_exp = {}

        def do_st(u, a, kt):
            hs, half = units[u]
            q0 = max(128 * kt, 512 * half) if causal else 512 * half
            c = 512 * (half + 1) - q0
            sb_ = stbanks(u) if callable(stbanks) else stbanks
            b = sb_[scount[0] % len(sb_)]
            p = scount[0] % npb
            scount[0] += 1
            diag = causal and kt >= 4 * half

            def mm(e):
                last = score(e, "st", hs[a], kt, q0, c, bank[b][:, 0:c], u % 2 * 2 + a)
                if diag:
                    last = e.matmul(bank[b][:, 0:128], idb[:], maskk[:], start=False, stop=True,
                                    skip_group_check=True)
                return last
            t = pe.do(mm, free[b], t_row[u])
            t_stdone[u] = t
            te = act.do(lambda e: e.activation(Pb[p][:, 0:c], bank[b][:, 0:c], ACT.Exp, scale=scale), t, t_sfree[p])
            free[b] = te
            t_exp[u, a, kt] = (te, p, q0)
            if summed is not None:
                t_sfree[p] = [None, summed(u, a, kt, Pb[p], te)]
                if kt == 1:
                    p0 = t_exp[u, a, 0][1]
                    t_sfree[p0] = [t_sfree[p0][0], t_sfree[p][1]]

        def do_pv(u, aks):
            hs, half = units[u]
            b = 4 + half
            nk = 4 * half + 4 if causal else NT

            def mm(e):
                for a, kt in aks:
                    _, p, q0 = t_exp[u, a, kt]
                    v = value(hs[a], kt)
                    g = w * (a * G + kt % G)
                    last = e.matmul(bank[b][g:g + v.shape[1], q0 - 512 * half:512], v, Pb[p][:, 0:512 * (half + 1) - q0],
                                    start=(kt < G), stop=(kt + G >= nk), skip_group_check=True)
                return last
            t = pe.do(mm, [t_exp[u, a, kt][0] for a, kt in aks], free[b] if aks[0] == (0, 0) else None, extra(u, "pv"))
            for a, kt in aks:
                p = t_exp[u, a, kt][1]
                t_sfree[p] = [t, t_sfree[p][1]] if summed is not None else t
            if aks[-1] == (nh - 1, nk - 1):
                to = act.do(lambda e: e.activation(OT[half][:], bank[b][:], ACT.Copy), t, t_ot[half])
                free[b] = to
                later(3, lambda: evac(u, hs, half, to, t_ot, later))

        due = []

        def later(n, f):
            due.append((scount[0] + n, f))

        t_ot = [t_p0, t_p0]

        def run_due():
            for d in [d for d in due if d[0] <= scount[0]]:
                due.remove(d)
                d[1]()

        first = [lambda s=s: do_max(0, s) for s in max_steps(0)]

        def run():
            while first:
                first.pop(0)()
            do_neg(0)
            do_tr(0)
            do_row(0)
            if n > 1 and ahead == 2:
                for s in max_steps(1):
                    do_max(1, s)
            for u in range(n):
                hs, half = units[u]
                nk = (4 * half + 4 if causal else NT) * nh
                steps = max_steps(u + ahead) if u + ahead < n else []
                total, given = len(steps), 0
                last_max = nk if ahead == 2 else nk - 5
                at = 0 if ahead == 2 else nk - 4
                extra(u, "begin")
                aks = []
                for k in range(nk):
                    a, kt = k % nh, k // nh
                    if k == at and u + 1 < n:
                        do_neg(u + 1)
                    do_st(u, a, kt)
                    if k == at + 1 and u + 1 < n:
                        do_tr(u + 1)
                        do_row(u + 1)
                    while given < total and given * last_max < total * (k + 1):
                        do_max(u + ahead, steps[given])
                        given += 1
                    extra(u, ("step", k))
                    aks.append((a, kt))
                    if len(aks) == G * nh:
                        due.append((scount[0] + 2, lambda u=u, aks=aks: do_pv(u, aks)))
                        aks = []
                    run_due()
            while due:
                scount[0] += 1
                run_due()
        return first, run

    t_h_cur = t_h
    scratch = nc.dram_tensor("scratch", (512, 3, T), BF16, kind="Internal").ap()
    scratch1 = nc.dram_tensor("scratch1", (512, 3, T), BF16, kind="Internal").ap()
    t_more = []
    t_modpe = gates()
    t_stacks, t_v, t_pjo, load_heads = project16(0, wsp, t_wqk, t_wsp, [t_modpe, t_g[0]], None, scratch=scratch,
                                                 between=lambda: t_more.extend(later_loads()))
    t_k, t_w3, t_w4 = t_more

    fold_steps = []
    t_wab, t_mo, t_fold = [], [], []

    def fold_parts():
        def qk(rows, dst, g, c0):
            t = {}

            def product(q):
                def mm(e):
                    for i in range(4 * q, 4 * q + 4):
                        last = e.matmul(bank[7][0:rows, 64 * i:64 * i + 64], qbn[:, 8 * g + i, c0:c0 + rows],
                                        kvbk[:, 8 * g + i, :], start=True, stop=True)
                    return last
                t[0] = pe.do(mm, t_w3, free[7])

            def put():
                free[7] = act.do(lambda e: e.activation(dst[:, 8 * g:8 * g + 8, :].rearrange("p h c -> p (h c)"),
                                                        bank[7][0:rows, :], ACT.Copy), t[0])
                t_wab.append(free[7])
            return [lambda: product(0), lambda: product(1), put]

        def v(g):
            t = {}

            def product(q):
                def mm(e):
                    for s in range(2):
                        h = 4 * g + 2 * q + s
                        last = e.matmul(bank[7][64 * s:64 * s + 64, 256 * q:256 * q + 256], kvbv[:, h, :], owT[:, h, :],
                                        start=True, stop=True)
                    return last
                t[0] = pe.do(mm, t_w3, free[7])

            def put():
                free[7] = act.do(lambda e: e.activation(mo[:, 2 * g:2 * g + 2, :].rearrange("p a c -> p (a c)"),
                                                        bank[7][:], ACT.Copy), t[0])
                t_mo.append(free[7])
            return [lambda: product(0), lambda: product(1), put]
        for g in range(4):
            fold_steps.extend(v(g))
        for g in range(2):
            fold_steps.extend(qk(128, waba, g, 0))
            fold_steps.extend(qk(64, wabb, g, 128))
    fold_parts()

    L = Region(MP.at)
    sq = L.sb("sq", [128, 192], F32)
    ss = L.sb("ss", [128, NT, 2], F32)
    rr = L.sb("rr", [128, NT, 2], F32)
    rq = L.sb("rq", [128, NT, 2], F32)
    gw_ = L.sb("gw_", [128, NT, 2], F32)
    gm_ = L.sb("gm_", [128, NT], F32)
    qkv = L.sb("qkv", [128, 2, 256 + 64], F32)
    raw = sb("raw", [128, NT, 256], F32, at=HTP + 4 * NT * D)
    t_pj0 = [(act.sem, act.n), (dve.sem, dve.n)]
    t3 = None
    for i in range(NT):
        b = i % 4

        def mm(e, i=i, b=b):
            for k in range(2):
                last = e.matmul(bank[b][:, 0:258], hT[:, k, i * 128:(i + 1) * 128], w0a[:, k, :],
                                start=(k == 0), stop=(k == 1))
            return last
        t = pe.do(mm, t_w2, t_h[i // 4], free[b])
        t = act.do(lambda e, i=i, b=b: e.activation(raw[:, i, :], bank[b][:, 0:256], ACT.Copy), t)
        t_gw = act.do(lambda e, i=i, b=b: e.activation(gw_[:, i, :], bank[b][:, 256:258], ACT.Copy))
        free[b] = t_gw
        t2 = dve.do(lambda e, i=i: e.tensor_tensor_reduce(sq[:], raw[:, i, 0:192], raw[:, i, 0:192], 1.0 / 192, 0.0,
                                                          ALU.mult, ALU.add, ss[:, i, 0:1]), t, t3)
        t3 = dve.do(lambda e, i=i: e.tensor_tensor_reduce(sq[:, 0:64], raw[:, i, 192:256], raw[:, i, 192:256],
                                                          1.0 / 64, 0.0, ALU.mult, ALU.add, ss[:, i, 1:2]), t2)
    t = dve.do(lambda e: e.tensor_scalar(rr[:], ss[:], 1e-6, None, ALU.add), t2, t3)
    t = act.do(lambda e: e.activation(rr[:], rr[:], ACT.Sqrt), t)
    t_rq = dve.do(lambda e: e.reciprocal(rq[:], rr[:]), t)
    t = dve.do(lambda e: e.tensor_tensor(gw_[:], gw_[:], gsb[:].unsqueeze(1).to_broadcast([128, NT, 2]), ALU.add),
               t_gw)
    t = dve.do(lambda e: e.tensor_reduce(gm_[:], gw_[:], AX, ALU.max), t)
    t = dve.do(lambda e: e.tensor_tensor(gw_[:], gw_[:], gm_[:].unsqueeze(2).to_broadcast([128, NT, 2]),
                                         ALU.subtract), t)
    t = act.do(lambda e: e.activation(gw_[:], gw_[:], ACT.Exp), t)
    t = dve.do(lambda e: e.tensor_reduce(gm_[:], gw_[:], AX, ALU.add), t)
    t = dve.do(lambda e: e.reciprocal(gm_[:], gm_[:]), t)
    t_gat = dve.do(lambda e: e.tensor_tensor(gat[:], gw_[:], gm_[:].unsqueeze(2).to_broadcast([128, NT, 2]),
                                             ALU.mult), t)
    t_ones = pool.do(lambda e: e.memset(ones1[:], 1.0))
    t_qt = [None] * NT
    for half in range(2):
        b0, b1, b2 = 0, 1, 2
        for j in range(4):
            i = 4 * half + j
            z = i % 2

            def sc(e, i=i, z=z):
                e.scalar_tensor_tensor(out=qkv[:, z, 0:192], in0=raw[:, i, 0:192], scalar=rq[:, i, 0:1],
                                       in1=lnw[:, 0:192], op0=ALU.mult, op1=ALU.mult)
                return e.scalar_tensor_tensor(out=qkv[:, z, 192:256], in0=raw[:, i, 192:256], scalar=rq[:, i, 1:2],
                                              in1=lnw[:, 192:256], op0=ALU.mult, op1=ALU.mult)
            t = dve.do(sc, t_rq, t_w2, t_qt[i - 2] if i > 1 else None)
            t = dve.do(lambda e, z=z: e.tensor_copy(qkv[:, z, 256:320], qkv[:, z, 192:256]), t)
            t_kvx = dve.do(lambda e, i=i, z=z: e.tensor_copy(kvx[:, i, 0:64], qkv[:, z, 192:256]), t)

            def tr(e, j=j, z=z):
                js = slice(j * 128, (j + 1) * 128)
                e.transpose(bank[b0][:, js], qkv[:, z, 0:128], idf[:])
                e.transpose(bank[b1][0:64, js], qkv[:, z, 128:192], idf[:])
                return e.transpose(bank[b2][:, js], qkv[:, z, 192:320], idf[:])
            t_qt[i] = pe.do(tr, t_kvx, t, free[b0], free[b1], free[b2])
        cs = slice(half * 512, half * 512 + 512)
        free[b0] = act.do(lambda e, cs=cs: e.activation(qmTa[:, cs], bank[b0][:], ACT.Copy), t_qt[4 * half + 3])
        free[b1] = act.do(lambda e, cs=cs: e.activation(qmTb[:, cs], bank[b1][0:64, :], ACT.Copy), t_qt[4 * half + 3])
        free[b2] = act.do(lambda e, cs=cs: e.activation(kvT[:, cs], bank[b2][:], ACT.Copy), t_qt[4 * half + 3])
    t_lat = [(act.sem, act.n), t_kvx, t_ones]

    t_mc = pool.do(lambda e: e.memset(mcat[:], 1.0))
    units = [((h,), half) for h in range(H) for half in range(2)]

    def score16(e, kind, h, i, j, c, o, u=None):
        if kind == "max":
            return e.matmul(o, qst[0:99, h, i * 128:(i + 1) * 128], kst[0:99, h, j * 512:j * 512 + c],
                            start=True, stop=True)
        return e.matmul(o, kst[0:107, h, i * 128:(i + 1) * 128], qst[0:107, h, j:j + c], start=True, stop=True)

    def value16(h, kt):
        return vx[:, kt, h * 17:h * 17 + 17]

    t_rc = {}

    def evac16(gated, dst, causal, OT):
        def f(u, hs, half, to, t_ot, later):
            h = hs[0]

            def mm(e):
                for j in range(4):
                    rows = 32 * (j + 1) if causal and half == 0 else 128
                    last = e.matmul(bank[6][:, 128 + 17 * j:145 + 17 * j], OT[half][0:rows, 128 * j:128 * j + 128],
                                    esum[0:rows, :], start=True, stop=True)
                return last
            t = pe.do(mm, to, free[6])
            t_ot[half] = t
            r = rcp[:, u % 2, :]
            v = bank[6][:, 128:196].rearrange("p (j c) -> p j c", c=17)
            tr = dve.do(lambda e: e.reciprocal(r, v[:, :, 16]), t)
            if gated:
                tr = dve.do(lambda e: e.tensor_tensor(r, r, gat[:, 4 * half:4 * half + 4, 1], ALU.mult), tr, t_gat)
            free[6] = dve.do(lambda e: e.tensor_tensor(dst[:, 4 * half:4 * half + 4, h * 16:h * 16 + 16],
                                                       v[:, :, 0:16], r.unsqueeze(2).to_broadcast([128, 4, 16]),
                                                       ALU.mult), tr)
        return f

    def clear(t):
        for b in (4, 5):
            free[b] = dve.do(lambda e, b=b: e.memset(bank[b][:], 0.0), free[b], t)

    t_pj1 = [(act.sem, act.n), (dve.sem, dve.n), (pe.sem, pe.n), t_pjo]

    def extra16(t_stack, tv):
        def f(u, what):
            if what == "max":
                return [t_stack[min(u // 8, 2)], t_mc]
            if what == "pv":
                return tv
            return None
        return f

    OTa = [sb(f"OTa{i}", [128, 512], F32, at=HTP + 4 * NT * D + 2048 * i) for i in range(2)]
    S2 = Region(S0)
    QKh, QKl = [[None] * 4, [None] * 4], [[None] * 4, [None] * 4]
    for QK, part in ((QKh, "h"), (QKl, "l")):
        for i2 in range(2):
            for n in range(2):
                for i in (2 * i2, 2 * i2 + 1):
                    QK[n][i] = S2.sb(f"qk{n}{part}{i}", [128, T], F32R)
    M0 = Region(WSP)
    t12 = M0.sb("t12", [128, 2, 512], F32)
    Rt = M0.sb("Rt", [128, 512], F32)
    M2 = Region(PBE - 2048)
    mrow = [M2.sb(f"mrow{i}", [11, 512], BF16) for i in range(4)]
    onesr = M2.sb("onesr", [11, 128], BF16)
    OTm = [M2.sb(f"OTm{i}", [128, 512], F32) for i in range(2)]
    Ps = [MP.sb(f"Ps{i}", [128, 512], F32) for i in range(3)] + [sb("Ps3", [128, 512], F32, at=HN)]
    t_old = []

    def latent_keys(pair, waits):
        def kvh(e):
            for i in (2 * pair, 2 * pair + 1):
                r = slice(0, 64) if i % 2 == 0 else slice(64, 128)
                last = e.activation(QKh[1][i][r, :], kvT[r, :], ACT.Copy)
            return last

        def kvl(e):
            for i in (2 * pair, 2 * pair + 1):
                r = slice(0, 64) if i % 2 == 0 else slice(64, 128)
                last = e.tensor_tensor(QKl[1][i][r, :], kvT[r, :], QKh[1][i][r, :].bitcast(F32), ALU.subtract)
            return last
        th = act.do(kvh, waits, t_lat)
        t_kv[pair] = [th, dve.do(kvl, th, waits)]

    t_kv = [None, None]
    t_qk = {}
    t_t12, t_R = [None], [None]

    def prep_steps(p, waits):
        z = 2 * (p % 2)
        done = t_qk.setdefault(p, [])

        def rope(n, half):
            cs = slice(half * 512, half * 512 + 512)
            t = {}

            def product():
                def mm(e):
                    if n == 1:
                        for k in range(2):
                            last = e.matmul(bank[7][:], wkpe[:, k, p, :], hT[:, k, cs], start=(k == 0), stop=(k == 1))
                        return last
                    e.matmul(bank[7][:], wqpa[:, p, :], qmTa[:, cs], start=True, stop=False)
                    return e.matmul(bank[7][:], wqpb[:, p, :], qmTb[:, cs], start=False, stop=True)
                t[0] = pe.do(mm, free[7], t_lat, t_w4, (l_cs.sem, l_cs.n))

            def swap():
                def f(e):
                    for q in range(4):
                        last = e.activation(t12[32 * (q ^ 1):32 * (q ^ 1) + 32, 1, :], bank[7][32 * q:32 * q + 32, :],
                                            ACT.Copy)
                    return last
                t[1] = act.do(f, t[0], t_t12[0], *waits)

            def turn():
                ts = pool.do(lambda e: e.tensor_tensor(t12[:, 1, :], t12[:, 1, :], sinT[:, cs], ALU.mult), t[1])
                tc = dve.do(lambda e: e.tensor_tensor(t12[:, 0, :], bank[7][:], cosT[:, cs], ALU.mult), t[1],
                            t_t12[0], *waits)
                free[7] = tc
                t[2] = pool.do(lambda e: e.tensor_tensor(Rt[:], t12[:, 0, :], t12[:, 1, :], ALU.add), tc, ts, t_R[0])
                t_t12[0] = t[2]

            def high():
                def hi(e):
                    e.activation(QKh[n][z][64:128, cs], Rt[64:128, :], ACT.Copy)
                    return e.activation(QKh[n][z + 1][0:64, cs], Rt[0:64, :], ACT.Copy)
                t[3] = act.do(hi, t[2], *waits)

            def low():
                def lo(e):
                    e.tensor_tensor(QKl[n][z][64:128, cs], Rt[64:128, :], QKh[n][z][64:128, cs].bitcast(F32),
                                    ALU.subtract)
                    return e.tensor_tensor(QKl[n][z + 1][0:64, cs], Rt[0:64, :], QKh[n][z + 1][0:64, cs].bitcast(F32),
                                           ALU.subtract)
                tl = dve.do(lo, t[3], *waits)
                t_R[0] = tl
                done.extend([t[3], tl])
            return [product, swap, turn, high, low]

        def lat(half):
            cs = slice(half * 512, half * 512 + 512)
            t = {}

            def product():
                def mm(e):
                    wa = waba[:, 2 * p:2 * p + 2, :].rearrange("p h c -> p (h c)")
                    wb = wabb[:, 2 * p:2 * p + 2, :].rearrange("p h c -> p (h c)")
                    e.matmul(bank[7][:], wa, qmTa[:, cs], start=True, stop=False)
                    return e.matmul(bank[7][:], wb, qmTb[:, cs], start=False, stop=True)
                t[0] = pe.do(mm, free[7], t_lat, t_wab)

            def high():
                def hi(e):
                    e.activation(QKh[0][z][0:64, cs], bank[7][0:64, :], ACT.Copy)
                    return e.activation(QKh[0][z + 1][64:128, cs], bank[7][64:128, :], ACT.Copy)
                t[1] = act.do(hi, t[0], *waits)

            def low():
                def lo(e):
                    e.tensor_tensor(QKl[0][z][0:64, cs], bank[7][0:64, :], QKh[0][z][0:64, cs].bitcast(F32),
                                    ALU.subtract)
                    return e.tensor_tensor(QKl[0][z + 1][64:128, cs], bank[7][64:128, :],
                                           QKh[0][z + 1][64:128, cs].bitcast(F32), ALU.subtract)
                tl = dve.do(lo, t[1])
                free[7] = tl
                done.extend([t[1], tl])
            return [product, high, low]
        r = [rope(1, 0), rope(1, 1), rope(0, 0), rope(0, 1)]
        q = [lat(0), lat(1)]
        steps = [(r[0][0],), (r[0][1],), (r[0][2],),
                 (r[1][0],), (r[1][1], r[0][3]), (r[0][4], r[1][2]),
                 (q[0][0],), (q[0][1], r[1][3]), (q[0][2], r[1][4]),
                 (r[2][0],), (r[2][1],), (r[2][2],),
                 (r[3][0],), (r[3][1], r[2][3]), (r[2][4], r[3][2]),
                 (q[1][0],), (q[1][1], r[3][3]), (q[1][2], r[3][4])]
        return steps

    def bufs(h):
        i = 2 * ((h // 2) % 2) + h % 2
        return QKh[0][i], QKl[0][i], QKh[1][i], QKl[1][i]

    def score_main(e, kind, h, i, j, c, o, u=None):
        qh, ql, kh, kl = bufs(h)
        if kind == "max":
            return e.matmul(o, qh[:, i * 128:(i + 1) * 128], kh[:, j * 512:j * 512 + c], start=True, stop=True)
        ks, qs = slice(i * 128, (i + 1) * 128), slice(j, j + c)
        e.matmul(o, kh[:, ks], qh[:, qs], start=True, stop=False)
        e.matmul(o, kh[:, ks], ql[:, qs], start=False, stop=False)
        e.matmul(o, kl[:, ks], qh[:, qs], start=False, stop=False)
        return e.matmul(o, onesr[:], mrow[u][:], start=False, stop=True)

    t_acc = [None] * NT
    t_ps = [t_old] * 4
    held = {}

    def summed(u, a, kt, P, te):
        z = u % 2 * 2 + a
        o = Ps[z][:]
        if kt == 0:
            held[z] = P
            return None
        first = held[z][:] if kt == 1 else o
        t = pool.do(lambda e: e.tensor_tensor(o, first, P[:], ALU.add), te, t_ps[z])
        t_ps[z] = t
        return t

    def evac_main(u, hs, half, to, t_ot, later):
        p, b, z = hs[0] // 2, 4 + half, u % 2 * 2

        def den(e):
            for a in range(2):
                last = e.matmul(bank[b][64 * a:64 * a + 64, :], ones1[:], Ps[z + a][:], start=True, stop=True)
            return last
        t = pe.do(den, t_ps[z], t_ps[z + 1], free[b], t_ones)
        t_ps[z] = t_ps[z + 1] = t

        def quarter(j):
            js = slice(128 * j, 128 * j + 128)
            tr = dve.do(lambda e: e.reciprocal(Ps[z][:, js], bank[b][:, js]), t)
            t_ps[z] = tr
            if j == 3:
                free[b] = tr
            tn[j] = dve.do(lambda e: e.tensor_tensor(OTm[half][:, js], OTm[half][:, js], Ps[z][:, js], ALU.mult), tr, to)
            t_ps[z] = tn[j]

        def project(q):
            def mm(e):
                for s in range(2):
                    j = 2 * q + s
                    last = e.matmul(bank[6][:, 256 * s:256 * s + 256], OTm[half][:, 128 * j:128 * j + 128],
                                    mo[:, p, :], start=True, stop=True)
                return last
            t2 = pe.do(mm, tn[2 * q + 1], free[6], t_mo)
            t_ot[half] = t2
            i = 4 * half + 2 * q
            o, src = acc[:, i:i + 2, :].rearrange("p a c -> p (a c)"), bank[6][:]
            if p == 0:
                t2 = dve.do(lambda e: e.tensor_copy(o, src), t2)
            else:
                t2 = dve.do(lambda e: e.tensor_tensor(o, o, src, ALU.add), t2, t_acc[i])
            t_acc[i] = t2
            free[6] = t2
        tn = {}
        for j in range(4):
            later(1 + j, lambda j=j: quarter(j))
        later(4, lambda: project(0))
        later(6, lambda: project(1))

    chunks = []

    def extra_main(u, what):
        p = u // 2
        if what == "max":
            return [list(t_qk[p]), t_kv[p % 2]]
        if what == "pv":
            return t_lat
        if what == "begin":
            if u % 2 == 0 and p + 1 < 8:
                chunks.extend(prep_steps(p + 1, [(pe.sem, pe.n)]))
            return None
        if isinstance(what, tuple) and chunks:
            for f in chunks.pop(0):
                f()
        return None

    units_main = [((2 * p, 2 * p + 1), half) for p in range(8) for half in range(2)]
    first_main, run_main = attention(units_main, False, score_main, mrow, lambda h, kt: kvx[:, kt, :], evac_main,
                                     (2, 3), extra_main, SC0, 1, t_old, OTm, 8, summed, ahead=1)

    early = []

    def extra_first(u, what):
        if what == "begin" and u == 18:
            w = [(pe.sem, pe.n), (dve.sem, dve.n)]
            early.append([lambda: latent_keys(0, w)])
            early.extend(prep_steps(0, w))
        if isinstance(what, tuple) and u < 14 and what[1] % 2 == 1:
            if fold_steps:
                fold_steps.pop(0)()
            elif 2 not in t_stacks:
                t_cs = [(act.sem, act.n)]
                l_cs.dma(cosT[:], a["cosT"], t_cs)
                l_cs.dma(sinT[:], a["sinT"], t_cs)
                load_heads(2, t_cs)
        if isinstance(what, tuple):
            if u < 30 and what[1] % 4 == 1 and early:
                for f in early.pop(0):
                    f()
            if u >= 30:
                while early:
                    for f in early.pop(0):
                        f()
                first_main.pop(0)()
        return extra_pat(u, what)
    extra_pat = extra16(t_stacks, t_v)
    clear(t_lat)
    _, run = attention(units, False, score16, None, value16, evac16(True, pctx, False, OTa), lambda u: (2, 3, 7) if 7 <= u < 18 else (2, 3),
                       extra_first, 0.25, 4, t_pj1, OTa, 9, mxbanks=(0, 1))
    run()
    t_old.extend([(pe.sem, pe.n), (dve.sem, dve.n), (act.sem, act.n)])
    t_zero = dve.do(lambda e: e.tensor_copy(onesr[:], ones3[0:11, :]), t_old, t_k)
    latent_keys(1, t_old)
    run_main()

    def out_projection(src, w, t_src, add, t_w, region, name):
        cT = region.sb(name, [128, 2, 2, 128], F32)
        t_x_new, t_c0 = [], [None, None]
        tmp = region.sb(name + "t", [128, 2, D], F32)
        for i in range(NT):
            z = i % 2

            def tr(e, i=i, z=z):
                for k in range(2):
                    last = e.transpose(bank[z][:, k * 128:(k + 1) * 128], src[:, i, k * 128:(k + 1) * 128], idf[:])
                return last
            t = pe.do(tr, t_src, free[z])
            t = act.do(lambda e, z=z: e.activation(cT[:, z, :, :].rearrange("p k c -> p (k c)"), bank[z][:, 0:256],
                                                   ACT.Copy), t, t_c0[z])
            free[z] = t

            def mm(e, z=z):
                for k in range(2):
                    last = e.matmul(bank[2 + z][:, 0:256], cT[:, z, k, :], w[:, 3, k, :], start=(k == 0),
                                    stop=(k == 1))
                return last
            t = pe.do(mm, t, free[2 + z], t_w)
            t_c0[z] = t
            t = dve.do(lambda e, i=i, z=z: add(e, tmp[:, z, :], bank[2 + z][:, 0:256], i), t, t_src)
            free[2 + z] = t
            layer = 0 if name == "cT0" else 1
            t = dve.do(lambda e, z=z, layer=layer: e.tensor_tensor(tmp[:, z, :], tmp[:, z, :], gab[:, 2 * layer, :],
                                                                   ALU.mult), t, t_g[layer])
            t = dve.do(lambda e, i=i, z=z: e.tensor_tensor(x[:, i, :], x[:, i, :], tmp[:, z, :], ALU.add), t)
            t_x_new.append(t)
        return t_x_new

    t_x1 = out_projection(pctx, wsp, [(dve.sem, dve.n)], lambda e, o, b, i: e.scalar_tensor_tensor(
        out=o, in0=acc[:, i, :], scalar=gat[:, i, 0:1], in1=b, op0=ALU.mult, op1=ALU.add), t_wsp, Region(S0), "cT0")

    F = Region(PHASE)
    t_phase = [(pe.sem, pe.n), (dve.sem, dve.n), (act.sem, act.n), (pool.sem, pool.n)]
    acc0 = F.sb("acc0", [128, NT, D], F32)
    wr = F.sb("wr", [128, 2, 8], F32)
    tmpr = F.sb("tmpr", [128, 2], F32)
    wraw = F.sb("wraw", [128, 2, 6 * 256], F32)
    wh = [F.sb(f"wh{i}", [128, 6 * 256], F32R) for i in range(2)]
    wl = [F.sb(f"wl{i}", [128, 6 * 256], F32R) for i in range(2)]
    sg = F.sb("sg", [128, 2, 512], F32)
    hf = F.sb("hf", [128, 2, 512], F32)
    hh = [F.sb(f"hh{i}", [128, 2, T], F32R) for i in range(2)]
    hl = [F.sb(f"hl{i}", [128, 2, T], F32R) for i in range(2)]
    gz = F.sb("gz", [128, 8, 64], F32)
    g64 = F.sb("g64", [128, 3, NT * 64], F32)
    wm1 = F.sb("wm1", [128, 2, 1536], F32)
    scb1 = F.sb("scb1", [128, 2, 128], F32)
    gt1 = F.sb("gt1", [128, 2, 256], F32)
    l_f = group("f0")
    l_f.dma(wr[:], a["wr"], t_phase)
    l_f.dma(tmpr[:, 0:1], a["temp"].partition_broadcast(128), t_phase)
    t_fr = (l_f.sem, l_f.n)
    l_fw = [group("fw0"), group("fw1")]
    t_wraw = [None] * 8
    for i in range(2):
        t_wraw[i] = l_fw[i].dma(wraw[:, i, :], a["wf0"][i], t_phase)

    t_wm1 = l_mod.dma(wm1[:], a["wmod1"], t_phase)

    t_h, t_p = norm(0, True, t_x1, True)
    t_h_cur = t_h

    def logits(e):
        for i in range(NT):
            for k in range(2):
                last = e.matmul(bank[4][:, i * 8:i * 8 + 8], hT[:, k, i * 128:(i + 1) * 128], wr[:, k, :],
                                start=(k == 0), stop=(k == 1))
        return last
    t_lg = pe.do(logits, t_h[0], t_h[1], t_fr, free[4])
    columns, gates = modulation(1, wm1, scb1, gt1, t_wm1, (5, 6, 7), t_phase)
    columns()
    gates()
    t = dve.do(lambda e: e.reciprocal(tmpr[:, 1:2], tmpr[:, 0:1]), t_fr)
    Z = [gz[:, i, :] for i in range(8)]
    V = [gz[:, i, :].rearrange("p (i e) -> p i e", e=8) for i in range(8)]

    def chain(steps, t):
        for q, f in steps:
            t = q.do(f, t)
        return t

    def bc(v):
        return v.unsqueeze(2).to_broadcast([128, NT, 8])
    s1 = [g64[:, 0, i * 8:i * 8 + 8] for i in range(4)]
    big = g64[:, 1, :].rearrange("p (i j k) -> p i j k", j=8, k=8)
    big2 = g64[:, 2, :].rearrange("p (i j k) -> p i j k", j=8, k=8)
    small = [gz[:, 7, i * 8:i * 8 + 8] for i in range(4)]

    def rank_steps(f, ne, o, bigs, tri_):
        b1, b2 = bigs

        def pairs(e, op, dst, i):
            v = f[:, i, :]
            return e.tensor_tensor(dst[:, i, :, :], v.unsqueeze(1).to_broadcast([128, ne, ne]),
                                   v.unsqueeze(2).to_broadcast([128, ne, ne]), op)

        def gt(e):
            for i in range(NT):
                last = pairs(e, ALU.is_gt, b1, i)
            return last

        def eq(e):
            for i in range(NT):
                last = pairs(e, ALU.is_equal, b2, i)
            return last

        def low(e):
            for i in range(NT):
                last = e.tensor_tensor(b2[:, i, :, :], b2[:, i, :, :], tri_, ALU.mult)
            return last
        return [(dve, gt), (dve, eq), (dve, low),
                (dve, lambda e: e.tensor_tensor(b1.rearrange("p i j k -> p (i j k)"),
                                                b1.rearrange("p i j k -> p (i j k)"),
                                                b2.rearrange("p i j k -> p (i j k)"), ALU.add)),
                (dve, lambda e: e.tensor_reduce(o, b1.rearrange("p i j k -> p (i j) k"), AX, ALU.add))]

    t = chain([
        (dve, lambda e: e.tensor_scalar(Z[0], bank[4][:, 0:64], tmpr[:, 1:2], -1.0, ALU.mult, ALU.mult)),
        (act, lambda e: e.activation(Z[0], Z[0], ACT.Exp)),
        (dve, lambda e: e.tensor_scalar(Z[0], Z[0], 1.0, None, ALU.add)),
        (dve, lambda e: e.reciprocal(Z[0], Z[0])),
    ], [t, t_lg])
    free[4] = t
    t = chain([
        (dve, lambda e: e.tensor_scalar(Z[1], Z[0], G_C, None, ALU.subtract)),
        (dve, lambda e: e.scalar_tensor_tensor(out=Z[1], in0=Z[1], scalar=-1.0, in1=Z[1], op0=ALU.mult, op1=ALU.max)),
        (dve, lambda e: e.tensor_scalar(Z[2], Z[0], G_LO, None, ALU.is_ge)),
        (dve, lambda e: e.tensor_scalar(Z[3], Z[0], 0.5, None, ALU.is_le)),
        (dve, lambda e: e.tensor_tensor(Z[2], Z[2], Z[3], ALU.mult)),
        (act, lambda e: e.activation(Z[3], Z[1], ACT.Exp, scale=-1.0 / 0.1)),
        (act, lambda e: e.activation(Z[4], Z[1], ACT.Exp, scale=-1.0 / 0.3)),
        (dve, lambda e: e.tensor_tensor(Z[2], Z[2], Z[3], ALU.mult)),
        (dve, lambda e: e.tensor_reduce(small[0], V[2], AX, ALU.add)),
        (dve, lambda e: e.tensor_scalar(small[0], small[0], 1e-8, None, ALU.is_lt)),
    ] + rank_steps(V[4], 8, Z[5], (big, big2), tri[:, 0:8, 0:8]) + [
        (dve, lambda e: e.scalar_tensor_tensor(out=Z[4], in0=Z[5], scalar=2.0, in1=Z[4], op0=ALU.is_lt, op1=ALU.mult)),
        (dve, lambda e: e.tensor_reduce(small[1], V[4], AX, ALU.add)),
        (dve, lambda e: e.tensor_scalar(small[1], small[1], 1e-8, None, ALU.max)),
        (dve, lambda e: e.reciprocal(small[1], small[1])),
        (dve, lambda e: e.tensor_tensor(small[1], small[1], small[0], ALU.mult)),
        (dve, lambda e: e.tensor_tensor(V[4], V[4], bc(small[1]), ALU.mult)),
        (dve, lambda e: e.tensor_scalar(small[0], small[0], -1.0, 1.0, ALU.mult, ALU.add)),
        (dve, lambda e: e.tensor_tensor(V[2], V[2], bc(small[0]), ALU.mult)),
        (dve, lambda e: e.tensor_tensor(Z[2], Z[2], Z[4], ALU.add)),
        (dve, lambda e: e.tensor_reduce(small[2], V[2], AX, ALU.add)),
        (dve, lambda e: e.tensor_scalar(small[2], small[2], 1e-8, None, ALU.max)),
        (dve, lambda e: e.reciprocal(small[2], small[2])),
        (dve, lambda e: e.tensor_tensor(V[6], V[2], bc(small[2]), ALU.mult)),
    ], t)
    t_gw = t

    def three(e, o, lh, ll, rh, rl, start, stop, **k):
        e.matmul(o, lh, rh, start=start, stop=False, **k)
        e.matmul(o, lh, rl, start=False, stop=False, **k)
        return e.matmul(o, ll, rh, start=False, stop=stop, **k)

    t_down = {}
    t_hf = [None, None]
    t_sg = [None, None]
    t_a0 = [None] * NT
    down_q = []
    nf = [0]

    def split_w(e_):
        z = e_ % 2
        th = act.do(lambda e: e.activation(wh[z][:], wraw[:, z, :], ACT.Copy), t_wraw[e_], t_down.get(e_ - 2))
        tl = dve.do(lambda e: e.tensor_tensor(wl[z][:], wraw[:, z, :], wh[z][:].bitcast(F32), ALU.subtract), th)
        if e_ + 2 < 8:
            t_wraw[e_ + 2] = l_fw[z].dma(wraw[:, z, :], a["wf0"][e_ + 2], th, tl)
        return [th, tl]

    def up0(e_, m, half, tw):
        z = e_ % 2
        cs = slice(half * 512, half * 512 + 512)
        n = nf[0] % 2
        nf[0] += 1
        bg, bu = 2 * n, 2 * n + 1

        def mm(e):
            for g, b in ((0, bg), (1, bu)):
                for k in range(2):
                    ws = slice((2 * g + k) * 256 + m * 128, (2 * g + k) * 256 + m * 128 + 128)
                    last = three(e, bank[b][:], wh[z][:, ws], wl[z][:, ws], hTh[:, k, cs], hTl[:, k, cs], k == 0, k == 1)
            return last
        t = pe.do(mm, tw, t_p, free[bg], free[bu])
        t1 = act.do(lambda e: e.activation(sg[:, n, :], bank[bg][:], ACT.Silu), t, t_sg[n])
        free[bg] = t1
        t2 = dve.do(lambda e: e.tensor_tensor(hf[:, n, :], sg[:, n, :], bank[bu][:], ALU.mult), t1, t_hf[n])
        free[bu] = t_sg[n] = t2
        th = act.do(lambda e: e.activation(hh[z][:, m, cs], hf[:, n, :], ACT.Copy), t2, t_down.get(e_ - 2))
        tl = pool.do(lambda e: e.tensor_tensor(hl[z][:, m, cs], hf[:, n, :], hh[z][:, m, cs].bitcast(F32),
                                               ALU.subtract), th)
        t_hf[n] = tl
        return [th, tl]

    def down0(e_, i, th):
        z = e_ % 2
        b = 4 + i % 4
        ts = slice(i * 128, (i + 1) * 128)

        def mm(e):
            for k in range(2):
                ws = slice((4 + k) * 256, (5 + k) * 256)
                last = three(e, bank[b][:, 0:256], hh[z][:, k, ts], hl[z][:, k, ts], wh[z][:, ws], wl[z][:, ws],
                             k == 0, k == 1)
            return last
        t = pe.do(mm, th, free[b])
        t_down[e_] = t
        w = gz[:, 6, i * 8 + e_:i * 8 + e_ + 1]
        if e_ == 0:
            t = dve.do(lambda e: e.tensor_scalar(acc0[:, i, :], bank[b][:, 0:256], w, None, ALU.mult), t, t_gw)
        else:
            t = dve.do(lambda e: e.scalar_tensor_tensor(out=acc0[:, i, :], in0=bank[b][:, 0:256], scalar=w,
                                                        in1=acc0[:, i, :], op0=ALU.mult, op1=ALU.add), t, t_a0[i])
        free[b] = t_a0[i] = t

    tw = split_w(0)
    for e_ in range(8):
        ths = [[], []]
        for half in range(2):
            for m in range(2):
                ths[half] += up0(e_, m, half, tw)
                for _ in range(2):
                    if down_q:
                        down0(*down_q.pop(0))
        if e_ + 1 < 8:
            tw = split_w(e_ + 1)
        down_q = [(e_, i, ths[i // 4]) for i in range(NT)]
    for d in down_q:
        down0(*d)
    t_x2 = []
    for i in range(NT):
        t = dve.do(lambda e, i=i: e.tensor_tensor(acc0[:, i, :], acc0[:, i, :], gab[:, 1, :], ALU.mult), t_a0[i], t_g[0])
        t_x2.append(dve.do(lambda e, i=i: e.tensor_tensor(x[:, i, :], x[:, i, :], acc0[:, i, :], ALU.add), t))

    t_phase = [(pe.sem, pe.n), (dve.sem, dve.n), (act.sem, act.n), (pool.sem, pool.n)]
    bcol = F_at = Region(PHASE + 8 * 1024)
    w1a = F_at.sb("w1a", [128, 4, 2, 256], F32)
    bcol = F_at.sb("bcol", [128, 4], F32)
    bvb = F_at.sb("bvb", [128, 256], F32)
    bob = F_at.sb("bob", [128, 256], F32)
    octx = F_at.sb("octx", [128, NT, D], F32)
    assert F_at.at <= S0
    l_a1 = group("a1")
    l_a1.dma(w1a[:], a["w1a"], t_phase)
    l_a1.dma(bcol[:], a["bqk"], t_phase)
    l_a1.dma(bvb[:], a["bv"].partition_broadcast(128), t_phase)
    l_a1.dma(bob[:], a["bo"].partition_broadcast(128), t_phase)
    t_w1a = (l_a1.sem, l_a1.n)
    t_h, _ = norm(1, False, t_x2, False)
    t_h_cur = t_h
    t_stacks, t_v, t_pjo, load_heads = project16(1, w1a, t_w1a, t_w1a, t_phase, t_phase, bq=bcol[:, 0:2], bk=bcol[:, 2:4], bvb=bvb,
                                                 scratch=scratch1)
    load_heads(2, t_phase)
    t_pj = [(act.sem, act.n), (dve.sem, dve.n), (pe.sem, pe.n), t_pjo]
    t_mc = dve.do(lambda e: e.memset(mcat[:], 1.0), t_pj)
    clear(t_pj)
    _, run = attention(units, True, score16, None, value16, evac16(False, octx, True, OTa), (2, 3),
                       extra16(t_stacks, t_v), 0.25, 4, t_pj, OTa, 9, mxbanks=(0, 1, 7))
    run()
    t_x3 = out_projection(octx, w1a, [(dve.sem, dve.n)], lambda e, o, b, i: e.tensor_tensor(
        o, b, bob[:], ALU.add), t_w1a, Region(S0), "cT1")

    t_phase = [(pe.sem, pe.n), (dve.sem, dve.n), (act.sem, act.n), (pool.sem, pool.n)]
    E = Region(PHASE)
    cen = E.sb("cen", [128, 2, 16], F32)
    bib = E.sb("bib", [128, 16], F32)
    b1c = E.sb("b1c", [128, NF], F32)
    b2r = E.sb("b2r", [18, 256], F32)
    selt = E.sb("selt", [113, NF * 128], BF16)
    wr1 = E.sb("wr1", [128, 4, 512], F32)
    v1h = [E.sb(f"v1h{i}", [128, 512], F32R) for i in range(4)]
    v1l = [E.sb(f"v1l{i}", [128, 512], F32R) for i in range(4)]
    gc = E.sb("gc", [128, NT, 113], F32)
    g3 = E.sb("g3", [113, T], BF16)
    gT = E.sb("gT", [18, T], F32)
    sgm = E.sb("sgm", [128, 3, 128], F32)
    gb3 = E.sb("gb3", [128, NT, 16], BF16)
    pr1 = E.sb("pr1", [128, NT * 256], F32)
    pr2 = E.sb("pr2", [128, NT * 256], F32)
    rl = E.sb("rl", [128, 2, 512], F32)
    hg = E.sb("hg", [128, 2, 512], F32)
    h1h = [E.sb(f"h1h{i}", [128, T], F32R) for i in range(2)]
    h1l = [E.sb(f"h1l{i}", [128, T], F32R) for i in range(2)]
    fin = E.sb("fin", [128, 2, 512], F32)
    l_e = group("e")
    l_e.dma(cen[:], a["cen"], t_phase)
    l_e.dma(bib[:], a["ebias"].partition_broadcast(128), t_phase)
    l_e.dma(b1c[:], a["b1c"], t_phase)
    l_e.dma(b2r[:], a["b2r"], t_phase)
    l_e.dma(selt[64:113, :], a["sel"], t_phase)
    t_e = (l_e.sem, l_e.n)
    l_ew = [group(f"ew{i}") for i in range(4)]
    t_ew = [None] * NF
    for i in range(4):
        t_ew[i] = l_ew[i].dma(wr1[:, i, :], a["wf1"][i], t_phase)
    t_gc0 = dve.do(lambda e: e.memset(gc[:], 1.0), t_phase)

    t_h, t_p = norm(1, True, t_x3, True)

    def logits1(e):
        for i in range(NT):
            for k in range(2):
                last = e.matmul(bank[6][:, i * 16:i * 16 + 16], hT[:, k, i * 128:(i + 1) * 128], cen[:, k, :],
                                start=(k == 0), stop=(k == 1))
        return last
    t = pe.do(logits1, t_h[0], t_h[1], t_e, free[6])
    sgf = [sgm[:, i, :] for i in range(3)]
    sgv = [sgm[:, i, :].rearrange("p (i e) -> p i e", e=16) for i in range(3)]
    sm = sd
    t = chain([
        (act, lambda e: e.activation(sgf[0], bank[6][:, 0:128], ACT.Exp, scale=-1.0)),
        (dve, lambda e: e.tensor_scalar(sgf[0], sgf[0], 1.0, None, ALU.add)),
        (dve, lambda e: e.reciprocal(sgf[0], sgf[0])),
        (dve, lambda e: e.tensor_tensor(sgv[0], sgv[0], bib[:].unsqueeze(1).to_broadcast([128, NT, 16]), ALU.add)),
    ] + rank_steps(sgv[0], 16, sgf[1], (pr1[:].rearrange("p (i j k) -> p i j k", j=16, k=16),
                                        pr2[:].rearrange("p (i j k) -> p i j k", j=16, k=16)), tri[:]) + [
        (dve, lambda e: e.scalar_tensor_tensor(out=sgf[0], in0=sgf[1], scalar=4.0, in1=sgf[0], op0=ALU.is_lt,
                                               op1=ALU.mult)),
        (dve, lambda e: e.tensor_reduce(sm[:], sgv[0], AX, ALU.add)),
        (dve, lambda e: e.tensor_scalar(sm[:], sm[:], 1e-8, None, ALU.max)),
        (dve, lambda e: e.reciprocal(sm[:], sm[:])),
        (dve, lambda e: e.tensor_tensor(gc[:, :, 0:16], sgv[0], sm[:].unsqueeze(2).to_broadcast([128, NT, 16]),
                                        ALU.mult)),
        (dve, lambda e: e.tensor_copy(gb3[:], gc[:, :, 0:16])),
        (dve, lambda e: e.tensor_copy(gc[:, :, 64:80], gb3[:])),
        (dve, lambda e: e.tensor_tensor(sgv[1], gc[:, :, 0:16], gc[:, :, 64:80], ALU.subtract)),
        (dve, lambda e: e.tensor_copy(gb3[:], sgv[1])),
        (dve, lambda e: e.tensor_copy(gc[:, :, 80:96], gb3[:])),
        (dve, lambda e: e.tensor_tensor(gc[:, :, 96:112], sgv[1], gc[:, :, 80:96], ALU.subtract)),
    ], [t, t_gc0])
    free[6] = t
    t_gt = []
    for half in range(2):
        b = 6 + half

        def tr(e, half=half, b=b):
            for j in range(4):
                last = e.transpose(bank[b][0:113, j * 128:(j + 1) * 128], gc[:, 4 * half + j, :], idf[:])
            return last
        tt = pe.do(tr, t, free[b])
        cs = slice(half * 512, half * 512 + 512)
        t1 = act.do(lambda e, b=b, cs=cs: e.activation(g3[64:113, cs], bank[b][64:113, :], ACT.Copy), tt)
        t2 = act.do(lambda e, b=b, cs=cs: e.activation(gT[:, cs], bank[b][0:18, :], ACT.Copy), tt)
        free[b] = t2
        t_gt += [t1, t2]

    def begin_sums(e):
        for i in range(NT):
            o = bank[i // 2][:, 256 * (i % 2):256 * (i % 2) + 256]
            ts = slice(i * 128, (i + 1) * 128)
            e.matmul(o, gT[:, ts], b2r[:], start=(i % 2 == 0), stop=False, skip_group_check=True)
            for k in range(2):
                for part in (hTh, hTl):
                    last = e.matmul(o[:, k * 128:(k + 1) * 128], part[:, k, ts], idr[:], start=False, stop=False,
                                    skip_group_check=True)
        return last
    pe.do(begin_sums, t_gt, t_p, t_e, t_idr, free[0], free[1], free[2], free[3])

    t_w1 = [None] * NF
    t_dn = [None] * NF
    t_rl, t_hg = [None, None], [None, None]

    def split1(f):
        z = f % 4
        th = act.do(lambda e: e.activation(v1h[z][:], wr1[:, z, :], ACT.Copy), t_ew[f], t_dn[f - 4] if f > 3 else None)
        tl = pool.do(lambda e: e.tensor_tensor(v1l[z][:], wr1[:, z, :], v1h[z][:].bitcast(F32), ALU.subtract), th)
        if f + 4 < NF:
            t_ew[f + 4] = l_ew[z].dma(wr1[:, z, :], a["wf1"][f + 4], th, tl)
        t_w1[f] = [th, tl]

    def up1(f, half):
        z, y = f % 4, f % 2
        cs = slice(half * 512, half * 512 + 512)
        bu, bg = 4 + half, 6 + half

        def mm(e):
            e.matmul(bank[bg][:], selt[64:113, f * 128:(f + 1) * 128], g3[64:113, cs], start=True, stop=True)
            for k in range(2):
                ws = slice(k * 128, (k + 1) * 128)
                last = three(e, bank[bu][:], v1h[z][:, ws], v1l[z][:, ws], hTh[:, k, cs], hTl[:, k, cs], k == 0, k == 1)
            return last
        t = pe.do(mm, t_w1[f], t_gt, free[bu], free[bg])
        t1 = act.do(lambda e: e.activation(rl[:, half, :], bank[bu][:], ACT.Relu, bias=b1c[:, f:f + 1]), t, t_rl[half])
        free[bu] = t1
        t2 = dve.do(lambda e: e.tensor_tensor(hg[:, half, :], rl[:, half, :], bank[bg][:], ALU.mult), t1, t_hg[half])
        free[bg] = t_rl[half] = t2
        th = act.do(lambda e: e.activation(h1h[y][:, cs], hg[:, half, :], ACT.Copy), t2, t_dn[f - 2] if f > 1 else None)
        tl = dve.do(lambda e: e.tensor_tensor(h1l[y][:, cs], hg[:, half, :], h1h[y][:, cs].bitcast(F32), ALU.subtract),
                    th)
        t_hg[half] = tl
        return [th, tl]

    def down1(f, half, th):
        z, y = f % 4, f % 2

        def mm(e):
            for i in range(4 * half, 4 * half + 4):
                o = bank[i // 2][:, 256 * (i % 2):256 * (i % 2) + 256]
                ts = slice(i * 128, (i + 1) * 128)
                last = three(e, o, h1h[y][:, ts], h1l[y][:, ts], v1h[z][:, 256:512], v1l[z][:, 256:512], False,
                             f == NF - 1, skip_group_check=True)
            return last
        t_dn[f] = pe.do(mm, th)
        return t_dn[f]

    split1(0)
    split1(1)
    ready_h = []
    t_out = {}
    for f in range(NF):
        if f + 2 < NF:
            split1(f + 2)
        for half in range(2):
            th = up1(f, half)
            ready_h.append((f, half, th))
            if len(ready_h) > 2:
                down1(*ready_h.pop(0))
    for r in ready_h:
        t_out[r[1]] = down1(*r)
    l_o = group("out")
    out_v = out.rearrange("a (i p) d -> p (a i) d", p=128)
    t_st = [None, None]
    for j in range(4):
        g = gab[:, 3, :].unsqueeze(1).to_broadcast([128, 2, 256])
        o = fin[:, j % 2, :].rearrange("p (a c) -> p a c", a=2)
        src = bank[j][:].rearrange("p (a c) -> p a c", a=2)
        t = dve.do(lambda e, o=o, src=src, g=g: e.tensor_tensor(o, src, g, ALU.mult), t_out[j // 2], t_st[j % 2], t_g[1])
        xs = x[:, 2 * j:2 * j + 2, :]
        t = dve.do(lambda e, o=o, xs=xs: e.tensor_tensor(xs, xs, o, ALU.add), t)
        t_st[j % 2] = t
        l_o.dma(out_v[:, 2 * j:2 * j + 2, :], xs, t)
    sp.ops.append((lambda e: e.wait_ge(l_o.sem, l_o.n), (), False))

    with nc.Block() as block:
        block.sync(sp.replay)
        block.gpsimd(pool.replay)
        block.scalar(act.replay)
        block.vector(dve.replay)
        block.tensor(pe.replay)


def bits(x):
    u = np.ascontiguousarray(x, np.float32).view(np.uint32)
    return ((u + 0x7FFF + ((u >> 16) & 1)) >> 16).astype(np.uint16)


def value_of(b):
    return (b.astype(np.uint32) << 16).view(np.float32)


def constants():
    c = {}
    eye = np.eye(128, dtype=np.float32)
    c["idf"] = eye
    c["idb"] = bits(eye)
    q, k = np.arange(128)[:, None], np.arange(128)[None, :]
    c["maskq"] = bits(np.where(k > q, NEG, 0.0))
    c["maskk"] = np.ascontiguousarray(c["maskq"].T)
    dm = np.zeros((11, 4, 128), np.float32)
    dm[0:3] = 1.0
    for j in range(4):
        dm[3 + j, j] = 1.0
        dm[7 + j, j] = 1.0
    c["dmask"] = dm
    es = np.zeros((128, 17), np.float32)
    for g in range(4):
        es[32 * g:32 * g + 17] = np.eye(17)
    c["esum"] = es
    c["ones3"] = np.ones((128, 128), np.float32)
    c["ones3"][0:3] = 0.0
    j = np.arange(16)
    c["tri"] = np.broadcast_to((j[None, :] < j[:, None]).astype(np.float32), (128, 16, 16)).copy()
    inv = (np.float32(1.0) / np.power(np.float32(10000.0), np.arange(0, 64, 2, dtype=np.float32) / np.float32(64)))
    fr = np.outer(np.arange(T, dtype=np.float32), inv.astype(np.float32)).astype(np.float32)
    cos, sin = np.cos(fr).T.astype(np.float32), np.sin(fr).T.astype(np.float32)
    c["cosT"] = np.concatenate([cos] * 4, 0)
    c["sinT"] = np.concatenate([-sin, sin] * 2, 0)
    start = 2 ** (-2 ** (-(math.log2(H) - 3)))
    slopes = np.array([start * start ** i for i in range(H)], np.float32)
    al = (slopes[:, None] * (np.arange(T, dtype=np.float32) - np.float32(T - 1))[None, :]) * np.float32(4)
    rows = np.ones((11, H, T), np.float32)
    c["qrow"] = bits(rows)
    k0 = rows.copy()
    k0[0:3] = 0.0
    c["krow0"] = bits(k0)
    r = al.astype(np.float32)
    k1 = bits(rows)
    for i in range(3):
        k1[i] = bits(r)
        r = r - value_of(k1[i])
    c["krow1"] = k1
    sel = np.zeros((49, NF * 128), np.float32)
    ex = np.arange(NF * 128) // FF1
    for f in range((NS1 + NE1) * FF1):
        if ex[f] < NS1:
            sel[48, f] = 1.0
        else:
            for p in range(3):
                sel[16 * p + ex[f] - NS1, f] = 1.0
    c["sel"] = bits(sel)
    return c


def layout(i):
    def rows2(w):
        return np.ascontiguousarray(w.reshape(2, 128, -1).transpose(1, 0, 2))

    def cat(*w):
        return np.concatenate(w, 0)
    d = {"x": i["L0_attn_hidden_states"]}
    d["cc"] = np.ascontiguousarray(np.stack([i["L0_c"][0], i["L1_c"][0]], 0).reshape(2, 2, 128).transpose(2, 0, 1))
    d["wmod0"], d["wmod1"] = rows2(i["L0_wmod"]), rows2(i["L1_wmod"])
    kva = i["L0_attn_kv_a_w"]
    d["w0a"] = rows2(cat(i["L0_attn_q_a_w"], kva[:64], i["L0_attn_gate_w"]).T)
    d["q_ln"], d["kv_ln"], d["gate_b"] = i["L0_attn_q_a_ln_w"], i["L0_attn_kv_a_ln_w"], i["L0_attn_gate_b"]
    kpe = kva[64:].reshape(8, 2, 64, 256)[:, ::-1].reshape(1024, 256).T
    d["wkpe"] = np.ascontiguousarray(kpe.reshape(2, 128, 8, 128).transpose(1, 0, 2, 3))
    qb = i["L0_attn_q_b_w"].reshape(16, 192, 192)
    qpe = qb[:, 128:, :].reshape(8, 2, 64, 192)[:, ::-1].reshape(8, 128, 192).transpose(2, 0, 1)
    d["wqpa"], d["wqpb"] = np.ascontiguousarray(qpe[:128]), np.ascontiguousarray(qpe[128:])
    d["qbn"] = np.ascontiguousarray(qb[:, :128, :].transpose(1, 0, 2))
    kvb = i["L0_attn_kv_b_w"].reshape(16, 256, 64)
    d["kvbk"] = np.ascontiguousarray(kvb[:, :128].transpose(1, 0, 2))
    d["kvbv"] = np.ascontiguousarray(kvb[:, 128:].transpose(1, 0, 2))
    d["owT"] = np.ascontiguousarray(i["L0_attn_o_w"].reshape(256, 16, 128).transpose(2, 1, 0))
    d["wsp0"] = np.ascontiguousarray(np.stack(
        [rows2(i[f"L0_attn_sp_{n}_w"].T) for n in "qkvo"], 1))
    d["wr"], d["temp"] = rows2(i["L0_ffn_Wr"]), i["L0_ffn_temperature"]

    def tiles(w):
        return w.reshape(8, 2, 128, 256).transpose(0, 2, 1, 3).reshape(8, 128, 512)
    d["wf0"] = np.ascontiguousarray(np.concatenate(
        [tiles(i["L0_ffn_Wg"]), tiles(i["L0_ffn_Wu"]), tiles(i["L0_ffn_Wd"])], 2))
    d["w1a"] = np.ascontiguousarray(np.stack([rows2(i[f"L1_attn_W{n}"]) for n in "qkvo"], 1))
    d["bqk"] = np.ascontiguousarray(np.concatenate(
        [i["L1_attn_bq"].reshape(2, 128).T, i["L1_attn_bk"].reshape(2, 128).T], 1))
    d["bv"], d["bo"] = i["L1_attn_bv"], i["L1_attn_bo"]
    d["cen"] = rows2(i["L1_ffn_centroids"].T)
    d["ebias"] = i["L1_ffn_bias"]
    pad = NF * 128 - 18 * FF1
    w1 = cat(i["L1_ffn_shared_w1"], i["L1_ffn_routed_w1"]).transpose(1, 0, 2).reshape(256, 18 * FF1)
    w1 = np.concatenate([w1, np.zeros((256, pad), w1.dtype)], 1).reshape(2, 128, NF, 128).transpose(2, 1, 0, 3)
    w2 = cat(i["L1_ffn_shared_w2"], i["L1_ffn_routed_w2"]).reshape(18 * FF1, 256)
    w2 = cat(w2, np.zeros((pad, 256), w2.dtype)).reshape(NF, 128, 256)
    d["wf1"] = np.ascontiguousarray(np.concatenate([w1.reshape(NF, 128, 256), w2], 2))
    b1 = cat(i["L1_ffn_shared_b1"], i["L1_ffn_routed_b1"]).reshape(-1)
    d["b1c"] = np.ascontiguousarray(cat(b1, np.zeros(pad, b1.dtype)).reshape(NF, 128).T)
    d["b2r"] = np.ascontiguousarray(cat(i["L1_ffn_routed_b2"], i["L1_ffn_shared_b2"]))
    return d


def kernel(**inputs):
    import concourse.bacc as _bacc
    from concourse.bass_utils import run_bass_kernel_spmd as _run

    arrays = {k: np.ascontiguousarray(v) for k, v in layout({k: np.asarray(v) for k, v in inputs.items()}).items()}
    arrays.update(constants())
    nc = _bacc.Bacc("TRN2", target_bir_lowering=False, num_devices=1)
    aps = {n: nc.dram_tensor(n, v.shape, mybir.dt.from_np(v.dtype), kind="ExternalInput").ap()
           for n, v in arrays.items()}
    aps = {n: ap.bitcast(BF16) if arrays[n].dtype == np.uint16 else ap for n, ap in aps.items()}
    o = nc.dram_tensor("out_x", (1, T, D), F32, kind="ExternalOutput").ap()
    program(nc, aps, o)
    r = _run(nc, [arrays], core_ids=[0])
    return r.results[0]["out_x"]
```

```python
import math

import numpy as np

import concourse.bass as bass
from concourse import mybir

F32 = mybir.dt.float32
F32R = mybir.dt.float32r
BF16 = mybir.dt.bfloat16
ALU = mybir.AluOpType
ACT = mybir.ActivationFunctionType
AX = mybir.AxisListType.X

T, D, NT = 1024, 256, 8
H = 16
NE0, NE1, NS1, FF1 = 8, 16, 2, 176
NF = 25
NEG = -1e30
SC0 = 192.0 ** -0.5
G_LO = float(np.float32(0.5 - np.log(4.0 / 3.0)))
G_C = float(np.float32(1.0 / np.e))


LAG0 = (2, 2, 0, 2)
LAGM = (2, 3, -3, -1)
LAG1 = (2, 2, 0, 2)


class Queue:

    def __init__(self, sem):
        self.sem, self.n, self.ops = sem, 0, []

    def do(self, fn, *waits):
        self.n += 1
        self.ops.append((fn, waits, True))
        return (self.sem, self.n)

    def issue(self, fn, *waits):
        self.ops.append((fn, waits, False))

    def replay(self, eng):
        seen = {}

        def wait(w):
            if w is None:
                return
            if isinstance(w, list):
                for x in w:
                    wait(x)
                return
            sem, value = w
            if seen.get(id(sem), 0) < value:
                seen[id(sem)] = value
                eng.wait_ge(sem, value)

        for fn, waits, signals in self.ops:
            wait(list(waits))
            last = fn(eng)
            if signals:
                last.then_inc(self.sem, 1)


class Loads:

    def __init__(self, sem, queue):
        self.sem, self.q, self.n = sem, queue, 0

    def dma(self, dst, src, *waits):
        self.n += 16
        self.q.issue(lambda e: e.dma_start(dst, src).then_inc(self.sem, 16), *waits)
        return (self.sem, self.n)


def program(nc, a, out):
    def sem(name):
        return nc.alloc_semaphore(name)

    pe, dve, act, pool = (Queue(sem(f"q_{n}")) for n in ("pe", "dve", "act", "pool"))
    sp = Queue(sem("q_sp"))

    base = [16512]

    def sb(name, shape, dt, at=None):
        size = int(np.prod(shape[1:])) * (2 if dt == BF16 else 4)
        size = (size + 31) // 32 * 32
        if at is None:
            at = base[0]
            base[0] += size
        return nc.alloc_sbuf_tensor_at(name, list(shape), dt, offset=at)

    class Region:

        def __init__(self, at):
            self.at = at

        def sb(self, name, shape, dt):
            size = int(np.prod(shape[1:])) * (2 if dt == BF16 else 4)
            size = (size + 31) // 32 * 32
            t = nc.alloc_sbuf_tensor_at(name, list(shape), dt, offset=self.at)
            self.at += size
            assert self.at <= 229344, (name, self.at)
            return t

    bank = [nc.alloc_psum_tensor(f"bank{i}", [128, 512], F32) for i in range(8)]
    free = [None] * 8

    x = sb("x", [128, NT, D], F32)
    hT = sb("hT", [128, 2, T], F32)
    HTP = base[0]
    hTh = sb("hTh", [128, 2, T], F32R)
    hTl = sb("hTl", [128, 2, T], F32R)
    idf = sb("idf", [128, 128], F32)
    idr = sb("idr", [128, 128], F32R)
    ones1 = sb("ones1", [128, 64], F32)
    idb = sb("idb", [128, 128], BF16)
    maskq = sb("maskq", [128, 128], BF16)
    maskk = sb("maskk", [128, 128], BF16)
    dmask = sb("dmask", [11, 4, 128], F32)
    esum = sb("esum", [128, 17], F32)
    ones3 = sb("ones3", [128, 128], F32)
    tri = sb("tri", [128, 16, 16], F32)
    modc = sb("modc", [128, 2, 12], F32)
    gab = sb("gab", [128, 4, D], F32)
    HN = base[0]
    hn = sb("hn", [128, 2, D], F32)
    st6 = sb("st6", [128, NT, 6], F32)
    mv = sb("mv", [128, NT, 2], F32)
    sd = sb("sd", [128, NT], F32)
    rs = sb("rs", [128, NT], F32)
    mp = sb("mp", [128, 3, 2, 4, 2], F32)
    mcat = sb("mcat", [128, 2, 2, 11], F32)
    mbf = sb("mbf", [128, 2, 4], BF16)
    cc = sb("cc", [128, 2, 2], F32)
    sc_ = sb("sc_", [128, 2, 2], F32)
    rcp = sb("rcp", [128, 2, 4], F32)
    PHASE = base[0]

    loads = {}

    def group(name):
        loads[name] = Loads(sem(f"d_{name}"), sp)
        return loads[name]

    l_x, l_c, l_mod = [group("x0"), group("x1")], group("c"), group("mod")
    A = Region(PHASE)
    KV = A.at
    cosT = A.sb("cosT", [128, T], F32)
    sinT = A.sb("sinT", [128, T], F32)
    W0A = A.at
    w0a = A.sb("w0a", [128, 2, 258], F32)
    WSP = A.at
    wsp = A.sb("wsp", [128, 4, 2, 256], F32)
    wkpe = A.sb("wkpe", [128, 2, 8, 128], F32)
    wqpa = A.sb("wqpa", [128, 8, 128], F32)
    wqpb = A.sb("wqpb", [64, 8, 128], F32)
    waba = A.sb("waba", [128, 16, 64], F32)
    wabb = A.sb("wabb", [64, 16, 64], F32)
    mo = A.sb("mo", [128, 8, 256], F32)
    MP = Region(A.at)
    A.at += 6144
    lnw = A.sb("lnw", [128, 256], F32)
    qmTa = A.sb("qmTa", [128, T], F32)
    qmTb = A.sb("qmTb", [64, T], F32)
    kvT = A.sb("kvT", [128, T], F32)
    kvx = A.sb("kvx", [128, NT, 64], F32)
    gat = A.sb("gat", [128, NT, 2], F32)
    gsb = A.sb("gsb", [128, 2], F32)
    pctx = sb("pctx", [128, NT, D], F32, at=HTP)
    acc = sb("acc", [128, NT, D], F32, at=HTP + 4 * NT * D)
    S0 = A.at
    PB = Region(S0 + 64 * 1024)
    Pb = [PB.sb(f"Pb{i}", [128, 512], F32) for i in range(9)]
    PBE = PB.at
    vx = PB.sb("vx", [128, NT, 16 * 17], F32)
    S = Region(S0)
    qst = S.sb("qst", [107, 16, T], BF16)
    kst = S.sb("kst", [107, 16, T], BF16)
    PJ = Region(S0 + 64 * 1024)
    res = PJ.sb("res", [128, 2, 512], F32)
    stg = [PJ.sb(f"stg{i}", [128, 3, T], BF16) for i in range(2)]

    qbn = sb("qbn", [128, 16, 192], F32, at=S0 + 48 * 1024)
    kvbk = sb("kvbk", [128, 16, 64], F32, at=S0 + 60 * 1024)
    owT = sb("owT", [128, 16, 256], F32, at=S0 + 16 * 1024)
    kvbv = sb("kvbv", [128, 16, 64], F32, at=KV)
    C = Region(S0 + 32 * 1024)
    wm0 = C.sb("wm0", [128, 2, 1536], F32)
    scb0 = C.sb("scb0", [128, 2, 128], F32)
    gt0 = C.sb("gt0", [128, 2, 256], F32)

    l_c.dma(idf[:], a["idf"])
    l_c.dma(cc[:], a["cc"])
    t_c = (l_c.sem, l_c.n)
    t_x = []
    for i in range(2):
        t_x += [(l_x[i].dma(x[:, 4 * i:4 * i + 4, :],
                            a["x"].rearrange("a (i p) d -> p (a i) d", p=128)[:, 4 * i:4 * i + 4, :]))] * 4
    t_wm_a = l_mod.dma(wm0[:, :, 0:512], a["wmod0"][:, :, 0:512])
    l_w, l_wv = group("w"), group("wv")
    t_wqk = l_w.dma(wsp[:, 0:2, :, :], a["wsp0"][:, 0:2, :, :])
    t_wm = group("mod2").dma(wm0[:, :, 512:1536], a["wmod0"][:, :, 512:1536])
    t_wsp = l_wv.dma(wsp[:, 2:4, :, :], a["wsp0"][:, 2:4, :, :])
    l_w2 = group("w2")
    l_w2.dma(w0a[:], a["w0a"])
    l_w2.dma(lnw[:, 0:192], a["q_ln"].partition_broadcast(128))
    l_w2.dma(lnw[:, 192:256], a["kv_ln"].partition_broadcast(128))
    l_w2.dma(gsb[:], a["gate_b"].partition_broadcast(128))
    t_w2 = (l_w2.sem, l_w2.n)
    l_k, l_w3, l_w4, l_cs = group("k"), group("w3"), group("w4"), group("cs")

    def later_loads():
        for d, n in ((idb, "idb"), (maskq, "maskq"), (maskk, "maskk"), (dmask, "dmask"), (tri, "tri"), (esum, "esum"),
                     (ones3, "ones3")):
            l_k.dma(d[:], a[n])
        for d, n in ((qbn, "qbn"), (kvbk, "kvbk"), (owT, "owT"), (kvbv, "kvbv")):
            l_w3.dma(d[:], a[n])
        for d, n in ((wkpe, "wkpe"), (wqpa, "wqpa"), (wqpb, "wqpb")):
            l_w4.dma(d[:], a[n])
        return (l_k.sem, l_k.n), (l_w3.sem, l_w3.n), (l_w4.sem, l_w4.n)

    t_idr = act.do(lambda e: e.activation(idr[:], idf[:], ACT.Copy), t_c)

    t_mod, t_g = {}, {}

    def modulation(layer, wm, scb, tmp, t_w, banks, waits=None):
        c, s = cc[:, layer, :], sc_[:, layer, :]
        t = act.do(lambda e: e.activation(s, c, ACT.Silu), t_c)

        def spread(e):
            for k in range(2):
                last = e.tensor_scalar(scb[:, k, :], idf[:], 0.0, sc_[:, layer, k:k + 1], ALU.mult, ALU.add)
            return last
        t_s = dve.do(spread, t, waits)
        b0, b1, b2 = banks

        def columns(starts=(0, 6), t_w=t_w):
            def mm(e):
                for j in [s + i for s in starts for i in range(4)]:
                    for k in range(2):
                        last = e.matmul(bank[b0][:, j:j + 1], wm[:, k, j * 128:(j + 1) * 128], scb[:, k, 0:1],
                                        start=(k == 0), stop=(k == 1))
                return last
            tc = pe.do(mm, t_s, t_w, free[b0])

            def put(e):
                for s in starts:
                    e.tensor_copy(modc[:, layer, s:s + 2], bank[b0][:, s:s + 2])
                    last = e.tensor_scalar(modc[:, layer, s + 2:s + 4], bank[b0][:, s + 2:s + 4], 1.0, None, ALU.add)
                return last
            def finish():
                free[b0] = t_mod[layer] = dve.do(put, tc)
            return finish

        def gates():
            def rows(e):
                for g, b in ((0, b1), (1, b2)):
                    for k in range(2):
                        lo = 512 + 768 * g
                        last = e.matmul(bank[b][:, 0:256], scb[:, k, :], wm[:, k, lo:lo + 256],
                                        start=(k == 0), stop=(k == 1))
                return last
            tr = pe.do(rows, t_s, t_w, free[b1], free[b2])
            for g, bn in ((0, b1), (1, b2)):
                b, o, m = bank[bn][:, 0:256], gab[:, 2 * layer + g, :], tmp[:, g, :]
                ta = dve.do(lambda e, b=b, m=m: e.tensor_scalar(m, b, -1.0, 0.25, ALU.mult, ALU.max), tr)
                ta = dve.do(lambda e, b=b, m=m: e.scalar_tensor_tensor(out=m, in0=b, scalar=1.0, in1=m,
                                                                      op0=ALU.mult, op1=ALU.max), ta)
                tb = dve.do(lambda e, b=b, o=o: e.tensor_scalar(o, b, 0.0, 2.0, ALU.is_ge, ALU.mult), tr)
                free[bn] = tb
                t_g[layer] = dve.do(lambda e, o=o, m=m: e.scalar_tensor_tensor(out=o, in0=o, scalar=-1.0, in1=m,
                                                                              op0=ALU.add, op1=ALU.mult), ta, tb)
            return tr
        return columns, gates

    def bn(i, t):
        return dve.do(lambda e: e.bn_stats(st6[:, i, :], x[:, i, :]), t)

    def norm(layer, second, t_in, parts, hook=None):
        s0, c0 = (6, 8) if second else (0, 2)
        t_h, t_p, t_rs = [], [], {}
        t_tr = [None] * NT

        def stats(half):
            ts = []
            hs = slice(4 * half, 4 * half + 4)
            for i in range(4 * half, 4 * half + 4):
                ts.append(bn(i, t_in[i]) if hook else t_in[i])
            for j in range(4):
                t = dve.do(lambda e, i=4 * half + j: e.bn_aggr(mv[:, i, :], st6[:, i, :]), ts[j])
            t = dve.do(lambda e: e.tensor_scalar(sd[:, hs], mv[:, hs, 1], 1e-5, None, ALU.add), t)
            t = act.do(lambda e: e.activation(sd[:, hs], sd[:, hs], ACT.Sqrt), t)
            t_rs[half] = dve.do(lambda e: e.reciprocal(rs[:, hs], sd[:, hs]), t)

        def turn(half):
            b0, b1 = 2 * half, 2 * half + 1
            for j in range(4):
                i = 4 * half + j
                t_n = dve.do(lambda e, i=i: e.tensor_scalar(hn[:, i % 2, :], x[:, i, :], mv[:, i, 0:1], rs[:, i:i + 1],
                                                            ALU.subtract, ALU.mult), t_rs[half],
                             t_tr[i - 2] if i > 1 else None)

                def tr(e, i=i, j=j):
                    e.transpose(bank[b0][:, j * 128:(j + 1) * 128], hn[:, i % 2, 0:128], idf[:])
                    return e.transpose(bank[b1][:, j * 128:(j + 1) * 128], hn[:, i % 2, 128:256], idf[:])
                t_tr[i] = pe.do(tr, t_n, t_c, free[b0], free[b1])

        def put(half):
            b0 = 2 * half
            tt = []
            cs = slice(half * 512, half * 512 + 512)
            for k in range(2):
                te = act.do(lambda e, k=k, b=b0 + k: e.activation(
                    hT[:, k, cs], bank[b][:], ACT.Identity, bias=modc[:, layer, s0 + k:s0 + k + 1],
                    scale=modc[:, layer, c0 + k:c0 + k + 1]), t_tr[4 * half + 3], t_mod[layer])
                free[b0 + k] = te
                tt.append(te)
                if parts:
                    th = act.do(lambda e, k=k: e.activation(hTh[:, k, cs], hT[:, k, cs], ACT.Copy), te)
                    tl = dve.do(lambda e, k=k: e.tensor_tensor(
                        hTl[:, k, cs], hT[:, k, cs], hTh[:, k, cs].bitcast(F32), ALU.subtract), th)
                    t_p.extend([th, tl])
            t_h.append(tt)
        stats(0)
        if hook:
            stats(1)
        turn(0)
        if not hook:
            stats(1)
            put(0)
        turn(1)
        if hook:
            hook()
            put(0)
        put(1)
        return t_h, t_p

    columns, gates = modulation(0, wm0, scb0, gt0, t_wm, (4, 5, 6))
    t_h, _ = norm(0, False, t_x, False, lambda: columns((0,), t_wm_a)())

    BLK = (0, 2, 1, 3)
    GROUPS = ((0, 4), (4, 8), (8, 16))

    def project16(layer, w, t_wqk, t_wv, t_stack_free, t_pj_free, bq=None, bk=None, bvb=None, scratch=None,
                  between=None, after=None, later_v=False):
        g_out = [group(f"so{layer}{i}") for i in range(2)]
        g_in = [group(f"si{layer}{i}") for i in range(3)]
        t_stack, t_out = {}, {}
        t_res = [None, None]
        QP, KP = (0, 0, 1, 0, 2, 1), (0, 1, 0, 2, 0, 1)

        def load_heads(g, waits):
            h0, h1 = GROUPS[g]
            hs = slice(h0, h1)
            m = [t_out[h0 // 8], t_out[2 + h0 // 8]]
            for n, (st, parts) in enumerate(((qst, QP), (kst, KP))):
                for s, part in enumerate(parts):
                    src = scratch[n * 256 + 16 * h0:n * 256 + 16 * h1, part, :].rearrange("(h d) t -> d h t", d=16)
                    g_in[g].dma(st[16 * s:16 * s + 16, hs, :], src, m, waits)
                g_in[g].dma(st[96:107, hs, :], a["qrow" if n == 0 else f"krow{layer}"][:, hs, :], waits)
            t_stack[g] = (g_in[g].sem, g_in[g].n)

        for blk, (n, m) in enumerate(((0, 0), (1, 0), (0, 1), (1, 1))):
            bias = (bq, bk)[n]
            z = blk % 2
            for half in range(2):
                b = 4 + (2 * blk + half) % 4
                cs = slice(half * 512, half * 512 + 512)

                def mm(e, n=n, m=m, b=b, cs=cs):
                    for k in range(2):
                        last = e.matmul(bank[b][:], w[:, n, k, m * 128:(m + 1) * 128], hT[:, k, cs],
                                        start=(k == 0), stop=(k == 1))
                    return last
                bc_ = 0.0 if bias is None else bias[:, m:m + 1]
                t_o = t_out.get(BLK[blk - 2]) if blk > 1 else None

                def run(mm=mm, bc_=bc_, b=b, cs=cs, half=half, z=z, t_o=t_o, bias=bias):
                    t = pe.do(mm, t_wqk, t_h_cur[half], free[b])
                    t1 = act.do(lambda e: e.activation(stg[z][:, 0, cs], bank[b][:],
                                                       ACT.Copy if bias is None else ACT.Identity, bias=bc_), t, t_o,
                                t_pj_free)
                    t2 = dve.do(lambda e: e.scalar_tensor_tensor(out=res[:, half, :], in0=bank[b][:], scalar=bc_,
                                                                 in1=stg[z][:, 0, cs], op0=ALU.add, op1=ALU.subtract),
                                t1, t_res[half], t_pj_free)
                    free[b] = t2
                    t3 = act.do(lambda e: e.activation(stg[z][:, 1, cs], res[:, half, :], ACT.Copy), t2)
                    t_res[half] = dve.do(lambda e: e.tensor_tensor(stg[z][:, 2, cs], res[:, half, :],
                                                                   stg[z][:, 1, cs], ALU.subtract), t3)
                    return t_res[half]
                t4 = run()
            row = (n * 2 + m) * 128
            t_out[n * 2 + m] = g_out[z].dma(scratch[row:row + 128, :, :], stg[z][:], t4)
            if blk == 1:
                if after:
                    after()
                load_heads(0, t_stack_free)
            if blk == 3:
                load_heads(1, t_stack_free)
                if between:
                    between()
        t_v = []

        def values():
            tm = pool.do(lambda e: e.memset(vx[:].rearrange("p i (h c) -> p (i h) c", c=17)[:, :, 16:17], 1.0), t_pj_free)
            for i in range(NT):
                b = 6 + i % 2

                def mm(e, i=i, b=b):
                    for k in range(2):
                        last = e.matmul(bank[b][:, 0:256], hT[:, k, i * 128:(i + 1) * 128], w[:, 2, k, :],
                                        start=(k == 0), stop=(k == 1))
                    return last
                t = pe.do(mm, t_wv, t_h_cur[i // 4], free[b])
                dst = vx[:, i, :].rearrange("p (h c) -> p h c", c=17)[:, :, 0:16]
                src = bank[b][:, 0:256].rearrange("p (h c) -> p h c", c=16)
                if bvb is None:
                    t = act.do(lambda e, dst=dst, src=src: e.activation(dst, src, ACT.Copy), t, t_pj_free)
                else:
                    t = dve.do(lambda e, dst=dst, src=src: e.tensor_tensor(
                        dst, src, bvb[:].rearrange("p (h c) -> p h c", c=16), ALU.add), t, t_pj_free)
                free[b] = t
                t_v.append(t)
            t_v.append(tm)
        if not later_v:
            values()

        return t_stack, t_v, list(t_out.values()), load_heads, values

    def attention(units, causal, score, row, value, evac, stbanks, extra, scale, G, t_p0, OT, npb, summed=None,
                  mxbanks=(0, 1), ahead=2, lag=(2, 3, 0, 2), max_first=False):
        n = len(units)
        nh = len(units[0][0])
        w = 128 // (G * nh)
        t_mp, t_tr, t_row = {}, {}, {}
        t_neg = {}
        t_sfree = [t_p0 if summed is None else [t_p0, None]] * len(Pb)
        scount = [0]
        mcount = [0]

        def max_steps(u):
            hs, half = units[u]
            steps = []
            for a in range(nh):
                for j in range(4):
                    qi = 4 * half + j
                    for kh in range(2):
                        keys = (qi + 1) * 128 if causal else T
                        c = min(512, keys - 512 * kh)
                        if c > 0:
                            steps.append((a, j, qi, kh, c))
            return steps

        def do_max(u, step):
            a, j, qi, kh, c = step
            hs, half = units[u]
            mb = mxbanks(u) if callable(mxbanks) else mxbanks
            b = mb[mcount[0] % len(mb)]
            mcount[0] += 1
            diag = causal and (qi // 4) == kh

            def mm(e):
                last = score(e, "max", hs[a], qi, kh, c, bank[b][:, 0:c])
                if diag:
                    last = e.matmul(bank[b][:, c - 128:c], idb[:], maskq[:], start=False, stop=True,
                                    skip_group_check=True)
                return last
            t = pe.do(mm, free[b], extra(u, "max"))
            t = dve.do(lambda e: e.tensor_reduce(mp[:, u % 3, a, j, kh:kh + 1], bank[b][:, 0:c], AX, ALU.max), t)
            free[b] = t
            t_mp[u] = t

        def do_neg(u):
            hs, half = units[u]
            two = not (causal and half == 0)
            dst, low = mcat[:, u % 2, 0:nh, 3:7], mcat[:, u % 2, 0:nh, 7:11]
            if two:
                t = dve.do(lambda e: e.tensor_reduce(dst, mp[:, u % 3, 0:nh, :, :], AX, ALU.max, negate=True),
                           t_mp[u], t_tr.get(u - 2, t_p0))
            else:
                t = dve.do(lambda e: e.tensor_scalar(dst, mp[:, u % 3, 0:nh, :, 0], -1.0, None, ALU.mult),
                           t_mp[u], t_tr.get(u - 2, t_p0))
            t = dve.do(lambda e: e.tensor_copy(mbf[:, 0:nh, :], dst), t)
            t = dve.do(lambda e: e.tensor_tensor(low, dst, mbf[:, 0:nh, :], ALU.subtract), t)
            t_neg[u] = t

        def do_tr(u):
            def tr(e):
                for a in range(nh):
                    last = e.transpose(bank[6][0:11, 128 * a:128 * a + 128], mcat[:, u % 2, a, :], idf[:])
                return last
            t_tr[u] = pe.do(tr, t_neg[u], free[6], t_k)

        def do_row(u):
            hs, half = units[u]
            for a in range(nh):
                o = (qst[96:107, hs[a], half * 512:half * 512 + 512] if row is None else row[u % 2 * 2 + a][0:11, :])
                t = dve.do(lambda e, a=a, o=o: e.tensor_tensor(
                    o.rearrange("p (j c) -> p j c", j=4),
                    bank[6][0:11, 128 * a:128 * a + 128].unsqueeze(1).to_broadcast([11, 4, 128]),
                    dmask[:], ALU.mult), t_tr[u], t_stdone.get(u - 2, t_p0))
            free[6] = t
            t_row[u] = t

        t_stdone = {}
        t_exp = {}

        def do_st(u, a, kt):
            hs, half = units[u]
            q0 = max(128 * kt, 512 * half) if causal else 512 * half
            c = 512 * (half + 1) - q0
            sb_ = stbanks(u) if callable(stbanks) else stbanks
            b = sb_[scount[0] % len(sb_)]
            p = scount[0] % npb
            scount[0] += 1
            diag = causal and kt >= 4 * half

            def mm(e):
                last = score(e, "st", hs[a], kt, q0, c, bank[b][:, 0:c], u % 2 * 2 + a)
                if diag:
                    last = e.matmul(bank[b][:, 0:128], idb[:], maskk[:], start=False, stop=True,
                                    skip_group_check=True)
                return last
            t = pe.do(mm, free[b], t_row[u])
            t_stdone[u] = t
            te = act.do(lambda e: e.activation(Pb[p][:, 0:c], bank[b][:, 0:c], ACT.Exp, scale=scale), t, t_sfree[p])
            free[b] = te
            t_exp[u, a, kt] = (te, p, q0)
            if summed is not None:
                t_sfree[p] = [None, summed(u, a, kt, Pb[p], te)]
                if kt == 1:
                    p0 = t_exp[u, a, 0][1]
                    t_sfree[p0] = [t_sfree[p0][0], t_sfree[p][1]]

        def do_pv(u, aks):
            hs, half = units[u]
            b = 4 + half
            nk = 4 * half + 4 if causal else NT

            def mm(e):
                for a, kt in aks:
                    _, p, q0 = t_exp[u, a, kt]
                    v = value(hs[a], kt)
                    g = w * (a * G + kt % G)
                    last = e.matmul(bank[b][g:g + v.shape[1], q0 - 512 * half:512], v, Pb[p][:, 0:512 * (half + 1) - q0],
                                    start=(kt < G), stop=(kt + G >= nk), skip_group_check=True)
                return last
            t = pe.do(mm, [t_exp[u, a, kt][0] for a, kt in aks], free[b] if aks[0] == (0, 0) else None, extra(u, "pv"))
            for a, kt in aks:
                p = t_exp[u, a, kt][1]
                t_sfree[p] = [t, t_sfree[p][1]] if summed is not None else t
            if aks[-1] == (nh - 1, nk - 1):
                to = act.do(lambda e: e.activation(OT[half][:], bank[b][:], ACT.Copy), t, t_ot[half])
                free[b] = to
                later(lag[1], lambda: evac(u, hs, half, to, t_ot, later))

        due = []

        def later(n, f):
            due.append((scount[0] + n, f))

        t_ot = [t_p0, t_p0]

        def run_due():
            for d in [d for d in due if d[0] <= scount[0]]:
                due.remove(d)
                d[1]()

        first = [lambda s=s: do_max(0, s) for s in max_steps(0)]

        def run():
            while first:
                first.pop(0)()
            do_neg(0)
            do_tr(0)
            do_row(0)
            if n > 1 and ahead == 2:
                for s in max_steps(1):
                    do_max(1, s)
            for u in range(n):
                hs, half = units[u]
                nk = (4 * half + 4 if causal else NT) * nh
                steps = max_steps(u + ahead) if u + ahead < n else []
                total, given = len(steps), 0
                last_max = nk if ahead == 2 else nk - 4
                at = lag[2] % nk
                extra(u, "begin")
                aks = []
                for k in range(nk):
                    a, kt = k % nh, k // nh
                    if k == at and u + 1 < n:
                        do_neg(u + 1)
                    if max_first:
                        while given < total and given * last_max < total * (k + 1):
                            do_max(u + ahead, steps[given])
                            given += 1
                    do_st(u, a, kt)
                    if k == lag[3] % nk and u + 1 < n:
                        do_tr(u + 1)
                        do_row(u + 1)
                    while given < total and given * last_max < total * (k + 1):
                        do_max(u + ahead, steps[given])
                        given += 1
                    extra(u, ("step", k))
                    aks.append((a, kt))
                    if len(aks) == G * nh:
                        due.append((scount[0] + lag[0], lambda u=u, aks=aks: do_pv(u, aks)))
                        aks = []
                    run_due()
            while due:
                scount[0] += 1
                run_due()
        return first, run

    t_h_cur = t_h
    scratch = nc.dram_tensor("scratch", (512, 3, T), BF16, kind="Internal").ap()
    scratch1 = nc.dram_tensor("scratch1", (512, 3, T), BF16, kind="Internal").ap()
    t_more = []
    t_free0 = []

    def more_modulation():
        columns((6,))()
        t_free0.append(gates())
        t_free0.append(t_g[0])
    t_stacks, t_v, t_pjo, load_heads, values = project16(0, wsp, t_wqk, t_wsp, t_free0, None, scratch=scratch,
                                                 between=lambda: t_more.extend(later_loads()), after=more_modulation, later_v=True)
    t_k, t_w3, t_w4 = t_more

    fold_steps = []
    t_wab, t_mo, t_fold = [], [], []

    def fold_parts():
        def qk(rows, dst, g, c0):
            t = {}

            def product(q):
                def mm(e):
                    for i in range(4 * q, 4 * q + 4):
                        last = e.matmul(bank[7][0:rows, 64 * i:64 * i + 64], qbn[:, 8 * g + i, c0:c0 + rows],
                                        kvbk[:, 8 * g + i, :], start=True, stop=True)
                    return last
                t[0] = pe.do(mm, t_w3, free[7])

            def put():
                free[7] = act.do(lambda e: e.activation(dst[:, 8 * g:8 * g + 8, :].rearrange("p h c -> p (h c)"),
                                                        bank[7][0:rows, :], ACT.Copy), t[0])
                t_wab.append(free[7])
            return [lambda: product(0), lambda: product(1), put]

        def v(g):
            t = {}

            def product(q):
                def mm(e):
                    for s in range(2):
                        h = 4 * g + 2 * q + s
                        last = e.matmul(bank[7][64 * s:64 * s + 64, 256 * q:256 * q + 256], kvbv[:, h, :], owT[:, h, :],
                                        start=True, stop=True)
                    return last
                t[0] = pe.do(mm, t_w3, free[7])

            def put():
                free[7] = act.do(lambda e: e.activation(mo[:, 2 * g:2 * g + 2, :].rearrange("p a c -> p (a c)"),
                                                        bank[7][:], ACT.Copy), t[0])
                t_mo.append(free[7])
            return [lambda: product(0), lambda: product(1), put]
        for g in range(4):
            fold_steps.extend(v(g))
        for g in range(2):
            fold_steps.extend(qk(128, waba, g, 0))
            fold_steps.extend(qk(64, wabb, g, 128))
    fold_parts()

    L = Region(MP.at)
    sq = L.sb("sq", [128, 192], F32)
    ss = L.sb("ss", [128, NT, 2], F32)
    rr = L.sb("rr", [128, NT, 2], F32)
    rq = L.sb("rq", [128, NT, 2], F32)
    gw_ = L.sb("gw_", [128, NT, 2], F32)
    gm_ = L.sb("gm_", [128, NT], F32)
    qkv = L.sb("qkv", [128, 2, 256 + 64], F32)
    raw = sb("raw", [128, NT, 256], F32, at=HTP + 4 * NT * D)
    t_pj0 = [(act.sem, act.n), (dve.sem, dve.n)]
    t3 = None
    for i in range(NT):
        b = i % 4

        def mm(e, i=i, b=b):
            for k in range(2):
                last = e.matmul(bank[b][:, 0:258], hT[:, k, i * 128:(i + 1) * 128], w0a[:, k, :],
                                start=(k == 0), stop=(k == 1))
            return last
        t = pe.do(mm, t_w2, t_h[i // 4], free[b])
        t = act.do(lambda e, i=i, b=b: e.activation(raw[:, i, :], bank[b][:, 0:256], ACT.Copy), t)
        t_gw = act.do(lambda e, i=i, b=b: e.activation(gw_[:, i, :], bank[b][:, 256:258], ACT.Copy))
        free[b] = t_gw
        t2 = dve.do(lambda e, i=i: e.tensor_tensor_reduce(sq[:], raw[:, i, 0:192], raw[:, i, 0:192], 1.0 / 192, 0.0,
                                                          ALU.mult, ALU.add, ss[:, i, 0:1]), t, t3)
        t3 = dve.do(lambda e, i=i: e.tensor_tensor_reduce(sq[:, 0:64], raw[:, i, 192:256], raw[:, i, 192:256],
                                                          1.0 / 64, 0.0, ALU.mult, ALU.add, ss[:, i, 1:2]), t2)
    values()
    t = dve.do(lambda e: e.tensor_scalar(rr[:], ss[:], 1e-6, None, ALU.add), t2, t3)
    t = act.do(lambda e: e.activation(rr[:], rr[:], ACT.Sqrt), t)
    t_rq = dve.do(lambda e: e.reciprocal(rq[:], rr[:]), t)
    t = dve.do(lambda e: e.tensor_tensor(gw_[:], gw_[:], gsb[:].unsqueeze(1).to_broadcast([128, NT, 2]), ALU.add),
               t_gw)
    t = dve.do(lambda e: e.tensor_reduce(gm_[:], gw_[:], AX, ALU.max), t)
    t = dve.do(lambda e: e.tensor_tensor(gw_[:], gw_[:], gm_[:].unsqueeze(2).to_broadcast([128, NT, 2]),
                                         ALU.subtract), t)
    t = act.do(lambda e: e.activation(gw_[:], gw_[:], ACT.Exp), t)
    t = dve.do(lambda e: e.tensor_reduce(gm_[:], gw_[:], AX, ALU.add), t)
    t = dve.do(lambda e: e.reciprocal(gm_[:], gm_[:]), t)
    t_gat = dve.do(lambda e: e.tensor_tensor(gat[:], gw_[:], gm_[:].unsqueeze(2).to_broadcast([128, NT, 2]),
                                             ALU.mult), t)
    t_ones = pool.do(lambda e: e.memset(ones1[:], 1.0))
    t_qt = [None] * NT
    for half in range(2):
        b0, b1, b2 = 0, 1, 2
        for j in range(4):
            i = 4 * half + j
            z = i % 2

            def sc(e, i=i, z=z):
                e.scalar_tensor_tensor(out=qkv[:, z, 0:192], in0=raw[:, i, 0:192], scalar=rq[:, i, 0:1],
                                       in1=lnw[:, 0:192], op0=ALU.mult, op1=ALU.mult)
                return e.scalar_tensor_tensor(out=qkv[:, z, 192:256], in0=raw[:, i, 192:256], scalar=rq[:, i, 1:2],
                                              in1=lnw[:, 192:256], op0=ALU.mult, op1=ALU.mult)
            t = dve.do(sc, t_rq, t_w2, t_qt[i - 2] if i > 1 else None)
            t = dve.do(lambda e, z=z: e.tensor_copy(qkv[:, z, 256:320], qkv[:, z, 192:256]), t)
            t_kvx = dve.do(lambda e, i=i, z=z: e.tensor_copy(kvx[:, i, 0:64], qkv[:, z, 192:256]), t)

            def tr(e, j=j, z=z):
                js = slice(j * 128, (j + 1) * 128)
                e.transpose(bank[b0][:, js], qkv[:, z, 0:128], idf[:])
                e.transpose(bank[b1][0:64, js], qkv[:, z, 128:192], idf[:])
                return e.transpose(bank[b2][:, js], qkv[:, z, 192:320], idf[:])
            t_qt[i] = pe.do(tr, t_kvx, t, free[b0], free[b1], free[b2])
        cs = slice(half * 512, half * 512 + 512)
        free[b0] = act.do(lambda e, cs=cs: e.activation(qmTa[:, cs], bank[b0][:], ACT.Copy), t_qt[4 * half + 3])
        free[b1] = act.do(lambda e, cs=cs: e.activation(qmTb[:, cs], bank[b1][0:64, :], ACT.Copy), t_qt[4 * half + 3])
        free[b2] = act.do(lambda e, cs=cs: e.activation(kvT[:, cs], bank[b2][:], ACT.Copy), t_qt[4 * half + 3])
    t_lat = [(act.sem, act.n), t_kvx, t_ones]

    t_mc = pool.do(lambda e: e.memset(mcat[:], 1.0))
    units = [((h,), half) for h in range(H) for half in range(2)]

    def score16(e, kind, h, i, j, c, o, u=None):
        if kind == "max":
            return e.matmul(o, qst[0:99, h, i * 128:(i + 1) * 128], kst[0:99, h, j * 512:j * 512 + c],
                            start=True, stop=True)
        return e.matmul(o, kst[0:107, h, i * 128:(i + 1) * 128], qst[0:107, h, j:j + c], start=True, stop=True)

    def value16(h, kt):
        return vx[:, kt, h * 17:h * 17 + 17]

    t_rc = {}

    def evac16(gated, dst, causal, OT):
        def f(u, hs, half, to, t_ot, later):
            h = hs[0]

            def mm(e):
                for j in range(4):
                    rows = 32 * (j + 1) if causal and half == 0 else 128
                    last = e.matmul(bank[6][:, 128 + 17 * j:145 + 17 * j], OT[half][0:rows, 128 * j:128 * j + 128],
                                    esum[0:rows, :], start=True, stop=True)
                return last
            t = pe.do(mm, to, free[6])
            t_ot[half] = t
            r = rcp[:, u % 2, :]
            v = bank[6][:, 128:196].rearrange("p (j c) -> p j c", c=17)
            tr = dve.do(lambda e: e.reciprocal(r, v[:, :, 16]), t)
            if gated:
                tr = dve.do(lambda e: e.tensor_tensor(r, r, gat[:, 4 * half:4 * half + 4, 1], ALU.mult), tr, t_gat)
            free[6] = dve.do(lambda e: e.tensor_tensor(dst[:, 4 * half:4 * half + 4, h * 16:h * 16 + 16],
                                                       v[:, :, 0:16], r.unsqueeze(2).to_broadcast([128, 4, 16]),
                                                       ALU.mult), tr)
        return f

    def clear(t):
        for b in (4, 5):
            free[b] = dve.do(lambda e, b=b: e.memset(bank[b][:], 0.0), free[b], t)

    t_pj1 = [(act.sem, act.n), (dve.sem, dve.n), (pe.sem, pe.n), t_pjo]

    def extra16(t_stack, tv, t_clear):
        def f(u, what):
            if u == 0 and what == ("step", 0):
                clear(t_clear)
            if what == "max":
                return [t_stack[min(u // 8, 2)], t_mc]
            if what == "pv":
                return tv
            return None
        return f

    OTa = [sb(f"OTa{i}", [128, 512], F32, at=HTP + 4 * NT * D + 2048 * i) for i in range(2)]
    S2 = Region(S0)
    QKh, QKl = [[None] * 4, [None] * 4], [[None] * 4, [None] * 4]
    for QK, part in ((QKh, "h"), (QKl, "l")):
        for i2 in range(2):
            for n in range(2):
                for i in (2 * i2, 2 * i2 + 1):
                    QK[n][i] = S2.sb(f"qk{n}{part}{i}", [128, T], F32R)
    M0 = Region(WSP)
    t12 = M0.sb("t12", [128, 2, 512], F32)
    Rt = M0.sb("Rt", [128, 512], F32)
    M2 = Region(PBE - 2048)
    mrow = [M2.sb(f"mrow{i}", [11, 512], BF16) for i in range(4)]
    onesr = M2.sb("onesr", [11, 128], BF16)
    OTm = [M2.sb(f"OTm{i}", [128, 512], F32) for i in range(2)]
    Ps = [MP.sb(f"Ps{i}", [128, 512], F32) for i in range(3)] + [sb("Ps3", [128, 512], F32, at=HN)]
    t_old = []

    def latent_keys(pair, waits):
        def kvh(e):
            for i in (2 * pair, 2 * pair + 1):
                r = slice(0, 64) if i % 2 == 0 else slice(64, 128)
                last = e.activation(QKh[1][i][r, :], kvT[r, :], ACT.Copy)
            return last

        def kvl(e):
            for i in (2 * pair, 2 * pair + 1):
                r = slice(0, 64) if i % 2 == 0 else slice(64, 128)
                last = e.tensor_tensor(QKl[1][i][r, :], kvT[r, :], QKh[1][i][r, :].bitcast(F32), ALU.subtract)
            return last
        th = act.do(kvh, waits, t_lat)
        t_kv[pair] = [th, dve.do(kvl, th, waits)]

    t_kv = [None, None]
    t_qk = {}
    t_t12, t_R = [None], [None]

    def prep_steps(p, waits):
        z = 2 * (p % 2)
        done = t_qk.setdefault(p, [])

        def rope(n, half):
            cs = slice(half * 512, half * 512 + 512)
            t = {}

            def product():
                def mm(e):
                    if n == 1:
                        for k in range(2):
                            last = e.matmul(bank[7][:], wkpe[:, k, p, :], hT[:, k, cs], start=(k == 0), stop=(k == 1))
                        return last
                    e.matmul(bank[7][:], wqpa[:, p, :], qmTa[:, cs], start=True, stop=False)
                    return e.matmul(bank[7][:], wqpb[:, p, :], qmTb[:, cs], start=False, stop=True)
                t[0] = pe.do(mm, free[7], t_lat, t_w4, (l_cs.sem, l_cs.n))

            def swap():
                def f(e):
                    for q in range(4):
                        last = e.activation(t12[32 * (q ^ 1):32 * (q ^ 1) + 32, 1, :], bank[7][32 * q:32 * q + 32, :],
                                            ACT.Copy)
                    return last
                t[1] = act.do(f, t[0], t_t12[0], *waits)

            def turn():
                ts = pool.do(lambda e: e.tensor_tensor(t12[:, 1, :], t12[:, 1, :], sinT[:, cs], ALU.mult), t[1])
                tc = dve.do(lambda e: e.tensor_tensor(t12[:, 0, :], bank[7][:], cosT[:, cs], ALU.mult), t[1],
                            t_t12[0], *waits)
                free[7] = tc
                t[2] = pool.do(lambda e: e.tensor_tensor(Rt[:], t12[:, 0, :], t12[:, 1, :], ALU.add), tc, ts, t_R[0])
                t_t12[0] = t[2]

            def high():
                def hi(e):
                    e.activation(QKh[n][z][64:128, cs], Rt[64:128, :], ACT.Copy)
                    return e.activation(QKh[n][z + 1][0:64, cs], Rt[0:64, :], ACT.Copy)
                t[3] = act.do(hi, t[2], *waits)

            def low():
                def lo(e):
                    e.tensor_tensor(QKl[n][z][64:128, cs], Rt[64:128, :], QKh[n][z][64:128, cs].bitcast(F32),
                                    ALU.subtract)
                    return e.tensor_tensor(QKl[n][z + 1][0:64, cs], Rt[0:64, :], QKh[n][z + 1][0:64, cs].bitcast(F32),
                                           ALU.subtract)
                tl = dve.do(lo, t[3], *waits)
                t_R[0] = tl
                done.extend([t[3], tl])
            return [product, swap, turn, high, low]

        def lat(half):
            cs = slice(half * 512, half * 512 + 512)
            t = {}

            def product():
                def mm(e):
                    wa = waba[:, 2 * p:2 * p + 2, :].rearrange("p h c -> p (h c)")
                    wb = wabb[:, 2 * p:2 * p + 2, :].rearrange("p h c -> p (h c)")
                    e.matmul(bank[7][:], wa, qmTa[:, cs], start=True, stop=False)
                    return e.matmul(bank[7][:], wb, qmTb[:, cs], start=False, stop=True)
                t[0] = pe.do(mm, free[7], t_lat, t_wab)

            def high():
                def hi(e):
                    e.activation(QKh[0][z][0:64, cs], bank[7][0:64, :], ACT.Copy)
                    return e.activation(QKh[0][z + 1][64:128, cs], bank[7][64:128, :], ACT.Copy)
                t[1] = act.do(hi, t[0], *waits)

            def low():
                def lo(e):
                    e.tensor_tensor(QKl[0][z][0:64, cs], bank[7][0:64, :], QKh[0][z][0:64, cs].bitcast(F32),
                                    ALU.subtract)
                    return e.tensor_tensor(QKl[0][z + 1][64:128, cs], bank[7][64:128, :],
                                           QKh[0][z + 1][64:128, cs].bitcast(F32), ALU.subtract)
                tl = dve.do(lo, t[1])
                free[7] = tl
                done.extend([t[1], tl])
            return [product, high, low]
        r = [rope(1, 0), rope(1, 1), rope(0, 0), rope(0, 1)]
        q = [lat(0), lat(1)]
        steps = [(r[0][0],), (r[0][1],), (r[0][2],),
                 (r[0][3], q[0][0]), (r[0][4], q[0][1]), (q[0][2],),
                 (r[1][0],), (r[1][1],), (r[1][2],),
                 (r[1][3], r[2][0]), (r[2][1], r[1][4]), (r[2][2],),
                 (r[2][3], q[1][0]), (q[1][1], r[2][4]), (q[1][2],),
                 (r[3][0],), (r[3][1],), (r[3][2],), (r[3][3],), (r[3][4],)]
        return steps

    def bufs(h):
        i = 2 * ((h // 2) % 2) + h % 2
        return QKh[0][i], QKl[0][i], QKh[1][i], QKl[1][i]

    def score_main(e, kind, h, i, j, c, o, u=None):
        qh, ql, kh, kl = bufs(h)
        if kind == "max":
            return e.matmul(o, qh[:, i * 128:(i + 1) * 128], kh[:, j * 512:j * 512 + c], start=True, stop=True)
        ks, qs = slice(i * 128, (i + 1) * 128), slice(j, j + c)
        e.matmul(o, kh[:, ks], qh[:, qs], start=True, stop=False)
        e.matmul(o, kh[:, ks], ql[:, qs], start=False, stop=False)
        e.matmul(o, kl[:, ks], qh[:, qs], start=False, stop=False)
        return e.matmul(o, onesr[:], mrow[u][:], start=False, stop=True)

    t_acc = [None] * NT
    t_ps = [t_old] * 4
    held = {}

    def summed(u, a, kt, P, te):
        z = u % 2 * 2 + a
        o = Ps[z][:]
        if kt == 0:
            held[z] = P
            return None
        first = held[z][:] if kt == 1 else o
        t = pool.do(lambda e: e.tensor_tensor(o, first, P[:], ALU.add), te, t_ps[z])
        t_ps[z] = t
        return t

    def evac_main(u, hs, half, to, t_ot, later):
        p, b, z = hs[0] // 2, 4 + half, u % 2 * 2

        def den(e):
            for a in range(2):
                last = e.matmul(bank[b][64 * a:64 * a + 64, :], ones1[:], Ps[z + a][:], start=True, stop=True)
            return last
        t = pe.do(den, t_ps[z], t_ps[z + 1], free[b], t_ones)
        t_ps[z] = t_ps[z + 1] = t

        def quarter(j):
            js = slice(128 * j, 128 * j + 128)
            tr = dve.do(lambda e: e.reciprocal(Ps[z][:, js], bank[b][:, js]), t)
            t_ps[z] = tr
            if j == 3:
                free[b] = tr
            tn[j] = pool.do(lambda e: e.tensor_tensor(OTm[half][:, js], OTm[half][:, js], Ps[z][:, js], ALU.mult), tr, to)
            t_ps[z] = tn[j]

        def project(q):
            def mm(e):
                for s in range(2):
                    j = 2 * q + s
                    last = e.matmul(bank[6][:, 256 * s:256 * s + 256], OTm[half][:, 128 * j:128 * j + 128],
                                    mo[:, p, :], start=True, stop=True)
                return last
            t2 = pe.do(mm, tn[2 * q + 1], free[6], t_mo)
            t_ot[half] = t2
            i = 4 * half + 2 * q
            o, src = acc[:, i:i + 2, :].rearrange("p a c -> p (a c)"), bank[6][:]
            if p == 0:
                t2 = dve.do(lambda e: e.tensor_copy(o, src), t2)
            else:
                t2 = dve.do(lambda e: e.tensor_tensor(o, o, src, ALU.add), t2, t_acc[i])
            t_acc[i] = t2
            free[6] = t2
        tn = {}
        for j in range(4):
            later(1 + j, lambda j=j: quarter(j))
        later(4, lambda: project(0))
        later(6, lambda: project(1))

    chunks = []

    def extra_main(u, what):
        p = u // 2
        if what == "max":
            return [list(t_qk[p]), t_kv[p % 2]]
        if what == "pv":
            return t_lat
        if what == "begin":
            if u == 0:
                latent_keys(1, t_old)
            if u % 2 == 0 and p + 1 < 8:
                chunks.extend(prep_steps(p + 1, [(pe.sem, pe.n)]))
            return None
        if isinstance(what, tuple) and chunks:
            for f in chunks.pop(0):
                f()
        return None

    units_main = [((2 * p, 2 * p + 1), half) for p in range(8) for half in range(2)]
    first_main, run_main = attention(units_main, False, score_main, mrow, lambda h, kt: kvx[:, kt, :], evac_main,
                                     (2, 3), extra_main, SC0, 1, t_old, OTm, 8, summed, ahead=1,
                                     lag=LAGM)

    early = []

    def extra_first(u, what):
        if what == "begin" and u == 18:
            w = [(pe.sem, pe.n), (dve.sem, dve.n)]
            early.append([lambda: latent_keys(0, w)])
            early.extend(prep_steps(0, w))
        if isinstance(what, tuple) and u < 14 and what[1] % 2 == 1:
            if fold_steps:
                fold_steps.pop(0)()
            elif 2 not in t_stacks:
                t_cs = [(act.sem, act.n)]
                l_cs.dma(cosT[:], a["cosT"], t_cs)
                l_cs.dma(sinT[:], a["sinT"], t_cs)
                load_heads(2, t_cs)
        if isinstance(what, tuple):
            if u < 30 and what[1] % 4 == 3 and early:
                for f in early.pop(0):
                    f()
            if u >= 30:
                while early:
                    for f in early.pop(0):
                        f()
                first_main.pop(0)()
        return extra_pat(u, what)
    extra_pat = extra16(t_stacks, t_v, t_lat)
    _, run = attention(units, False, score16, None, value16, evac16(True, pctx, False, OTa), lambda u: (2, 3, 7) if 7 <= u < 18 else (2, 3),
                       extra_first, 0.25, 4, t_pj1, OTa, 9, mxbanks=(0, 1), lag=LAG0)
    run()
    t_old.extend([(pe.sem, pe.n), (dve.sem, dve.n), (act.sem, act.n)])
    t_zero = dve.do(lambda e: e.tensor_copy(onesr[:], ones3[0:11, :]), t_old, t_k)
    run_main()

    def out_projection(src, w, t_src, add, t_w, region, name):
        cT = region.sb(name, [128, 4, 2, 128], F32)
        t_x_new, t_c0 = [], [None] * 4
        tmp = region.sb(name + "t", [128, 4, D], F32)
        layer = 0 if name == "cT0" else 1
        t_ct, t_tmp, adds = {}, {}, []

        def turn(i):
            z = i % 4

            def tr(e):
                for k in range(2):
                    last = e.transpose(bank[z][:, k * 128:(k + 1) * 128], src[:, i, k * 128:(k + 1) * 128], idf[:])
                return last
            t = pe.do(tr, t_src, free[z])
            t_ct[i] = free[z] = act.do(lambda e: e.activation(
                cT[:, z, :, :].rearrange("p k c -> p (k c)"), bank[z][:, 0:256], ACT.Copy), t, t_c0[z])

        def product(i):
            z = i % 4

            def mm(e):
                for k in range(2):
                    last = e.matmul(bank[4 + z][:, 0:256], cT[:, z, k, :], w[:, 3, k, :], start=(k == 0), stop=(k == 1))
                return last
            t = t_c0[z] = pe.do(mm, t_ct[i], free[4 + z], t_w)
            t = free[4 + z] = dve.do(lambda e: add(e, tmp[:, z, :], bank[4 + z][:, 0:256], i), t, t_src,
                                     t_tmp.get(z))
            t = pool.do(lambda e: e.tensor_tensor(tmp[:, z, :], tmp[:, z, :], gab[:, 2 * layer, :], ALU.mult), t,
                        t_g[layer])
            adds.append((i, t))

        def put(i, t):
            z = i % 4
            t_tmp[z] = dve.do(lambda e: e.tensor_tensor(x[:, i, :], x[:, i, :], tmp[:, z, :], ALU.add), t)
            t_x_new.append(bn(i, t_tmp[z]))
        for i in range(NT + 2):
            if i < NT:
                turn(i)
            if i >= 2:
                product(i - 2)
            if len(adds) > 2:
                put(*adds.pop(0))
        for v in adds:
            put(*v)
        return t_x_new

    t_att = [(pe.sem, pe.n), (dve.sem, dve.n), (act.sem, act.n), (pool.sem, pool.n)]
    F = Region(PHASE)
    G = Region(S0 + 8 * 1024)
    wraw = G.sb("wraw", [128, 2, 6 * 256], F32)
    wh = [G.sb(f"wh{i}", [128, 6 * 256], F32R) for i in range(2)]
    wl = [G.sb(f"wl{i}", [128, 6 * 256], F32R) for i in range(2)]
    wr = G.sb("wr", [128, 2, 8], F32)
    tmpr = G.sb("tmpr", [128, 2], F32)
    gz = G.sb("gz", [128, 8, 64], F32)
    g64 = G.sb("g64", [128, 3, NT * 64], F32)
    sg = G.sb("sg", [128, 2, 512], F32)
    wm1 = G.sb("wm1", [128, 2, 1536], F32)
    scb1 = G.sb("scb1", [128, 2, 128], F32)
    gt1 = G.sb("gt1", [128, 2, 256], F32)
    acc0 = F.sb("acc0", [128, NT, D], F32)
    w1a = F.sb("w1a", [128, 4, 2, 256], F32)
    bcol = F.sb("bcol", [128, 4], F32)
    bvb = F.sb("bvb", [128, 256], F32)
    bob = F.sb("bob", [128, 256], F32)
    octx = sb("octx", [128, NT, D], F32, at=F.at)
    hf = F.sb("hf", [128, 2, 512], F32)
    hh = [F.sb(f"hh{i}", [128, 2, T], F32R) for i in range(2)]
    hl = [F.sb(f"hl{i}", [128, 2, T], F32R) for i in range(2)]
    assert F.at <= S0
    t_wm1 = l_mod.dma(wm1[:], a["wmod1"], t_att)
    l_f = group("f0")
    l_f.dma(wr[:], a["wr"], t_att)
    l_f.dma(tmpr[:, 0:1], a["temp"].partition_broadcast(128), t_att)
    t_fr = (l_f.sem, l_f.n)
    l_fw = [group("fw0"), group("fw1")]
    t_wraw = [None] * 8
    for i in range(2):
        t_wraw[i] = l_fw[i].dma(wraw[:, i, :], a["wf0"][i], t_att)

    columns, gates = modulation(1, wm1, scb1, gt1, t_wm1, (7, 5, 6), t_att)
    t_x1 = out_projection(pctx, wsp, [(dve.sem, dve.n)], lambda e, o, b, i: e.scalar_tensor_tensor(
        out=o, in0=acc[:, i, :], scalar=gat[:, i, 0:1], in1=b, op0=ALU.mult, op1=ALU.add), t_wsp, Region(S0), "cT0")
    t_phase = [(pe.sem, pe.n), (dve.sem, dve.n), (act.sem, act.n), (pool.sem, pool.n)]
    l_a1 = group("a1")
    l_a1.dma(w1a[:], a["w1a"], t_phase)
    l_a1.dma(bcol[:], a["bqk"], t_phase)
    l_a1.dma(bvb[:], a["bv"].partition_broadcast(128), t_phase)
    l_a1.dma(bob[:], a["bo"].partition_broadcast(128), t_phase)
    t_w1a = (l_a1.sem, l_a1.n)

    put_columns = columns()
    t_h, t_p = norm(0, True, t_x1, True)
    put_columns()
    t_h_cur = t_h

    def logits(e):
        for i in range(NT):
            for k in range(2):
                last = e.matmul(bank[4][:, i * 8:i * 8 + 8], hT[:, k, i * 128:(i + 1) * 128], wr[:, k, :],
                                start=(k == 0), stop=(k == 1))
        return last
    t_lg = pe.do(logits, t_h[0], t_h[1], t_fr, free[4])
    t = dve.do(lambda e: e.reciprocal(tmpr[:, 1:2], tmpr[:, 0:1]), t_fr)
    Z = [gz[:, i, :] for i in range(8)]
    V = [gz[:, i, :].rearrange("p (i e) -> p i e", e=8) for i in range(8)]

    def chain(steps, t):
        for q, f in steps:
            t = q.do(f, t)
        return t

    def bc(v):
        return v.unsqueeze(2).to_broadcast([128, NT, 8])
    s1 = [g64[:, 0, i * 8:i * 8 + 8] for i in range(4)]
    big = g64[:, 1, :].rearrange("p (i j k) -> p i j k", j=8, k=8)
    big2 = g64[:, 2, :].rearrange("p (i j k) -> p i j k", j=8, k=8)
    small = [gz[:, 7, i * 8:i * 8 + 8] for i in range(4)]

    def rank_steps(f, ne, o, bigs, tri_):
        b1, b2 = bigs

        def pairs(e, op, dst, i):
            v = f[:, i, :]
            return e.tensor_tensor(dst[:, i, :, :], v.unsqueeze(1).to_broadcast([128, ne, ne]),
                                   v.unsqueeze(2).to_broadcast([128, ne, ne]), op)

        def gt(e):
            for i in range(NT):
                last = pairs(e, ALU.is_gt, b1, i)
            return last

        def eq(e):
            for i in range(NT):
                last = pairs(e, ALU.is_equal, b2, i)
            return last

        def low(e):
            for i in range(NT):
                last = e.tensor_tensor(b2[:, i, :, :], b2[:, i, :, :], tri_, ALU.mult)
            return last
        return [(dve, gt), (dve, eq), (dve, low),
                (dve, lambda e: e.tensor_tensor(b1.rearrange("p i j k -> p (i j k)"),
                                                b1.rearrange("p i j k -> p (i j k)"),
                                                b2.rearrange("p i j k -> p (i j k)"), ALU.add)),
                (dve, lambda e: e.tensor_reduce(o, b1.rearrange("p i j k -> p (i j) k"), AX, ALU.add))]

    gating = [
        (dve, lambda e: e.tensor_scalar(Z[0], bank[4][:, 0:64], tmpr[:, 1:2], -1.0, ALU.mult, ALU.mult)),
        (act, lambda e: e.activation(Z[0], Z[0], ACT.Exp)),
        (dve, lambda e: e.tensor_scalar(Z[0], Z[0], 1.0, None, ALU.add)),
        (dve, lambda e: e.reciprocal(Z[0], Z[0])),
        (dve, lambda e: e.tensor_scalar(Z[1], Z[0], G_C, None, ALU.subtract)),
        (dve, lambda e: e.scalar_tensor_tensor(out=Z[1], in0=Z[1], scalar=-1.0, in1=Z[1], op0=ALU.mult, op1=ALU.max)),
        (dve, lambda e: e.tensor_scalar(Z[2], Z[0], G_LO, None, ALU.is_ge)),
        (dve, lambda e: e.tensor_scalar(Z[3], Z[0], 0.5, None, ALU.is_le)),
        (dve, lambda e: e.tensor_tensor(Z[2], Z[2], Z[3], ALU.mult)),
        (act, lambda e: e.activation(Z[3], Z[1], ACT.Exp, scale=-1.0 / 0.1)),
        (act, lambda e: e.activation(Z[4], Z[1], ACT.Exp, scale=-1.0 / 0.3)),
        (dve, lambda e: e.tensor_tensor(Z[2], Z[2], Z[3], ALU.mult)),
        (dve, lambda e: e.tensor_reduce(small[0], V[2], AX, ALU.add)),
        (dve, lambda e: e.tensor_scalar(small[0], small[0], 1e-8, None, ALU.is_lt)),
    ] + rank_steps(V[4], 8, Z[5], (big, big2), tri[:, 0:8, 0:8]) + [
        (dve, lambda e: e.scalar_tensor_tensor(out=Z[4], in0=Z[5], scalar=2.0, in1=Z[4], op0=ALU.is_lt, op1=ALU.mult)),
        (dve, lambda e: e.tensor_reduce(small[1], V[4], AX, ALU.add)),
        (dve, lambda e: e.tensor_scalar(small[1], small[1], 1e-8, None, ALU.max)),
        (dve, lambda e: e.reciprocal(small[1], small[1])),
        (dve, lambda e: e.tensor_tensor(small[1], small[1], small[0], ALU.mult)),
        (dve, lambda e: e.tensor_tensor(V[4], V[4], bc(small[1]), ALU.mult)),
        (dve, lambda e: e.tensor_scalar(small[0], small[0], -1.0, 1.0, ALU.mult, ALU.add)),
        (dve, lambda e: e.tensor_tensor(V[2], V[2], bc(small[0]), ALU.mult)),
        (dve, lambda e: e.tensor_tensor(Z[2], Z[2], Z[4], ALU.add)),
        (dve, lambda e: e.tensor_reduce(small[2], V[2], AX, ALU.add)),
        (dve, lambda e: e.tensor_scalar(small[2], small[2], 1e-8, None, ALU.max)),
        (dve, lambda e: e.reciprocal(small[2], small[2])),
        (dve, lambda e: e.tensor_tensor(V[6], V[2], bc(small[2]), ALU.mult)),
    ]
    t_gw = [t, t_lg]

    n_gating = len(gating)

    def gate_steps(n):
        nonlocal t_gw
        for _ in range(min(n, len(gating))):
            q, f = gating.pop(0)
            t_gw = q.do(f, t_gw)
            if len(gating) == n_gating - 1:
                free[4] = t_gw

    def three(e, o, lh, ll, rh, rl, start, stop, **k):
        e.matmul(o, lh, rh, start=start, stop=False, **k)
        e.matmul(o, lh, rl, start=False, stop=False, **k)
        return e.matmul(o, ll, rh, start=False, stop=stop, **k)

    t_down = {}
    t_hf = [None, None]
    t_sg = [None, None]
    t_a0 = [None] * NT
    down_q = []
    nf = [0]

    t_up = {}
    t_half = {}

    def split_up(e_):
        z = e_ % 2
        th = act.do(lambda e: e.activation(wh[z][:, 0:1024], wraw[:, z, 0:1024], ACT.Copy), t_wraw[e_],
                    t_up.get(e_ - 2))
        tl = dve.do(lambda e: e.tensor_tensor(wl[z][:, 0:1024], wraw[:, z, 0:1024], wh[z][:, 0:1024].bitcast(F32),
                                              ALU.subtract), th)
        t_half[e_] = [th, tl]
        return [th, tl]

    def split_down(e_):
        z = e_ % 2
        th = act.do(lambda e: e.activation(wh[z][:, 1024:1536], wraw[:, z, 1024:1536], ACT.Copy), t_wraw[e_],
                    t_down.get(e_ - 2))
        tl = pool.do(lambda e: e.tensor_tensor(wl[z][:, 1024:1536], wraw[:, z, 1024:1536],
                                               wh[z][:, 1024:1536].bitcast(F32), ALU.subtract), th)
        if e_ + 2 < 8:
            t_wraw[e_ + 2] = l_fw[z].dma(wraw[:, z, :], a["wf0"][e_ + 2], th, tl, t_half[e_])
        return [th, tl]

    def up0(e_, m, half, tw):
        z = e_ % 2
        cs = slice(half * 512, half * 512 + 512)
        n = nf[0] % 2
        nf[0] += 1
        bg, bu = 2 * n, 2 * n + 1

        def mm(e):
            for g, b in ((0, bg), (1, bu)):
                for k in range(2):
                    ws = slice((2 * g + k) * 256 + m * 128, (2 * g + k) * 256 + m * 128 + 128)
                    last = three(e, bank[b][:], wh[z][:, ws], wl[z][:, ws], hTh[:, k, cs], hTl[:, k, cs], k == 0, k == 1)
            return last
        t = t_up[e_] = pe.do(mm, tw, t_p, free[bg], free[bu])
        t1 = act.do(lambda e: e.activation(sg[:, n, :], bank[bg][:], ACT.Silu), t, t_sg[n])
        free[bg] = t1
        t2 = dve.do(lambda e: e.tensor_tensor(hf[:, n, :], sg[:, n, :], bank[bu][:], ALU.mult), t1, t_hf[n])
        free[bu] = t_sg[n] = t2
        th = act.do(lambda e: e.activation(hh[z][:, m, cs], hf[:, n, :], ACT.Copy), t2, t_down.get(e_ - 2))
        tl = pool.do(lambda e: e.tensor_tensor(hl[z][:, m, cs], hf[:, n, :], hh[z][:, m, cs].bitcast(F32),
                                               ALU.subtract), th)
        t_hf[n] = tl
        return [th, tl]

    def down0(e_, i, th, tw):
        z = e_ % 2
        b = 4 + i % 4
        ts = slice(i * 128, (i + 1) * 128)

        def mm(e):
            for k in range(2):
                ws = slice((4 + k) * 256, (5 + k) * 256)
                last = three(e, bank[b][:, 0:256], hh[z][:, k, ts], hl[z][:, k, ts], wh[z][:, ws], wl[z][:, ws],
                             k == 0, k == 1)
            return last
        t = pe.do(mm, th, tw, free[b])
        t_down[e_] = t
        w = gz[:, 6, i * 8 + e_:i * 8 + e_ + 1]
        if e_ == 0:
            t = dve.do(lambda e: e.tensor_scalar(acc0[:, i, :], bank[b][:, 0:256], w, None, ALU.mult), t, t_gw)
        else:
            t = dve.do(lambda e: e.scalar_tensor_tensor(out=acc0[:, i, :], in0=bank[b][:, 0:256], scalar=w,
                                                        in1=acc0[:, i, :], op0=ALU.mult, op1=ALU.add), t, t_a0[i])
        free[b] = t_a0[i] = t
        if e_ == 7:
            t = pool.do(lambda e: e.tensor_tensor(acc0[:, i, :], acc0[:, i, :], gab[:, 1, :], ALU.mult), t, t_g[0])
            t_x2.append(bn(i, dve.do(lambda e: e.tensor_tensor(x[:, i, :], x[:, i, :], acc0[:, i, :], ALU.add), t)))

    t_x2 = []
    tw = split_up(0)
    gate_steps(10)
    for e_ in range(8):
        ths = [[], []]
        for half in range(2):
            for m in range(2):
                ths[half] += up0(e_, m, half, tw)
                if e_ == 0:
                    gate_steps(10)
                for _ in range(2):
                    if down_q:
                        down0(*down_q.pop(0))
                if (half, m) == (0, 1) and e_ + 1 < 8:
                    tw_next = split_up(e_ + 1)
        twd = split_down(e_)
        if e_ == 0:
            gate_steps(len(gating))
        if e_ == 1:
            gates()
        tw = tw_next
        down_q = [(e_, i, ths[i // 4], twd) for i in range(NT)]
    for d in down_q:
        down0(*d)

    t_phase = [(pe.sem, pe.n), (dve.sem, dve.n), (act.sem, act.n), (pool.sem, pool.n)]
    t_h, _ = norm(1, False, t_x2, False)
    t_h_cur = t_h
    t_stacks, t_v, t_pjo, load_heads, _ = project16(1, w1a, t_w1a, t_w1a, t_phase, t_phase, bq=bcol[:, 0:2], bk=bcol[:, 2:4], bvb=bvb,
                                                 scratch=scratch1)
    load_heads(2, t_phase)
    t_pj = [(act.sem, act.n), (dve.sem, dve.n), (pe.sem, pe.n), t_pjo]
    t_mc = dve.do(lambda e: e.memset(mcat[:], 1.0), t_phase)
    _, run = attention(units, True, score16, None, value16, evac16(False, octx, True, OTa), (2, 3),
                       extra16(t_stacks, t_v, t_pj), 0.25, 4, t_pj, OTa, 9, mxbanks=(0, 1, 7), lag=LAG1)
    run()
    t_att = [(pe.sem, pe.n), (dve.sem, dve.n), (act.sem, act.n), (pool.sem, pool.n)]
    t_x3 = out_projection(octx, w1a, [(dve.sem, dve.n)], lambda e, o, b, i: e.tensor_tensor(
        o, b, bob[:], ALU.add), t_w1a, Region(S0), "cT1")

    E = Region(S0 + 16 * 1024)
    cen = E.sb("cen", [128, 2, 16], F32)
    bib = E.sb("bib", [128, 16], F32)
    b1c = E.sb("b1c", [128, NF], F32)
    b2r = E.sb("b2r", [18, 256], F32)
    selt = E.sb("selt", [113, NF * 128], BF16)
    wr1 = E.sb("wr1", [128, 4, 512], F32)
    v1h = [E.sb(f"v1h{i}", [128, 512], F32R) for i in range(4)]
    v1l = [E.sb(f"v1l{i}", [128, 512], F32R) for i in range(4)]
    gc = E.sb("gc", [128, NT, 113], F32)
    g3 = E.sb("g3", [113, T], BF16)
    gT = E.sb("gT", [18, T], F32)
    sgm = E.sb("sgm", [128, 3, 128], F32)
    gb3 = E.sb("gb3", [128, NT, 16], BF16)
    pad = E.sb("pad", [128, 2, NT, 24], F32)
    top = E.sb("top", [128, NT, 8], F32)
    ngt = E.sb("ngt", [128, NT], F32)
    rl = E.sb("rl", [128, 2, 512], F32)
    hg = E.sb("hg", [128, 2, 512], F32)
    h1h = [E.sb(f"h1h{i}", [128, T], F32R) for i in range(2)]
    h1l = [E.sb(f"h1l{i}", [128, T], F32R) for i in range(2)]
    fin = E.sb("fin", [128, 2, 512], F32)
    l_e = group("e")
    l_e.dma(cen[:], a["cen"], t_att)
    l_e.dma(bib[:], a["ebias"].partition_broadcast(128), t_att)
    l_e.dma(b1c[:], a["b1c"], t_att)
    l_e.dma(b2r[:], a["b2r"], t_att)
    l_e.dma(selt[64:113, :], a["sel"], t_att)
    t_e = (l_e.sem, l_e.n)
    l_ew = [group(f"ew{i}") for i in range(4)]
    t_ew = [None] * NF
    for i in range(4):
        t_ew[i] = l_ew[i].dma(wr1[:, i, :], a["wf1"][i], t_att)
    t_gc0 = dve.do(lambda e: e.memset(gc[:], 1.0), t_att)
    t_gc0 = dve.do(lambda e: e.memset(pad[:], 0.0), t_att)

    t_h, t_p = norm(1, True, t_x3, True)

    def logits1(e):
        for i in range(NT):
            for k in range(2):
                last = e.matmul(bank[6][:, i * 16:i * 16 + 16], hT[:, k, i * 128:(i + 1) * 128], cen[:, k, :],
                                start=(k == 0), stop=(k == 1))
        return last
    t = pe.do(logits1, t_h[0], t_h[1], t_e, free[6])
    sgf = [sgm[:, i, :] for i in range(3)]
    sgv = [sgm[:, i, :].rearrange("p (i e) -> p i e", e=16) for i in range(3)]
    sm = sd
    padded = [pad[:, i, :, :] for i in range(2)]
    t4 = top[:, :, 3:4].to_broadcast([128, NT, 16])

    def top8(e):
        for i in range(NT):
            last = e.max(top[:, i, :], sgv[0][:, i, :])
        return last
    gating = [
        (act, lambda e: e.activation(sgf[0], bank[6][:, 0:128], ACT.Exp, scale=-1.0)),
        (dve, lambda e: e.tensor_scalar(sgf[0], sgf[0], 1.0, None, ALU.add)),
        (dve, lambda e: e.reciprocal(sgf[0], sgf[0])),
        (dve, lambda e: e.tensor_tensor(sgv[0], sgv[0], bib[:].unsqueeze(1).to_broadcast([128, NT, 16]), ALU.add)),
        (dve, top8),
        (dve, lambda e: e.tensor_tensor(sgv[1], sgv[0], t4, ALU.is_gt)),
        (dve, lambda e: e.tensor_tensor(padded[0][:, :, 8:24], sgv[0], t4, ALU.is_equal)),
        (dve, lambda e: e.tensor_reduce(ngt[:], sgv[1], AX, ALU.add)),
        (dve, lambda e: e.tensor_tensor(padded[1][:, :, 8:24], padded[0][:, :, 8:24], padded[0][:, :, 7:23], ALU.add)),
        (dve, lambda e: e.tensor_copy(sgv[2], padded[0][:, :, 8:24])),
        (dve, lambda e: e.tensor_tensor(padded[0][:, :, 8:24], padded[1][:, :, 8:24], padded[1][:, :, 6:22], ALU.add)),
        (dve, lambda e: e.tensor_tensor(padded[1][:, :, 8:24], padded[0][:, :, 8:24], padded[0][:, :, 4:20], ALU.add)),
        (dve, lambda e: e.tensor_tensor(padded[0][:, :, 8:24], padded[1][:, :, 8:24], padded[1][:, :, 0:16], ALU.add)),
        (dve, lambda e: e.tensor_tensor(padded[1][:, :, 8:24], padded[0][:, :, 7:23],
                                        ngt[:].unsqueeze(2).to_broadcast([128, NT, 16]), ALU.add)),
        (dve, lambda e: e.scalar_tensor_tensor(out=sgv[2], in0=padded[1][:, :, 8:24], scalar=4.0, in1=sgv[2],
                                               op0=ALU.is_lt, op1=ALU.mult)),
        (dve, lambda e: e.tensor_tensor(sgf[1], sgf[1], sgf[2], ALU.add)),
        (dve, lambda e: e.tensor_tensor(sgf[0], sgf[0], sgf[1], ALU.mult)),
        (dve, lambda e: e.tensor_reduce(sm[:], sgv[0], AX, ALU.add)),
        (dve, lambda e: e.tensor_scalar(sm[:], sm[:], 1e-8, None, ALU.max)),
        (dve, lambda e: e.reciprocal(sm[:], sm[:])),
        (dve, lambda e: e.tensor_tensor(gc[:, :, 0:16], sgv[0], sm[:].unsqueeze(2).to_broadcast([128, NT, 16]),
                                        ALU.mult)),
        (dve, lambda e: e.tensor_copy(gb3[:], gc[:, :, 0:16])),
        (dve, lambda e: e.tensor_copy(gc[:, :, 64:80], gb3[:])),
        (dve, lambda e: e.tensor_tensor(sgv[1], gc[:, :, 0:16], gc[:, :, 64:80], ALU.subtract)),
        (dve, lambda e: e.tensor_copy(gb3[:], sgv[1])),
        (dve, lambda e: e.tensor_copy(gc[:, :, 80:96], gb3[:])),
        (dve, lambda e: e.tensor_tensor(gc[:, :, 96:112], sgv[1], gc[:, :, 80:96], ALU.subtract)),
    ]
    t_lg = t
    def begin_sums(e):
        for i in range(NT):
            o = bank[i // 2][:, 256 * (i % 2):256 * (i % 2) + 256]
            ts = slice(i * 128, (i + 1) * 128)
            for k in range(2):
                for part in (hTh, hTl):
                    last = e.matmul(o[:, k * 128:(k + 1) * 128], part[:, k, ts], idr[:],
                                    start=(i % 2 == 0 and k == 0 and part is hTh), stop=False, skip_group_check=True)
        return last
    pe.do(begin_sums, t_p, t_idr, free[0], free[1], free[2], free[3])

    def bias_sums(e):
        for i in range(NT):
            o = bank[i // 2][:, 256 * (i % 2):256 * (i % 2) + 256]
            last = e.matmul(o, gT[:, i * 128:(i + 1) * 128], b2r[:], start=False, stop=False, skip_group_check=True)
        return last

    t_w1 = [None] * NF
    t_dn = [None] * NF
    t_rl, t_hg = [None, None], [None, None]

    def split1(f):
        z = f % 4
        th = act.do(lambda e: e.activation(v1h[z][:], wr1[:, z, :], ACT.Copy), t_ew[f], t_dn[f - 4] if f > 3 else None)
        tl = pool.do(lambda e: e.tensor_tensor(v1l[z][:], wr1[:, z, :], v1h[z][:].bitcast(F32), ALU.subtract), th)
        if f + 4 < NF:
            t_ew[f + 4] = l_ew[z].dma(wr1[:, z, :], a["wf1"][f + 4], th, tl)
        t_w1[f] = [th, tl]

    def up1(f, half):
        z, y = f % 4, f % 2
        cs = slice(half * 512, half * 512 + 512)
        bu, bg = 4 + half, 6 + half

        def mm(e):
            for k in range(2):
                ws = slice(k * 128, (k + 1) * 128)
                last = three(e, bank[bu][:], v1h[z][:, ws], v1l[z][:, ws], hTh[:, k, cs], hTl[:, k, cs], k == 0, k == 1)
            return last
        t = pe.do(mm, t_w1[f], t_p, free[bu])
        t1 = act.do(lambda e: e.activation(rl[:, half, :], bank[bu][:], ACT.Relu, bias=b1c[:, f:f + 1]), t, t_rl[half],
                    t_e)
        free[bu] = t1

        def gated():
            t = pe.do(lambda e: e.matmul(bank[bg][:], selt[64:113, f * 128:(f + 1) * 128], g3[64:113, cs], start=True,
                                         stop=True), t_gt, free[bg], t_e)
            t2 = dve.do(lambda e: e.tensor_tensor(hg[:, half, :], rl[:, half, :], bank[bg][:], ALU.mult), t1, t,
                        t_hg[half])
            free[bg] = t_rl[half] = t2
            th = act.do(lambda e: e.activation(h1h[y][:, cs], hg[:, half, :], ACT.Copy), t2,
                        t_dn[f - 2] if f > 1 else None)
            tl = dve.do(lambda e: e.tensor_tensor(h1l[y][:, cs], hg[:, half, :], h1h[y][:, cs].bitcast(F32),
                                                  ALU.subtract), th)
            t_hg[half] = tl
            return [th, tl]
        return gated

    def down1(f, half, th):
        z, y = f % 4, f % 2

        def mm(e):
            for i in range(4 * half, 4 * half + 4):
                o = bank[i // 2][:, 256 * (i % 2):256 * (i % 2) + 256]
                ts = slice(i * 128, (i + 1) * 128)
                last = three(e, o, h1h[y][:, ts], h1l[y][:, ts], v1h[z][:, 256:512], v1l[z][:, 256:512], False,
                             f == NF - 1, skip_group_check=True)
            return last
        t_dn[f] = pe.do(mm, th)
        return t_dn[f]

    split1(0)
    split1(1)
    t = chain(gating[:1], [t_lg, t_gc0])
    free[6] = t
    first_up = [up1(0, 0), up1(0, 1)]
    t = chain(gating[1:], t)
    free[6] = t
    t_gt = []
    for half in range(2):
        b = 6 + half

        def tr(e, half=half, b=b):
            for j in range(4):
                last = e.transpose(bank[b][0:113, j * 128:(j + 1) * 128], gc[:, 4 * half + j, :], idf[:])
            return last
        tt = pe.do(tr, t, free[b])
        cs = slice(half * 512, half * 512 + 512)
        t1 = act.do(lambda e, b=b, cs=cs: e.activation(g3[64:113, cs], bank[b][64:113, :], ACT.Copy), tt)
        t2 = act.do(lambda e, b=b, cs=cs: e.activation(gT[:, cs], bank[b][0:18, :], ACT.Copy), tt)
        free[b] = t2
        t_gt += [t1, t2]

    pe.do(bias_sums, t_gt, t_e)

    ready_h = []
    t_out = {}
    for f in range(NF):
        if f + 2 < NF:
            split1(f + 2)
        for half in range(2):
            th = (first_up[half] if f == 0 else up1(f, half))()
            ready_h.append((f, half, th))
            if len(ready_h) > 2:
                down1(*ready_h.pop(0))
    for r in ready_h:
        t_out[r[1]] = down1(*r)
    l_o = group("out")
    out_v = out.rearrange("a (i p) d -> p (a i) d", p=128)
    t_st = [None, None]
    for j in range(4):
        g = gab[:, 3, :].unsqueeze(1).to_broadcast([128, 2, 256])
        o = fin[:, j % 2, :].rearrange("p (a c) -> p a c", a=2)
        src = bank[j][:].rearrange("p (a c) -> p a c", a=2)
        t = dve.do(lambda e, o=o, src=src, g=g: e.tensor_tensor(o, src, g, ALU.mult), t_out[j // 2], t_st[j % 2], t_g[1])
        xs = x[:, 2 * j:2 * j + 2, :]
        t = dve.do(lambda e, o=o, xs=xs: e.tensor_tensor(xs, xs, o, ALU.add), t)
        t_st[j % 2] = t
        l_o.dma(out_v[:, 2 * j:2 * j + 2, :], xs, t)
    sp.ops.append((lambda e: e.wait_ge(l_o.sem, l_o.n), (), False))

    with nc.Block() as block:
        block.sync(sp.replay)
        block.gpsimd(pool.replay)
        block.scalar(act.replay)
        block.vector(dve.replay)
        block.tensor(pe.replay)


def bits(x):
    u = np.ascontiguousarray(x, np.float32).view(np.uint32)
    return ((u + 0x7FFF + ((u >> 16) & 1)) >> 16).astype(np.uint16)


def value_of(b):
    return (b.astype(np.uint32) << 16).view(np.float32)


def constants():
    c = {}
    eye = np.eye(128, dtype=np.float32)
    c["idf"] = eye
    c["idb"] = bits(eye)
    q, k = np.arange(128)[:, None], np.arange(128)[None, :]
    c["maskq"] = bits(np.where(k > q, NEG, 0.0))
    c["maskk"] = np.ascontiguousarray(c["maskq"].T)
    dm = np.zeros((11, 4, 128), np.float32)
    dm[0:3] = 1.0
    for j in range(4):
        dm[3 + j, j] = 1.0
        dm[7 + j, j] = 1.0
    c["dmask"] = dm
    es = np.zeros((128, 17), np.float32)
    for g in range(4):
        es[32 * g:32 * g + 17] = np.eye(17)
    c["esum"] = es
    c["ones3"] = np.ones((128, 128), np.float32)
    c["ones3"][0:3] = 0.0
    j = np.arange(16)
    c["tri"] = np.broadcast_to((j[None, :] < j[:, None]).astype(np.float32), (128, 16, 16)).copy()
    inv = (np.float32(1.0) / np.power(np.float32(10000.0), np.arange(0, 64, 2, dtype=np.float32) / np.float32(64)))
    fr = np.outer(np.arange(T, dtype=np.float32), inv.astype(np.float32)).astype(np.float32)
    cos, sin = np.cos(fr).T.astype(np.float32), np.sin(fr).T.astype(np.float32)
    c["cosT"] = np.concatenate([cos] * 4, 0)
    c["sinT"] = np.concatenate([-sin, sin] * 2, 0)
    start = 2 ** (-2 ** (-(math.log2(H) - 3)))
    slopes = np.array([start * start ** i for i in range(H)], np.float32)
    al = (slopes[:, None] * (np.arange(T, dtype=np.float32) - np.float32(T - 1))[None, :]) * np.float32(4)
    rows = np.ones((11, H, T), np.float32)
    c["qrow"] = bits(rows)
    k0 = rows.copy()
    k0[0:3] = 0.0
    c["krow0"] = bits(k0)
    r = al.astype(np.float32)
    k1 = bits(rows)
    for i in range(3):
        k1[i] = bits(r)
        r = r - value_of(k1[i])
    c["krow1"] = k1
    sel = np.zeros((49, NF * 128), np.float32)
    ex = np.arange(NF * 128) // FF1
    for f in range((NS1 + NE1) * FF1):
        if ex[f] < NS1:
            sel[48, f] = 1.0
        else:
            for p in range(3):
                sel[16 * p + ex[f] - NS1, f] = 1.0
    c["sel"] = bits(sel)
    return c


def layout(i):
    def rows2(w):
        return np.ascontiguousarray(w.reshape(2, 128, -1).transpose(1, 0, 2))

    def cat(*w):
        return np.concatenate(w, 0)
    d = {"x": i["L0_attn_hidden_states"]}
    d["cc"] = np.ascontiguousarray(np.stack([i["L0_c"][0], i["L1_c"][0]], 0).reshape(2, 2, 128).transpose(2, 0, 1))
    d["wmod0"], d["wmod1"] = rows2(i["L0_wmod"]), rows2(i["L1_wmod"])
    kva = i["L0_attn_kv_a_w"]
    d["w0a"] = rows2(cat(i["L0_attn_q_a_w"], kva[:64], i["L0_attn_gate_w"]).T)
    d["q_ln"], d["kv_ln"], d["gate_b"] = i["L0_attn_q_a_ln_w"], i["L0_attn_kv_a_ln_w"], i["L0_attn_gate_b"]
    kpe = kva[64:].reshape(8, 2, 64, 256)[:, ::-1].reshape(1024, 256).T
    d["wkpe"] = np.ascontiguousarray(kpe.reshape(2, 128, 8, 128).transpose(1, 0, 2, 3))
    qb = i["L0_attn_q_b_w"].reshape(16, 192, 192)
    qpe = qb[:, 128:, :].reshape(8, 2, 64, 192)[:, ::-1].reshape(8, 128, 192).transpose(2, 0, 1)
    d["wqpa"], d["wqpb"] = np.ascontiguousarray(qpe[:128]), np.ascontiguousarray(qpe[128:])
    d["qbn"] = np.ascontiguousarray(qb[:, :128, :].transpose(1, 0, 2))
    kvb = i["L0_attn_kv_b_w"].reshape(16, 256, 64)
    d["kvbk"] = np.ascontiguousarray(kvb[:, :128].transpose(1, 0, 2))
    d["kvbv"] = np.ascontiguousarray(kvb[:, 128:].transpose(1, 0, 2))
    d["owT"] = np.ascontiguousarray(i["L0_attn_o_w"].reshape(256, 16, 128).transpose(2, 1, 0))
    d["wsp0"] = np.ascontiguousarray(np.stack(
        [rows2(i[f"L0_attn_sp_{n}_w"].T) for n in "qkvo"], 1))
    d["wr"], d["temp"] = rows2(i["L0_ffn_Wr"]), i["L0_ffn_temperature"]

    def tiles(w):
        return w.reshape(8, 2, 128, 256).transpose(0, 2, 1, 3).reshape(8, 128, 512)
    d["wf0"] = np.ascontiguousarray(np.concatenate(
        [tiles(i["L0_ffn_Wg"]), tiles(i["L0_ffn_Wu"]), tiles(i["L0_ffn_Wd"])], 2))
    d["w1a"] = np.ascontiguousarray(np.stack([rows2(i[f"L1_attn_W{n}"]) for n in "qkvo"], 1))
    d["bqk"] = np.ascontiguousarray(np.concatenate(
        [i["L1_attn_bq"].reshape(2, 128).T, i["L1_attn_bk"].reshape(2, 128).T], 1))
    d["bv"], d["bo"] = i["L1_attn_bv"], i["L1_attn_bo"]
    d["cen"] = rows2(i["L1_ffn_centroids"].T)
    d["ebias"] = i["L1_ffn_bias"]
    pad = NF * 128 - 18 * FF1
    w1 = cat(i["L1_ffn_shared_w1"], i["L1_ffn_routed_w1"]).transpose(1, 0, 2).reshape(256, 18 * FF1)
    w1 = np.concatenate([w1, np.zeros((256, pad), w1.dtype)], 1).reshape(2, 128, NF, 128).transpose(2, 1, 0, 3)
    w2 = cat(i["L1_ffn_shared_w2"], i["L1_ffn_routed_w2"]).reshape(18 * FF1, 256)
    w2 = cat(w2, np.zeros((pad, 256), w2.dtype)).reshape(NF, 128, 256)
    d["wf1"] = np.ascontiguousarray(np.concatenate([w1.reshape(NF, 128, 256), w2], 2))
    b1 = cat(i["L1_ffn_shared_b1"], i["L1_ffn_routed_b1"]).reshape(-1)
    d["b1c"] = np.ascontiguousarray(cat(b1, np.zeros(pad, b1.dtype)).reshape(NF, 128).T)
    d["b2r"] = np.ascontiguousarray(cat(i["L1_ffn_routed_b2"], i["L1_ffn_shared_b2"]))
    return d


def kernel(**inputs):
    import concourse.bacc as _bacc
    from concourse.bass_utils import run_bass_kernel_spmd as _run

    arrays = {k: np.ascontiguousarray(v) for k, v in layout({k: np.asarray(v) for k, v in inputs.items()}).items()}
    arrays.update(constants())
    nc = _bacc.Bacc("TRN2", target_bir_lowering=False, num_devices=1)
    aps = {n: nc.dram_tensor(n, v.shape, mybir.dt.from_np(v.dtype), kind="ExternalInput").ap()
           for n, v in arrays.items()}
    aps = {n: ap.bitcast(BF16) if arrays[n].dtype == np.uint16 else ap for n, ap in aps.items()}
    o = nc.dram_tensor("out_x", (1, T, D), F32, kind="ExternalOutput").ap()
    program(nc, aps, o)
    r = _run(nc, [arrays], core_ids=[0])
    return r.results[0]["out_x"]
```
